# Optimizing a Trainium2 kernel written in Bass

```python
import numpy as np
import jax
import jax.numpy as jnp

def _softmax(x, axis=-1):
    return jax.nn.softmax(x, axis=axis)

def _gelu(x):
    return jax.nn.gelu(x, approximate=True)

def _silu(x):
    return jax.nn.silu(x)

def _sigmoid(x):
    return jax.nn.sigmoid(x)

def _layernorm(x, axis=-1, eps=1e-05):
    m = jnp.mean(x, axis=axis, keepdims=True)
    v = jnp.var(x, axis=axis, keepdims=True)
    return (x - m) / jnp.sqrt(v + eps)

def _scatter_add(tgt, idx, src, axis=0):
    return tgt.at[idx].add(src)

def _segment_sum(src, seg, n):
    return jax.ops.segment_sum(src, seg, n)
kernel_name = 'mk_conv_attn_hybrid_d2_conv_nchw256_r2_65a750'

def setup_inputs(seed: int=0):
    np.random.seed(seed)
    _w = jnp.asarray

    def _rec_inputs():
        import jax
        import jax.numpy as jnp
        _gk = jax.random.key(seed)
        x = 7.22e-05 + 1 * jax.random.normal(jax.random.fold_in(_gk, 1), (8, 128, 32, 32), jnp.float32)
        return x
    x = _rec_inputs()

    def _L0_conv_setup():
        import jax, jax.numpy as jnp
        import numpy as np

        def conv2d_same(x, w, b=None):
            out = jax.lax.conv_general_dilated(x, w, window_strides=(1, 1), padding='SAME', dimension_numbers=('NCHW', 'OIHW', 'NCHW'))
            if b is not None:
                out = out + b[None, :, None, None]
            return out

        def deform_conv(x, offset, wd, k=3, pad=1, dg=4):
            B, C, H, W = x.shape
            cg = C // dg
            K = k * k
            off = offset.reshape(B, dg, K, 2, H, W)
            dy, dx = (off[:, :, :, 0], off[:, :, :, 1])
            ky = (jnp.arange(K) // k - pad).astype(x.dtype)
            kx = (jnp.arange(K) % k - pad).astype(x.dtype)
            hh = jnp.arange(H, dtype=x.dtype)
            ww = jnp.arange(W, dtype=x.dtype)
            py = dy + ky[None, None, :, None, None] + hh[None, None, None, :, None]
            px = dx + kx[None, None, :, None, None] + ww[None, None, None, None, :]
            y0 = jnp.floor(py)
            x0 = jnp.floor(px)
            wy1 = py - y0
            wy0 = 1.0 - wy1
            wx1 = px - x0
            wx0 = 1.0 - wx1
            xg = x.reshape(B, dg, cg, H * W)

            def gather(yi, xi):
                valid = (yi >= 0) & (yi < H) & (xi >= 0) & (xi < W)
                yc = jnp.clip(yi, 0, H - 1).astype(jnp.int32)
                xc = jnp.clip(xi, 0, W - 1).astype(jnp.int32)
                idx = (yc * W + xc).reshape(B, dg, 1, K * H * W)
                g = jnp.take_along_axis(xg, jnp.broadcast_to(idx, (B, dg, cg, K * H * W)), axis=-1)
                g = g.reshape(B, dg, cg, K, H, W)
                return g * valid[:, :, None].astype(x.dtype)
            val = gather(y0, x0) * (wy0 * wx0)[:, :, None] + gather(y0, x0 + 1) * (wy0 * wx1)[:, :, None] + gather(y0 + 1, x0) * (wy1 * wx0)[:, :, None] + gather(y0 + 1, x0 + 1) * (wy1 * wx1)[:, :, None]
            wr = wd.reshape(wd.shape[0], dg, cg, K)
            return jnp.einsum('ogck,bgckhw->bohw', wr, val)
        key = jax.random.key(seed)
        k1, k2, k3, k4 = jax.random.split(key, 4)
        B, C, H, W = (8, 128, 32, 32)
        dg, ks = (4, 3)
        x = jax.random.normal(k1, (B, C, H, W), dtype=jnp.float32)
        w1 = jax.random.normal(k2, (C, C, 3, 3), dtype=jnp.float32) * 0.01
        b1 = jnp.zeros((C,), dtype=jnp.float32)
        w2 = jax.random.normal(k3, (dg * ks * ks * 2, C, 3, 3), dtype=jnp.float32) * 0.01
        b2 = jnp.zeros((dg * ks * ks * 2,), dtype=jnp.float32)
        wd = jax.random.normal(k4, (C, C, ks, ks), dtype=jnp.float32) * 0.01
        return {'x': x, 'w1': w1, 'b1': b1, 'w2': w2, 'b2': b2, 'wd': wd}
    _L0_conv_all = _L0_conv_setup()
    _L0_conv_in = {k: v for k, v in _L0_conv_all.items() if k in ('w1', 'b1', 'w2', 'b2', 'wd')}
    del _L0_conv_all

    def _L1_attn_setup():
        import jax, jax.numpy as jnp
        import numpy as np
        B, S, C = (8, 512, 128)
        H, KD = (8, 128)
        HEAD_DIM = KD // H
        key = jax.random.key(seed)
        ks = jax.random.split(key, 5)
        sc = 0.02
        return {'x': jax.random.normal(ks[0], (B, S, C), dtype=jnp.float32), 'Wq': jax.random.normal(ks[1], (H * KD, C), dtype=jnp.float32) * sc, 'Wk': jax.random.normal(ks[2], (KD, C), dtype=jnp.float32) * sc, 'Wv': jax.random.normal(ks[3], (KD, C), dtype=jnp.float32) * sc, 'Wo': jax.random.normal(ks[4], (C, H * KD), dtype=jnp.float32) * sc}
    _L1_attn_all = _L1_attn_setup()
    _L1_attn_in = {k: v for k, v in _L1_attn_all.items() if k in ('Wq', 'Wk', 'Wv', 'Wo')}
    del _L1_attn_all

    def _L1_ffn_setup():
        import jax, jax.numpy as jnp
        import numpy as np
        B, N, D = (16, 2048, 128)
        NUM_EXPERTS, TOP_K, HEADS = (4, 2, 4)
        N_EDGES = 524288
        LN_EPS = 1e-05

        def _layernorm(x, g, b):
            mu = x.mean(-1, keepdims=True)
            var = ((x - mu) ** 2).mean(-1, keepdims=True)
            return (x - mu) * jax.lax.rsqrt(var + LN_EPS) * g + b

        def _forward(x, edge_index, W_gat, att_src, att_dst, b_gat, ln_gamma, ln_beta, W1, b1, W2, b2):
            Bc, Nc, Dc = x.shape
            M = Bc * Nc
            x_flat = x.reshape(M, Dc)
            h = (x_flat @ W_gat).reshape(M, HEADS, NUM_EXPERTS)
            loops = jnp.arange(M, dtype=edge_index.dtype)
            src = jnp.concatenate([edge_index[0], loops])
            dst = jnp.concatenate([edge_index[1], loops])
            a_src = (h * att_src).sum(-1)
            a_dst = (h * att_dst).sum(-1)
            e = jax.nn.leaky_relu(a_src[src] + a_dst[dst], negative_slope=0.2)
            e_max = jax.ops.segment_max(e, dst, num_segments=M)
            ee = jnp.exp(e - e_max[dst])
            denom = jax.ops.segment_sum(ee, dst, num_segments=M)
            alpha = ee / (denom[dst] + 1e-16)
            msg = h[src] * alpha[:, :, None]
            agg = jax.ops.segment_sum(msg, dst, num_segments=M).reshape(M, HEADS * NUM_EXPERTS) + b_gat
            scores = _layernorm(agg, ln_gamma, ln_beta).reshape(M, HEADS, NUM_EXPERTS).mean(1)
            scores = scores.reshape(Bc, Nc, NUM_EXPERTS)
            topk_s, topk_i = jax.lax.top_k(scores, TOP_K)
            w = jax.nn.softmax(topk_s, axis=-1)
            out = jnp.zeros_like(x)
            for ei in range(NUM_EXPERTS):
                g = jnp.where(topk_i == ei, w, 0.0).sum(-1)
                hh = jax.nn.gelu(x @ W1[ei] + b1[ei], approximate=False)
                out = out + g[..., None] * (hh @ W2[ei] + b2[ei])
            return out
        key = jax.random.key(seed)
        ks = jax.random.split(key, 8)
        s = 0.05
        return {'x': jax.random.normal(ks[0], (B, N, D), jnp.float32), 'W_gat': jax.random.normal(ks[1], (D, HEADS * NUM_EXPERTS), jnp.float32) * s, 'att_src': jax.random.normal(ks[2], (HEADS, NUM_EXPERTS), jnp.float32) * s, 'att_dst': jax.random.normal(ks[3], (HEADS, NUM_EXPERTS), jnp.float32) * s, 'b_gat': jnp.zeros((HEADS * NUM_EXPERTS,), jnp.float32), 'ln_gamma': jnp.ones((HEADS * NUM_EXPERTS,), jnp.float32), 'ln_beta': jnp.zeros((HEADS * NUM_EXPERTS,), jnp.float32), 'W1': jax.random.normal(ks[4], (NUM_EXPERTS, D, 2 * D), jnp.float32) * s, 'b1': jnp.zeros((NUM_EXPERTS, 2 * D), jnp.float32), 'W2': jax.random.normal(ks[5], (NUM_EXPERTS, 2 * D, D), jnp.float32) * s, 'b2': jnp.zeros((NUM_EXPERTS, D), jnp.float32), 'edge_index': jax.random.randint(ks[6], (2, N_EDGES), 0, B * N, jnp.int32)}
    _L1_ffn_all = _L1_ffn_setup()
    _L1_ffn_in = {k: v for k, v in _L1_ffn_all.items() if k in ('W_gat', 'att_src', 'att_dst', 'b_gat', 'ln_gamma', 'ln_beta', 'W1', 'b1', 'W2', 'b2', 'edge_index')}
    del _L1_ffn_all
    return {'x': x, 'L0_conv_w1': _L0_conv_in['w1'], 'L0_conv_b1': _L0_conv_in['b1'], 'L0_conv_w2': _L0_conv_in['w2'], 'L0_conv_b2': _L0_conv_in['b2'], 'L0_conv_wd': _L0_conv_in['wd'], 'L1_attn_Wq': _L1_attn_in['Wq'], 'L1_attn_Wk': _L1_attn_in['Wk'], 'L1_attn_Wv': _L1_attn_in['Wv'], 'L1_attn_Wo': _L1_attn_in['Wo'], 'L1_ffn_W_gat': _L1_ffn_in['W_gat'], 'L1_ffn_att_src': _L1_ffn_in['att_src'], 'L1_ffn_att_dst': _L1_ffn_in['att_dst'], 'L1_ffn_b_gat': _L1_ffn_in['b_gat'], 'L1_ffn_ln_gamma': _L1_ffn_in['ln_gamma'], 'L1_ffn_ln_beta': _L1_ffn_in['ln_beta'], 'L1_ffn_W1': _L1_ffn_in['W1'], 'L1_ffn_b1': _L1_ffn_in['b1'], 'L1_ffn_W2': _L1_ffn_in['W2'], 'L1_ffn_b2': _L1_ffn_in['b2'], 'L1_ffn_edge_index': _L1_ffn_in['edge_index']}

def reference(x, L0_conv_w1, L0_conv_b1, L0_conv_w2, L0_conv_b2, L0_conv_wd, L1_attn_Wq, L1_attn_Wk, L1_attn_Wv, L1_attn_Wo, L1_ffn_W_gat, L1_ffn_att_src, L1_ffn_att_dst, L1_ffn_b_gat, L1_ffn_ln_gamma, L1_ffn_ln_beta, L1_ffn_W1, L1_ffn_b1, L1_ffn_W2, L1_ffn_b2, L1_ffn_edge_index):
    import jax
    import jax.numpy as jnp

    def _L0_conv_ref(x, w1, b1, w2, b2, wd):
        import jax, jax.numpy as jnp
        import numpy as np

        def conv2d_same(x, w, b=None):
            out = jax.lax.conv_general_dilated(x, w, window_strides=(1, 1), padding='SAME', dimension_numbers=('NCHW', 'OIHW', 'NCHW'))
            if b is not None:
                out = out + b[None, :, None, None]
            return out

        def deform_conv(x, offset, wd, k=3, pad=1, dg=4):
            B, C, H, W = x.shape
            cg = C // dg
            K = k * k
            off = offset.reshape(B, dg, K, 2, H, W)
            dy, dx = (off[:, :, :, 0], off[:, :, :, 1])
            ky = (jnp.arange(K) // k - pad).astype(x.dtype)
            kx = (jnp.arange(K) % k - pad).astype(x.dtype)
            hh = jnp.arange(H, dtype=x.dtype)
            ww = jnp.arange(W, dtype=x.dtype)
            py = dy + ky[None, None, :, None, None] + hh[None, None, None, :, None]
            px = dx + kx[None, None, :, None, None] + ww[None, None, None, None, :]
            y0 = jnp.floor(py)
            x0 = jnp.floor(px)
            wy1 = py - y0
            wy0 = 1.0 - wy1
            wx1 = px - x0
            wx0 = 1.0 - wx1
            xg = x.reshape(B, dg, cg, H * W)

            def gather(yi, xi):
                valid = (yi >= 0) & (yi < H) & (xi >= 0) & (xi < W)
                yc = jnp.clip(yi, 0, H - 1).astype(jnp.int32)
                xc = jnp.clip(xi, 0, W - 1).astype(jnp.int32)
                idx = (yc * W + xc).reshape(B, dg, 1, K * H * W)
                g = jnp.take_along_axis(xg, jnp.broadcast_to(idx, (B, dg, cg, K * H * W)), axis=-1)
                g = g.reshape(B, dg, cg, K, H, W)
                return g * valid[:, :, None].astype(x.dtype)
            val = gather(y0, x0) * (wy0 * wx0)[:, :, None] + gather(y0, x0 + 1) * (wy0 * wx1)[:, :, None] + gather(y0 + 1, x0) * (wy1 * wx0)[:, :, None] + gather(y0 + 1, x0 + 1) * (wy1 * wx1)[:, :, None]
            wr = wd.reshape(wd.shape[0], dg, cg, K)
            return jnp.einsum('ogck,bgckhw->bohw', wr, val)
        xd = jax.lax.stop_gradient(x)
        offset = conv2d_same(conv2d_same(xd, w1, b1), w2, b2)
        return jax.nn.relu(deform_conv(x, offset, wd, k=3, pad=1, dg=4))

    def _L1_attn_ref(x, Wq, Wk, Wv, Wo):
        import jax, jax.numpy as jnp
        import numpy as np
        B, S, C = (8, 512, 128)
        H, KD = (8, 128)
        HEAD_DIM = KD // H
        b, s, c = x.shape
        q = jnp.einsum('bsc,oc->bso', x, Wq).reshape(b, s, H, KD).transpose(0, 2, 1, 3)
        k = jnp.einsum('bsc,oc->bos', x, Wk)
        v_conv = jnp.einsum('bsc,oc->bos', x, Wv)
        v = v_conv.reshape(b, s, KD)
        scale = 1.0 / np.sqrt(HEAD_DIM).astype(np.float32)
        scores = jnp.einsum('bhsd,bdt->bhst', q, k) * scale
        attn = jax.nn.softmax(scores, axis=-1)
        ctx = jnp.einsum('bhst,btd->bhsd', attn, v)
        ctx = ctx.transpose(0, 2, 1, 3).reshape(b, H * KD, s)
        out = jnp.einsum('bcp,oc->bop', ctx, Wo)
        return out.transpose(0, 2, 1)

    def _L1_ffn_ref(x, W_gat, att_src, att_dst, b_gat, ln_gamma, ln_beta, W1, b1, W2, b2, edge_index):
        import jax, jax.numpy as jnp
        import numpy as np
        B, N, D = (16, 2048, 128)
        NUM_EXPERTS, TOP_K, HEADS = (4, 2, 4)
        N_EDGES = 524288
        LN_EPS = 1e-05

        def _layernorm(x, g, b):
            mu = x.mean(-1, keepdims=True)
            var = ((x - mu) ** 2).mean(-1, keepdims=True)
            return (x - mu) * jax.lax.rsqrt(var + LN_EPS) * g + b

        def _forward(x, edge_index, W_gat, att_src, att_dst, b_gat, ln_gamma, ln_beta, W1, b1, W2, b2):
            Bc, Nc, Dc = x.shape
            M = Bc * Nc
            x_flat = x.reshape(M, Dc)
            h = (x_flat @ W_gat).reshape(M, HEADS, NUM_EXPERTS)
            loops = jnp.arange(M, dtype=edge_index.dtype)
            src = jnp.concatenate([edge_index[0], loops])
            dst = jnp.concatenate([edge_index[1], loops])
            a_src = (h * att_src).sum(-1)
            a_dst = (h * att_dst).sum(-1)
            e = jax.nn.leaky_relu(a_src[src] + a_dst[dst], negative_slope=0.2)
            e_max = jax.ops.segment_max(e, dst, num_segments=M)
            ee = jnp.exp(e - e_max[dst])
            denom = jax.ops.segment_sum(ee, dst, num_segments=M)
            alpha = ee / (denom[dst] + 1e-16)
            msg = h[src] * alpha[:, :, None]
            agg = jax.ops.segment_sum(msg, dst, num_segments=M).reshape(M, HEADS * NUM_EXPERTS) + b_gat
            scores = _layernorm(agg, ln_gamma, ln_beta).reshape(M, HEADS, NUM_EXPERTS).mean(1)
            scores = scores.reshape(Bc, Nc, NUM_EXPERTS)
            topk_s, topk_i = jax.lax.top_k(scores, TOP_K)
            w = jax.nn.softmax(topk_s, axis=-1)
            out = jnp.zeros_like(x)
            for ei in range(NUM_EXPERTS):
                g = jnp.where(topk_i == ei, w, 0.0).sum(-1)
                hh = jax.nn.gelu(x @ W1[ei] + b1[ei], approximate=False)
                out = out + g[..., None] * (hh @ W2[ei] + b2[ei])
            return out
        return _forward(x, edge_index, W_gat, att_src, att_dst, b_gat, ln_gamma, ln_beta, W1, b1, W2, b2)

    def _gn(v, G=32, eps=1e-05):
        B_, C_, H_, W_ = v.shape
        g = v.reshape(B_, G, C_ // G, H_, W_)
        m = jnp.mean(g, axis=(2, 3, 4), keepdims=True)
        s = jnp.var(g, axis=(2, 3, 4), keepdims=True)
        return ((g - m) / jnp.sqrt(s + eps)).reshape(v.shape)

    def _ln_c(v, eps=1e-06):
        m = jnp.mean(v, axis=1, keepdims=True)
        s = jnp.var(v, axis=1, keepdims=True)
        return (v - m) / jnp.sqrt(s + eps)

    def _ln_t(v, eps=1e-05):
        m = jnp.mean(v, axis=-1, keepdims=True)
        s = jnp.var(v, axis=-1, keepdims=True)
        return (v - m) / jnp.sqrt(s + eps)

    def _to_tokens(v):
        B_, C_, H_, W_ = v.shape
        return v.reshape(B_, C_, H_ * W_).transpose(0, 2, 1)

    def _from_tokens(t, like):
        B_, C_, H_, W_ = like.shape
        return t.transpose(0, 2, 1).reshape(B_, C_, H_, W_)
    x = x + _L0_conv_ref(_gn(x), L0_conv_w1, L0_conv_b1, L0_conv_w2, L0_conv_b2, L0_conv_wd)
    t = _to_tokens(x)
    t = t + _L1_attn_ref(_ln_t(t), L1_attn_Wq, L1_attn_Wk, L1_attn_Wv, L1_attn_Wo)
    t = t + _L1_ffn_ref(_ln_t(t), L1_ffn_W_gat, L1_ffn_att_src, L1_ffn_att_dst, L1_ffn_b_gat, L1_ffn_ln_gamma, L1_ffn_ln_beta, L1_ffn_W1, L1_ffn_b1, L1_ffn_W2, L1_ffn_b2, L1_ffn_edge_index)
    x = _from_tokens(t, x)
    return x

_drawn_inputs = setup_inputs


def setup_inputs(seed=0):
    import zlib

    import numpy as np

    out = dict(_drawn_inputs(seed))
    spreads = {'L0_conv_b1': (0.0, 0.58),
     'L0_conv_b2': (0.0, 0.1),
     'L1_ffn_b_gat': (0.0, 1.726),
     'L1_ffn_ln_gamma': (1.0, 0.6),
     'L1_ffn_ln_beta': (0.0, 2.0),
     'L1_ffn_b1': (0.0, 0.8),
     'L1_ffn_b2': (0.0, 0.679)}
    factors = {'L1_attn_Wq': 8.0,
     'L1_attn_Wk': 8.0,
     'L1_attn_Wv': 8.0,
     'L1_attn_Wo': 8.0,
     'L1_ffn_att_src': 64.0,
     'L1_ffn_att_dst': 64.0,
     'L1_ffn_W_gat': 8.0}
    for name, (base, spread) in spreads.items():
        noise = np.random.default_rng([zlib.crc32(name.encode()), seed]).standard_normal(out[name].shape)
        drawn = base * np.exp(spread * noise) if base else spread * noise
        out[name] = jnp.asarray(drawn.astype(out[name].dtype))
    for name, factor in factors.items():
        out[name] = (out[name] * factor).astype(out[name].dtype)
    return out
```

```python
import concourse.bass as bass
from concourse import mybir
from contextlib import ExitStack

ds = bass.ds
f32 = mybir.dt.float32
bf16 = mybir.dt.bfloat16
i32 = mybir.dt.int32
u32 = mybir.dt.uint32
ALU = mybir.AluOpType
ACT = mybir.ActivationFunctionType
AX = mybir.AxisListType

P = 128
B, C, WID = 8, 128, 32
HW = WID * WID
NT = HW // P
DG, TAPS = 4, 9
CG = C // DG
NOFF = 2 * DG * TAPS
PITCH = WID + 2
PADN = 1280
BASE = 2 * PITCH + 2
CORNER = (0, 1, PITCH, PITCH + 1)
FRONT = 40
TROWS = PADN + FRONT
HEADS = 8
NODES = B * HW
HI = NODES // P
M = NODES
E = 524288
EXP, HF, PAY, RES = 4, 16, 20, 24
NPOS = E + NODES
PCOLS = NPOS // P
CHK = 80
NCH = PCOLS // CHK
NEG = -1e30
E_UNIT, E_CH = 8, 32
E_NU = E_CH // E_UNIT
E_ITERS = E // P // E_CH // 2

class Chain:
    def __init__(self,eng,sem,per=0): self.eng,self.sem,self.per,self.n,self.base=eng,sem,per,0,0
    def body(self,i): self.base=i*self.per; self.n=0
    def end(self): assert self.n==self.per,(self.n,self.per)
    def mark(self,ins): self.n+=1; return ins.then_inc(self.sem,1)
    def sync(self): self.eng.wait_ge(self.sem,self.base+self.n)
    def __call__(self,ins): self.mark(ins); self.sync()

def conv_phase(nc,A,table,x_all,idx_all,w4_all,wdT,ident,dbg=None):
    with ExitStack() as ctx:
        sb=lambda n,s,d: ctx.enter_context(nc.sbuf_tensor(n,s,d))
        pb=lambda n,s,d: ctx.enter_context(nc.psum_tensor(n,s,d))
        sem=lambda n: ctx.enter_context(nc.semaphore("c_"+n))
        w1n=sb("w1n",[P,C*TAPS],f32); w2n=sb("w2n",[NOFF,C*TAPS],f32); wdn=sb("wdn",[P,C*TAPS],f32)
        w1T=sb("w1T",[P,TAPS,P],f32); w2T=sb("w2T",[P,TAPS,NOFF],f32)
        b1=sb("b1c",[P,1],f32); b2=sb("b2c",[P,NOFF],f32)
        gavg=sb("gavg",[P,P],f32)
        bst=sb("bst",[P,B,2,6],f32); mv=sb("mv",[P,B,2],f32)
        mean=sb("mean",[P,B],f32); rstd=sb("rstd",[P,B],f32); dev=sb("dev",[P,B],f32)
        xpad=sb("xpad",[P,2,PADN],f32); hpad=sb("hpad",[P,2,PADN],f32)
        off=sb("off",[NOFF,2,512],f32)
        Fs=sb("Fs",[P,2,10,P],f32)
        pxi=sb("pxi",[P,NT],i32); pyx=sb("pyx",[P,NT,2],f32); yi=sb("yi",[P,NT],i32); xi=sb("xi",[P,NT],i32)
        kyx=sb("kyx",[P,DG*TAPS,2],f32); kyi=sb("kyi",[P,TAPS],i32); kxi=sb("kxi",[P,TAPS],i32)
        gbase=sb("gbase",[P,DG],i32); gbf=sb("gbf",[P,DG],f32)
        basec=sb("basec",[P,NT,NOFF],f32)
        pos=sb("posyx",[P,NT,NOFF],f32); fli=sb("fli",[P,NT,NOFF],i32); fl=sb("fl",[P,NT,NOFF],f32); gt=sb("gt",[P,NT,NOFF],f32)
        whi=sb("whi",[P,NT,NOFF],f32); wlo=sb("wlo",[P,NT,NOFF],f32)
        ixf=sb("ixf",[P,NT,DG*TAPS],f32)
        tp=[pb(f"tp{i}",[P,4,P],f32) for i in range(3)]
        st_ps=pb("st_ps",[P,B],f32)
        c1=[pb(f"c1_{i}",[P,512],f32) for i in range(2)]
        c2=[pb(f"c2_{i}",[P,4,NOFF],f32) for i in range(2)]
        s_const=sem("const"); s_x=sem("x"); s_w=sem("w"); s_b=sem("b"); s_wt=sem("wt"); s_wt_ev=sem("wt_ev")
        s_mean=sem("mean_in"); s_gm=sem("group_mean"); s_var=sem("var_in"); s_gv=sem("group_var"); s_sq=sem("sqrt")
        s_pad=sem("padded"); s_zero=sem("zeroed"); s_c1=sem("conv1_done"); s_h=sem("hidden_ready"); s_c2=sem("conv2_done")
        ztile=sb("ztile",[P,FRONT*DG],f32); s_edge=sem("table_edges")
        s_off=sem("offsets_out"); s_ot=sem("offsets_transposed")
        s_c2r=sem("conv2_read"); s_F=sem("pixels_transposed"); s_Fe=sem("pixels_ready"); s_T=[sem(f"table_written{i}") for i in range(2)]
        s_ch=sem("dve_chain"); s_lp=sem("dve_loop_chain"); s_xfree=sem("xpad_free"); s_base=sem("base_ready"); s_pc=sem("pool_chain")
        T5=table.rearrange("(b rg) (j c) -> b rg j c",b=B,j=4)
        block=ctx.enter_context(nc.Block())
        @block.sync
        def _(sp):
            for b in range(B):
                sp.dma_start(x_all[:,b,:],A['x'][b].rearrange("c h w -> c (h w)")).then_inc(s_x,16)
            sp.dma_start(w1n[:,:],A['L0_conv_w1'].rearrange("o c a b -> o (c a b)")).then_inc(s_w,16)
            sp.dma_start(w2n[:,:],A['L0_conv_w2'].rearrange("o c a b -> o (c a b)")).then_inc(s_w,16)
            sp.dma_start(wdn[:,:],A['L0_conv_wd'].rearrange("o c a b -> o (c a b)")).then_inc(s_w,16)
            sp.dma_start(b1[:,:],A['L0_conv_b1'].rearrange("(p a) -> p a",a=1)).then_inc(s_b,16)
            sp.dma_start(b2[:,:],A['L0_conv_b2'].rearrange("(a n) -> a n",a=1).to_broadcast([P,NOFF])).then_inc(s_b,16)
            sp.wait_ge(s_zero,1)
            for b in range(B):
                for r0 in (0,PADN):
                    sp.dma_start(table[(b*TROWS+r0)*DG:(b*TROWS+r0+FRONT)*DG,:].rearrange("r c -> (r c)").rearrange("(p n) -> p n",p=P),ztile[:,:]).then_inc(s_edge,16)
            sp.wait_ge(s_edge,16*2*B)
            with sp.Fori(0,B//2) as it:
                for q in range(2):
                    b=it*2+q
                    sp.wait_ge(s_Fe,3*b+6)
                    for j in range(4):
                        o=FRONT-CORNER[j]
                        sp.dma_start(T5[ds(b,1),o*DG:(o+PADN)*DG,j,:].rearrange("b (p rg) c -> (b p) rg c",p=P),
                                     Fs[:,q].rearrange("p r (g c) -> p (r g) c",g=DG)).then_inc(s_T[q],16)
            for q in range(2): sp.wait_ge(s_T[q],16*4*B//2)
        @block.gpsimd
        def _(pool):
            pc=Chain(pool,s_pc)
            pc.mark(nc.gpsimd.memset(ident[:,:],0.0)); pc.mark(nc.gpsimd.memset(gavg[:,:],0.25))
            pc(nc.gpsimd.iota(pxi[:,:],pattern=[[P,NT]],base=0,channel_multiplier=1))
            nc.gpsimd.iota(kyi[:,:],pattern=[[1,3],[0,3]],base=-1,channel_multiplier=0)
            nc.gpsimd.iota(kxi[:,:],pattern=[[0,3],[1,3]],base=-1,channel_multiplier=0)
            nc.gpsimd.iota(gbase[:,:],pattern=[[1,DG]],base=DG*(BASE+FRONT),channel_multiplier=0).then_inc(s_const,1)
            nc.gpsimd.affine_select(out=ident[:,:],in_=ident[:,:],compare_op=ALU.not_equal,fill=1.0,base=0,pattern=[[-1,P]],channel_multiplier=1)
            pc(nc.gpsimd.affine_select(out=gavg[:,:],in_=gavg[:,:],compare_op=ALU.is_ge,fill=0.0,base=0,pattern=[[-4,32],[0,4]],channel_multiplier=1))
            nc.gpsimd.affine_select(out=gavg[:,:],in_=gavg[:,:],compare_op=ALU.is_ge,fill=0.0,base=3,pattern=[[4,32],[0,4]],channel_multiplier=-1).then_inc(s_const,1)
        def trs():
            for t in range(TAPS): yield w1n[:,t::TAPS],w1T[:,t,:],P
            for t in range(TAPS): yield w2n[:,t::TAPS],w2T[:,t,:],NOFF
            for t in range(TAPS): yield wdn[:,t::TAPS],wdT[:,t,:],P
        @block.tensor
        def _(pe):
            pe.wait_ge(s_const,2); pe.wait_ge(s_w,48)
            for n,(src,dst,m) in enumerate(trs()):
                if n>=3: pe.wait_ge(s_wt_ev,n-2)
                nc.tensor.transpose(tp[n%3][:,0,0:m],src,ident[0:m,0:m]).then_inc(s_wt,1)
            pe.wait_ge(s_mean,1)
            nc.tensor.matmul(st_ps[:,:],gavg[:,:],mean[:,:],start=True,stop=True).then_inc(s_gm,1)
            pe.wait_ge(s_var,1)
            nc.tensor.matmul(st_ps[:,:],gavg[:,:],dev[:,:],start=True,stop=True).then_inc(s_gv,1)
            pe.wait_ge(s_wt_ev,27)
            pe.sem_inc(s_c1,4); pe.sem_inc(s_F,6); pe.sem_inc(s_c2,4); pe.sem_inc(s_ot,2)
            with pe.Fori(0,B//2) as it:
                for q in range(2):
                    b=it*2+q
                    pe.wait_ge(s_pad,b+1)
                    xv=xpad[:,q]
                    for r in range(3):
                        nt=min(4,10-4*r)
                        pe.wait_ge(s_Fe,3*b+r)
                        for k in range(nt):
                            last=nc.tensor.transpose(tp[r][:,k,:],xv[:,4*r+k::PADN//P],ident[:,:])
                        last.then_inc(s_F,1)
                    for h in range(2):
                        pe.wait_ge(s_off,b*2+h+1)
                        for t in range(TAPS):
                            o=BASE+(16*h+t//3-1)*PITCH+t%3-1
                            last=nc.tensor.matmul(c1[h][:,:],w1T[:,t,:],xv[:,o:o+16*PITCH].rearrange("p (r w) -> p r w",w=PITCH)[:,:,0:WID],start=(t==0),stop=(t==TAPS-1))
                        last.then_inc(s_c1,1)
                    hv=hpad[:,q]
                    pe.wait_ge(s_h,b*2+4)
                    for h in range(2):
                        pe.wait_ge(s_off,b*2+h+1)
                        for t in range(TAPS):
                            o=BASE+(16*h+t//3-1)*PITCH+t%3-1
                            last=nc.tensor.matmul(c1[h][0:NOFF,:],w2T[:,t,:],hv[:,o:o+16*PITCH].rearrange("p (r w) -> p r w",w=PITCH)[:,:,0:WID],start=(t==0),stop=(t==TAPS-1))
                        last.then_inc(s_c2,1)
                    for m in range(NT):
                        if m%4==0:
                            pe.wait_ge(s_off,b*2+m//4+3)
                            pe.wait_ge(s_c2r,b*2+m//4+1)
                        last=nc.tensor.transpose(c2[m//4][:,m%4,:],off[0:NOFF,m//4,(m%4)*P:(m%4+1)*P],ident[0:NOFF,0:NOFF])
                        if m%4==3: last.then_inc(s_ot,1)
        @block.scalar
        def _(act):
            for n,(src,dst,m) in enumerate(trs()):
                act.wait_ge(s_wt,n+1)
                nc.scalar.copy(dst,tp[n%3][:,0,0:m]).then_inc(s_wt_ev,1)
            act.wait_ge(s_var,2)
            nc.scalar.activation(rstd[:,:],rstd[:,:],ACT.Sqrt).then_inc(s_sq,1)
            act.sem_inc(s_Fe,3); act.sem_inc(s_h,2); act.sem_inc(s_off,2)
            act.wait_ge(s_b,32); act.wait_ge(s_zero,1)
            with act.Fori(0,B//2) as it:
                for q in range(2):
                    b=it*2+q
                    act.wait_ge(s_T[q],it*64)
                    for r in range(3):
                        nt=min(4,10-4*r)
                        act.wait_ge(s_F,b*3+r+7)
                        nc.scalar.activation(Fs[:,q,4*r:4*r+nt,:],tp[r][:,0:nt,:],ACT.Identity).then_inc(s_Fe,1)
                    for h in range(2):
                        act.wait_ge(s_c1,b*2+h+5)
                        act.wait_ge(s_c2,b*2+1)
                        o=BASE+16*h*PITCH
                        nc.scalar.activation(hpad[:,q,o:o+16*PITCH].rearrange("p (r w) -> p r w",w=PITCH)[:,:,0:WID],
                            c1[h][:,:].rearrange("p (r w) -> p r w",w=WID),ACT.Identity,bias=b1[:,0:1]).then_inc(s_h,1)
                    for h in range(2):
                        act.wait_ge(s_c2,b*2+h+5)
                        act.wait_ge(s_ot,b*2+h+1)
                        nc.scalar.activation(off[:,h,:],c1[h][0:NOFF,:],ACT.Identity).then_inc(s_off,1)
        @block.vector
        def _(dve):
            ch=Chain(dve,s_ch)
            nc.vector.memset(xpad[:,:,:],0.0)
            ch.mark(nc.vector.memset(ztile[:,:],0.0))
            ch(nc.vector.memset(hpad[:,:,:],0.0))
            dve.sem_inc(s_zero,1)
            ch.mark(nc.vector.memset(idx_all[:,B*NT*36:],0))
            dve.wait_ge(s_const,2)
            nc.vector.tensor_single_scalar(yi[:,:],pxi[:,:],5,op=ALU.logical_shift_right)
            ch(nc.vector.tensor_single_scalar(xi[:,:],pxi[:,:],31,op=ALU.bitwise_and))
            nc.vector.tensor_copy(pyx[:,:,0],yi[:,:])
            nc.vector.tensor_copy(pyx[:,:,1],xi[:,:])
            nc.vector.tensor_copy(gbf[:,:],gbase[:,:])
            kv=kyx[:,:,:].rearrange("p (g k) two -> p g k two",g=DG)
            nc.vector.tensor_copy(kv[:,:,:,0],kyi[:,:].unsqueeze(1).to_broadcast([P,DG,TAPS]))
            ch(nc.vector.tensor_copy(kv[:,:,:,1],kxi[:,:].unsqueeze(1).to_broadcast([P,DG,TAPS])))
            bv=basec[:,:,:].rearrange("p m (k two) -> p m k two",two=2)
            ch(nc.vector.tensor_tensor(bv,pyx[:,:,:].unsqueeze(2).to_broadcast([P,NT,DG*TAPS,2]),kyx[:,:,:].unsqueeze(1).to_broadcast([P,NT,DG*TAPS,2]),ALU.add))
            dve.wait_ge(s_b,32)
            ch(nc.vector.tensor_tensor(basec[:,:,:],basec[:,:,:],b2[:,:].unsqueeze(1).to_broadcast([P,NT,NOFF]),ALU.add))
            dve.wait_ge(s_x,16*B)
            for b in range(B):
                for h in range(2):
                    last=nc.vector.bn_stats(bst[:,b,h,:],x_all[:,b,h*512:(h+1)*512])
            ch(last)
            for b in range(B): last=nc.vector.bn_aggr(mv[:,b,:],bst[:,b,:,:])
            ch(last)
            nc.vector.tensor_copy(mean[:,:],mv[:,:,0]).then_inc(s_mean,1)
            dve.wait_ge(s_gm,1)
            dve.wait_ge(s_mean,1)
            ch(nc.vector.tensor_copy(mean[:,:],st_ps[:,:]))
            ch(nc.vector.tensor_sub(dev[:,:],mv[:,:,0],mean[:,:]))
            ch(nc.vector.tensor_mul(dev[:,:],dev[:,:],dev[:,:]))
            nc.vector.tensor_add(dev[:,:],dev[:,:],mv[:,:,1]).then_inc(s_var,1)
            dve.wait_ge(s_gv,1)
            nc.vector.tensor_scalar_add(rstd[:,:],st_ps[:,:],1e-5).then_inc(s_var,1)
            dve.wait_ge(s_sq,1)
            ch(nc.vector.reciprocal(rstd[:,:],rstd[:,:]))
            dve.sem_inc(s_c2r,2)
            lc=Chain(dve,s_lp,2*LK)
            with dve.Fori(0,B//2) as it:
                lc.body(it)
                for q in range(2):
                    b=it*2+q
                    def normalize(b,q):
                        nc.vector.tensor_scalar(xpad[:,q,BASE:BASE+WID*PITCH].rearrange("p (r w) -> p r w",w=PITCH)[:,:,0:WID],
                            x_all[:,ds(b,1),:].rearrange("p a (r w) -> p (a r) w",w=WID),mean[:,ds(b,1)],rstd[:,ds(b,1)],ALU.subtract,ALU.mult).then_inc(s_pad,1)
                    normalize(b,q)
                    for m in range(2):
                        dve.wait_ge(s_ot,b*2+m+3)
                        ins=nc.vector.tensor_tensor(pos[:,4*m:4*m+4,:],c2[m][:,:,:],basec[:,4*m:4*m+4,:],ALU.add)
                        lc.mark(ins)
                        if m==1: lc.sync()
                    dve.sem_inc(s_c2r,2)
                    lc(nc.vector.tensor_scalar(pos[:,:,:],pos[:,:,:],-3.0,34.0,ALU.max,ALU.min))
                    lc(nc.vector.tensor_copy(fli[:,:,:],pos[:,:,:]))
                    lc(nc.vector.tensor_copy(fl[:,:,:],fli[:,:,:]))
                    lc(nc.vector.tensor_tensor(gt[:,:,:],fl[:,:,:],pos[:,:,:],ALU.is_gt))
                    lc(nc.vector.tensor_tensor(fl[:,:,:],fl[:,:,:],gt[:,:,:],ALU.subtract))
                    lc(nc.vector.tensor_tensor(whi[:,:,:],pos[:,:,:],fl[:,:,:],ALU.subtract))
                    lc.mark(nc.vector.tensor_scalar(wlo[:,:,:],whi[:,:,:],-1.0,1.0,ALU.mult,ALU.add))
                    lc(nc.vector.tensor_scalar(fl[:,:,:],fl[:,:,:],-2.0,32.0,ALU.max,ALU.min))
                    fv=fl[:,:,:].rearrange("p m (k two) -> p m k two",two=2)
                    lc(nc.vector.scalar_tensor_tensor(ixf[:,:,:],fv[:,:,:,0],float(PITCH),fv[:,:,:,1],ALU.mult,ALU.add))
                    for g in range(DG):
                        lc.mark(nc.vector.tensor_scalar(idx_all[:,ds(b*288,288)].rearrange("p (m k g) -> p m k g",m=NT,k=TAPS)[:,:,:,g],
                            ixf[:,:,g*TAPS:(g+1)*TAPS],float(DG),gbf[:,g:g+1],ALU.mult,ALU.add))
                        for jy,jx in ((0,0),(0,1),(1,0),(1,1)):
                            wy=(wlo,whi)[jy][:,:,:].rearrange("p m (g k two) -> p m g k two",g=DG,two=2)[:,:,g,:,0]
                            wx=(wlo,whi)[jx][:,:,:].rearrange("p m (g k two) -> p m g k two",g=DG,two=2)[:,:,g,:,1]
                            lc.mark(nc.vector.tensor_tensor(w4_all[:,ds(b*1152,1152)].rearrange("p (m k c) -> p m k c",m=NT,k=TAPS)[:,:,:,4*g+2*jy+jx],wy,wx,ALU.mult))
                    lc.sync()
                    lc(nc.vector.tensor_scalar_add(gbf[:,:],gbf[:,:],float(DG*TROWS)))
                lc.end()
LK=32
def rank_phase(nc,A,srclist,seg,start_f,end_f,ident):
    edges=A['L1_ffn_edge_index']
    ctx=ExitStack()
    with ctx:
        sb=lambda n,s,d: ctx.enter_context(nc.sbuf_tensor(n,s,d))
        pb=lambda n,s,d: ctx.enter_context(nc.psum_tensor(n,s,d))
        sem=lambda n: ctx.enter_context(nc.semaphore("r_"+n))
        iota_i=sb("iota_i",[P,P],i32); iota_b=sb("iota_b",[P,P],bf16)
        part=sb("part",[P,1],i32)
        ident_b=sb("ident_b",[P,P],bf16); zeros=sb("zeros",[P,PCOLS],i32); node=sb("node",[P,HI],i32); sti=sb("r_sti",[P,HI],u32)
        before=sb("before",[P,P],f32)
        dst_i=sb("dst_i",[P,2,E_CH],i32); src_i=sb("src_i",[P,2,E_CH],i32)
        lo_i=sb("lo_i",[P,E_CH],i32); hi_i=sb("hi_i",[P,E_CH],i32)
        lo_b=sb("lo_b",[P,E_CH],bf16); hi_b=sb("hi_b",[P,E_CH],bf16)
        dropped=sb("dropped",[P,E_CH],f32)
        OL=sb("OL",[P,2,E_UNIT,P],bf16); OH=sb("OH",[P,2,E_UNIT,HI],bf16)
        OLT=sb("OLT",[P,2,2,4,P],f32)
        Gm=sb("Gm",[P,2,2,4,P],bf16)
        snap=sb("snap",[P,2,E_UNIT+1,HI],f32)
        start1=sb("start1",[P,HI],f32); cnt=sb("cnt",[P,HI],f32); incl=sb("incl",[P,HI],f32); rowb=sb("rowb",[P,1],f32)
        prod=sb("prod",[P,E_UNIT,HI],f32); posf=sb("posf",[P,E_CH],f32)
        pos=sb("pos",[P,2,E_CH],u32); srcs=sb("srcs",[P,2,E_CH],i32)
        D=[pb(f"D{i}",[P,E_UNIT,HI],f32) for i in range(2)]
        OLT16=sb("OLT16",[P,2,2,4,P],bf16); notbefore=sb("notbefore",[P,P],bf16)
        T=[pb(f"T{i}",[P,4,P],bf16) for i in range(2)]
        G=[pb(f"G{i}",[P,4,P],f32) for i in range(2)]
        PP=[pb(f"PP{i}",[P,E_UNIT,HI],f32) for i in range(2)]
        S={}
        def s(n):
            if n not in S: S[n]=sem(n)
            return S[n]
        e_v=edges.rearrange("two (p c) -> two p c",p=P)
        block=ctx.enter_context(nc.Block())
        def load(sp,it,half,free):
            for row,t in ((1,dst_i),(0,src_i)):
                sp.dma_start(t[:,half,:], e_v[row,:,ds(it*2*E_CH+half*E_CH,E_CH)]).then_inc(s(f"ld{half}"),16)
        @block.sync
        def _(sp):
            sp.wait_ge(s("zeros"),1)
            sp.dma_start(srclist.rearrange("(p j) one -> p (j one)",p=P),zeros[:,:]).then_inc(s("cleared"),16)
            for k in range(5):
                sp.dma_start(seg.rearrange("(p k j) c -> k p (j c)",p=P,k=5)[k],zeros[:,:].bitcast(f32)).then_inc(s("cleared"),16)
            for p in range(2):
                with sp.Fori(0,E_ITERS) as it:
                    for half in range(2):
                        sp.wait_ge(s("chunk_used"), it*2+half+1+p*2*E_ITERS)
                        load(sp,it,half,None)
            sp.wait_ge(s("cleared"),96)
        @block.gpsimd
        def _(pool):
            nc.gpsimd.iota(iota_i[:,:],pattern=[[1,P]],base=0,channel_multiplier=0).then_inc(s("cst"),1)
            nc.gpsimd.memset(before[:,:],1.0).then_inc(s("cst"),1)
            nc.gpsimd.memset(ident[:,:],0.0).then_inc(s("cst"),1)
            pool.wait_ge(s("cst"),3)
            nc.gpsimd.affine_select(out=before[:,:],in_=before[:,:],compare_op=ALU.is_gt,fill=0.0,base=0,pattern=[[1,P]],channel_multiplier=-1).then_inc(s("cst"),1)
            nc.gpsimd.affine_select(out=ident[:,:],in_=ident[:,:],compare_op=ALU.not_equal,fill=1.0,base=0,pattern=[[-1,P]],channel_multiplier=1).then_inc(s("cst"),1)
            nc.gpsimd.iota(node[:,:],pattern=[[P,HI]],base=0,channel_multiplier=1).then_inc(s("node"),1)
            pool.wait_ge(s("cleared"),96); pool.wait_ge(s("self_ready"),1); pool.wait_ge(s("node"),1)
            def put(pos_ap,val_ap,done):
                nc.gpsimd.indirect_dma_start(out=srclist,out_offset=bass.IndirectOffsetOnAxis(ap=pos_ap,axis=0),in_=val_ap,in_offset=None,
                    bounds_check=NPOS-1,oob_is_err=False).then_inc(done,16)
            for i in range(HI): put(sti[:,i:i+1],node[:,i:i+1],s("self"))
            with pool.Fori(0,E_ITERS) as it:
                for half in range(2):
                    pool.wait_ge(s("pos_ready"), it*2+half+1)
                    pool.sem_inc(s("go"),1)
                    for j in range(E_CH): put(pos[:,half,j:j+1],srcs[:,half,j:j+1],s(f"scattered{half}"))
            pool.wait_ge(s("self"),16*HI)
            for half in range(2): pool.wait_ge(s(f"scattered{half}"),16*E_CH*E_ITERS)
        @block.scalar
        def _(act):
            with act.Fori(0,E_ITERS*2) as c_:
                for u in range(E_NU):
                    n=c_*E_NU+u
                    for g in range(2):
                        act.wait_ge(s("t_done"),n*2+g+1)
                        act.wait_ge(s("p_done"),n+1)
                        nc.scalar.activation(OLT[:,u%2,g],T[g][:,:,:],ACT.Relu)
                        nc.scalar.activation(OLT16[:,u%2,g],T[g][:,:,:],ACT.Relu).then_inc(s("olt_ready"),1)
                    for g in range(2):
                        act.wait_ge(s("g_done"),n*2+g+1)
                        nc.scalar.activation(Gm[:,u%2,g],G[g][:,:,:],ACT.Relu).then_inc(s("gm_ready"),1)
        @block.tensor
        def _(pe):
            pe.wait_ge(s("cst_b"),1)
            pe.sem_inc(s("cnt_used"),2)
            pe.wait_ge(s("zero_r"),1)
            nc.tensor.matmul(D[0][:,0,:],ident[:,:],start1[:,:],start=True,stop=False,skip_group_check=True)
            with pe.Fori(0,E_ITERS*E_NU) as n2:
                for q in range(2):
                    pe.wait_ge(s("c_ready"),n2*2+q+1)
                    for j in range(E_UNIT):
                        last=nc.tensor.matmul(D[0][:,0,:],OL[:,q,j,:],OH[:,q,j,:],start=False,stop=False,skip_group_check=True)
                    last.then_inc(s("cnt_used"),1)
            nc.tensor.matmul(D[0][:,0,:],ident[:,:],start1[:,:],start=False,stop=True,skip_group_check=True).then_inc(s("cnt_done"),1)
            pe.wait_ge(s("rows"),1)
            nc.tensor.matmul(PP[0][:,0,0:1],before[:,:],incl[:,HI-1:HI],start=True,stop=True).then_inc(s("base"),1)
            pe.sem_inc(s("p_done"),2); pe.sem_inc(s("olt_ready"),2); pe.sem_inc(s("gm_ready"),2)
            with pe.Fori(0,E_ITERS*2) as c_:
                def front(u):
                    n=c_*E_NU+u
                    q=u%2
                    pe.wait_ge(s("oh_ready"),n+1)
                    for g in range(2):
                        pe.wait_ge(s("olt_ready"),n*2+g+1)
                        for j in range(4):
                            last=nc.tensor.transpose(T[g][:,j,:],OL[:,q,4*g+j,:],ident_b[:,:])
                        last.then_inc(s("t_done"),1)
                    pe.wait_ge(s("snap_ready"),n)
                    for i in range(E_UNIT):
                        last=nc.tensor.matmul(D[q][:,i:E_UNIT,:],OL[:,q,i,:],OH[:,q,i:i+1,:].to_broadcast([P,E_UNIT-i,HI]),start=(i==0),stop=(i==E_UNIT-1))
                    last.then_inc(s("d_done"),1)
                    for g in range(2):
                        pe.wait_ge(s("olt_ready"),n*2+g+3)
                        pe.wait_ge(s("gm_ready"),n*2+g+1)
                        for j in range(4):
                            nc.tensor.matmul(G[g][:,j,:],OLT16[:,q,g,j,:],OLT16[:,q,g,j,:],start=True,stop=False)
                            last=nc.tensor.matmul(G[g][:,j,:],ident_b[:,:],notbefore[:,:],start=False,stop=True)
                        last.then_inc(s("g_done"),1)
                def back(u):
                    n=c_*E_NU+u
                    q=u%2
                    pe.wait_ge(s("snap_ready"),n+2)
                    pe.wait_ge(s("p_free"),n+1)
                    for g in range(2):
                        pe.wait_ge(s("gm_ready"),n*2+g+3)
                        for j in range(4):
                            t=4*g+j
                            prior=snap[:,q,t,:]
                            nc.tensor.matmul(PP[q][:,t,:],OLT[:,q,g,j,:],prior,start=True,stop=False)
                            last=nc.tensor.matmul(PP[q][:,t,:],Gm[:,q,g,j,:],OH[:,q,t,:],start=False,stop=True)
                    last.then_inc(s("p_done"),1)
                front(0)
                for u in range(1,E_NU):
                    front(u); back(u-1)
                back(E_NU-1)
        @block.vector
        def _(dve):
            ch=s("dve_chain"); k=[0]
            def link(ins):
                k[0]+=1; ins.then_inc(ch,1); dve.wait_ge(ch,k[0])
            dve.wait_ge(s("cst"),5)
            nc.vector.memset(zeros[:,:],0).then_inc(s("zeros"),1)
            nc.vector.tensor_copy(iota_b[:,:],iota_i[:,:])
            nc.vector.tensor_scalar(notbefore[:,:],before[:,:],1.0,None,ALU.subtract)
            nc.vector.tensor_copy(ident_b[:,:],ident[:,:]).then_inc(s("cst_b"),1)
            nc.vector.memset(start1[:,:],0.0).then_inc(s("zero_r"),1)
            dve.sem_inc(s("chunk_used"),2)
            dve.wait_ge(s("zero_r"),1)
            def split(it,half,p,slink):
                dve.wait_ge(s(f"ld{half}"),(it+1)*32+p*32*E_ITERS)
                nc.vector.tensor_single_scalar(lo_i[:,:],dst_i[:,half,:],127,op=ALU.bitwise_and)
                slink(nc.vector.tensor_single_scalar(hi_i[:,:],dst_i[:,half,:],7,op=ALU.logical_shift_right))
                nc.vector.tensor_copy(lo_b[:,:],lo_i[:,:])
                if p==1:
                    nc.vector.tensor_scalar(dropped[:,:],dst_i[:,half,:],float(M),float(1<<20),ALU.is_ge,ALU.mult)
                slink(nc.vector.tensor_copy(hi_b[:,:],hi_i[:,:]))
            def onehots(q,u):
                nc.vector.tensor_tensor(OL[:,q],lo_b[:,E_UNIT*u:E_UNIT*(u+1)].unsqueeze(2).to_broadcast([P,E_UNIT,P]),
                    iota_b[:,:].unsqueeze(1).to_broadcast([P,E_UNIT,P]),ALU.is_equal)
                return nc.vector.tensor_tensor(OH[:,q],hi_b[:,E_UNIT*u:E_UNIT*(u+1)].unsqueeze(2).to_broadcast([P,E_UNIT,HI]),
                    iota_b[:,0:HI].unsqueeze(1).to_broadcast([P,E_UNIT,HI]),ALU.is_equal)
            with dve.Fori(0,E_ITERS) as it:
                for half in range(2):
                    c=[0]
                    def sl(ins):
                        c[0]+=1; ins.then_inc(s("c_chain"),1); dve.wait_ge(s("c_chain"),it*4+half*2+c[0])
                    split(it,half,0,sl)
                    for u in range(E_NU):
                        n=it*2*E_NU+half*E_NU+u
                        dve.wait_ge(s("cnt_used"),n+1)
                        last=onehots(u%2,u)
                        last.then_inc(s("c_ready"),1)
                    dve.sem_inc(s("chunk_used"),1)
            dve.wait_ge(s("cnt_done"),1)
            link(nc.vector.tensor_scalar_add(cnt[:,:],D[0][:,0,:],1.0))
            nc.vector.tensor_tensor_scan(out=incl[:,:],data0=cnt[:,:],data1=cnt[:,:],initial=0.0,op0=ALU.add,op1=ALU.bypass).then_inc(s("rows"),1)
            dve.wait_ge(s("rows"),1)
            dve.wait_ge(s("base"),1)
            link(nc.vector.tensor_copy(rowb[:,:],PP[0][:,0,0:1]))
            link(nc.vector.tensor_sub(start1[:,:],incl[:,:],cnt[:,:]))
            nc.vector.tensor_scalar(start1[:,:],start1[:,:],rowb[:,0:1],1.0,ALU.add,ALU.add).then_inc(s("fin"),1)
            dve.wait_ge(s("fin"),1)
            link(nc.vector.tensor_scalar_add(start_f[:,:],start1[:,:],-1.0))
            nc.vector.tensor_copy(sti[:,:],start_f[:,:]).then_inc(s("self_ready"),1)
            link(nc.vector.tensor_tensor(end_f[:,:],start_f[:,:],cnt[:,:],ALU.add))
            link(nc.vector.tensor_scalar_add(end_f[:,:],end_f[:,:],-1.0))
            nc.vector.tensor_copy(snap[:,1,E_UNIT,:],start1[:,:]).then_inc(s("snap_ready"),1)
            dve.sem_inc(s("p_free"),2)
            with dve.Fori(0,E_ITERS) as it:
                for half in range(2):
                    c=[0]
                    K=2+E_NU+1
                    def sl(ins):
                        c[0]+=1; ins.then_inc(s("m_chain"),1); dve.wait_ge(s("m_chain"),it*2*K+half*K+c[0])
                    split(it,half,1,sl)
                    def gen(u):
                        n=it*2*E_NU+half*E_NU+u
                        dve.wait_ge(s("p_done"),n+1)
                        onehots(u%2,u).then_inc(s("oh_ready"),1)
                    def snapshot(u):
                        n=it*2*E_NU+half*E_NU+u
                        dve.wait_ge(s("d_done"),n+1)
                        dve.wait_ge(s("p_done"),n+1)
                        dve.wait_ge(s("snap_ready"),n+1)
                        nc.vector.tensor_copy(snap[:,u%2,0],snap[:,1-u%2,E_UNIT])
                        nc.vector.tensor_tensor(snap[:,u%2,1:E_UNIT+1],D[u%2][:,:,:],snap[:,1-u%2,E_UNIT:E_UNIT+1,:].to_broadcast([P,E_UNIT,HI]),ALU.add).then_inc(s("snap_ready"),1)
                    def extract(u):
                        n=it*2*E_NU+half*E_NU+u
                        dve.wait_ge(s("p_done"),n+3)
                        dve.wait_ge(s("p_free"),n+2)
                        sl(nc.vector.tensor_tensor(prod[:,:,:],PP[u%2][:,:,:],OH[:,u%2],ALU.mult))
                        nc.vector.tensor_reduce(posf[:,E_UNIT*u:E_UNIT*(u+1)],prod[:,:,:],axis=AX.X,op=ALU.add).then_inc(s("p_free"),1)
                    gen(0); gen(1); snapshot(0)
                    for u in range(E_NU):
                        if u+1<E_NU: snapshot(u+1)
                        extract(u)
                        if u+2<E_NU: gen(u+2)
                    dve.wait_ge(s("p_free"),(it*2*E_NU+half*E_NU+E_NU)+2)
                    dve.wait_ge(s(f"scattered{half}"),it*16*E_CH)
                    sl(nc.vector.tensor_tensor(posf[:,:],posf[:,:],dropped[:,:],ALU.add))
                    nc.vector.tensor_copy(pos[:,half,:],posf[:,:])
                    nc.vector.tensor_scalar_min(srcs[:,half,:],src_i[:,half,:],float(M-1)).then_inc(s("pos_ready"),1)
                    dve.wait_ge(s("pos_ready"),it*2+half+1)
                    dve.sem_inc(s("chunk_used"),1)

def mix_phase(nc,A,table,x_all,t_all,idx_all,w4_all,wdT,ident):
    with ExitStack() as ctx:
        sb=lambda n,s,d: ctx.enter_context(nc.sbuf_tensor(n,s,d))
        sem=lambda n: ctx.enter_context(nc.semaphore("m_"+n))
        bank=[ctx.enter_context(nc.psum_tensor(f"bank{i}",[P,4,P],f32)) for i in range(8)]
        stage=sb("stage",[P,3,12],u32)
        patch=sb("patch",[P,3,3,DG,4*CG],f32)
        wp=sb("wp",[P,2,3,4,DG,CG],f32)
        vT=sb("vT",[P,2,3,P],f32)
        rl=sb("rl",[P,2,P],f32)
        tn=sb("tn",[P,2,P],f32); st=sb("lnst",[P,NT,6],f32); mv=sb("lnmv",[P,NT,2],f32); rs=sb("lnrs",[P,NT],f32)
        tnT=sb("tnT",[P,HW],f32)
        wnat=sb("wnat",[P,3,P*HEADS],f32)
        WqT=sb("WqT",[P,HEADS,P],f32); WkT=sb("WkT",[P,P],f32); WvT=sb("WvT",[P,P],f32); WoT=sb("WoT",[P,NT,P],f32)
        KT=sb("KT",[P,8,P],f32); V=sb("V",[P,8,P],f32); QT=sb("QT",[P,HW],f32)
        pr=sb("pr",[P,2,HW],f32); mx=sb("mx",[P,2],f32); nmx=sb("nmx",[P,2],f32); sm=sb("sm",[P,2],f32); ri=sb("ri",[P,2],f32)
        wos=sb("wos",[P,2,P],f32); GT=sb("GT",[P,HW],f32); Gs=sb("Gs",[P,8,P],f32)
        sm2=sb("sm2",[P,2,2],f32); mx2=sb("mx2",[P,2,2],f32)
        s_stage=[sem(f"staged{i}") for i in range(3)]; s_patch=[sem(f"patches{i}") for i in range(3)]
        xs=sb("xs",[P,2,P],f32); wqh=sb("wqh",[P,P],f32); s_go=sem("go"); s_xs=sem("x_tile"); s_pj=sem("projected"); s_wqh=sem("wq_head")
        s_w=sem("weights"); s_wt=sem("wt"); s_wte=sem("wt_out"); s_wp=sem("weighted"); s_v=sem("sampled"); s_ve=sem("sampled_out"); s_conv=sem("conv_done"); s_rl=sem("relu_out")
        s_t=sem("tokens"); s_ch=sem("dve_chain"); s_l=sem("dve_loop"); s_var=sem("variance"); s_sd=sem("deviation")
        s_tn=sem("normalized"); s_tt=sem("tn_transposed"); s_tte=sem("tnT_ready"); s_kv=sem("kv_done"); s_kve=sem("kv_ready")
        s_q=sem("q_done"); s_qe=sem("q_ready"); s_s=sem("scores"); s_m=sem("max_ready"); s_p=sem("probs"); s_wo=sem("scaled_wo"); s_g=sem("gathered")
        s_ge=sem("GT_ready"); s_gt=sem("G_transposed"); s_gs=sem("G_ready"); s_o=sem("head_out"); s_a=sem("head_added")
        block=ctx.enter_context(nc.Block())
        @block.sync
        def _(sp):
            sp.dma_start(wnat[:,0,:].rearrange("p (h c) -> p h c",c=P),A['L1_attn_Wq'].rearrange("(h p) c -> p h c",p=P)).then_inc(s_w,16)
            sp.dma_start(wnat[:,1,0:P],A['L1_attn_Wk']).then_inc(s_w,16)
            sp.dma_start(wnat[:,1,P:2*P],A['L1_attn_Wv']).then_inc(s_w,16)
            sp.dma_start(wnat[:,2,:],A['L1_attn_Wo']).then_inc(s_w,16)
        @block.gpsimd
        def _(pool):
            with pool.Fori(0,B*NT) as g:
                for k in range(3):
                    pool.wait_ge(s_stage[k],g+1)
                    pool.sem_inc(s_go,1)
                    for i in range(12):
                        nc.gpsimd.indirect_dma_start(out=patch[:,k,i//DG,i%DG,:],out_offset=None,in_=table,
                            in_offset=bass.IndirectOffsetOnAxis(ap=stage[:,k,i:i+1],axis=0)).then_inc(s_patch[k],16)
        wts=[(wnat[:,0,h*P:(h+1)*P],WqT[:,h,:]) for h in range(HEADS)]+[(wnat[:,1,0:P],WkT[:,:]),(wnat[:,1,P:2*P],WvT[:,:])]+[(wnat[:,2,i*P:(i+1)*P],WoT[:,i,:]) for i in range(NT)]
        @block.tensor
        def _(pe):
            pe.wait_ge(s_w,64)
            for n,(src,dst) in enumerate(wts):
                if n>=4: pe.wait_ge(s_wte,n-3)
                nc.tensor.transpose(bank[n%4][:,0,:],src,ident[:,:]).then_inc(s_wt,1)
            pe.wait_ge(s_wte,len(wts))
            pe.sem_inc(s_v,2); pe.sem_inc(s_pj,2); pe.sem_inc(s_conv,2); pe.sem_inc(s_tt,2); pe.sem_inc(s_g,2); pe.sem_inc(s_q,2)
            with pe.Fori(0,B) as b:
                with pe.Fori(0,NT//2) as m2:
                    for q in range(2):
                        g=b*NT+m2*2+q
                        def sample(k):
                            i=(q*3+k)%2
                            pe.wait_ge(s_wp,g*3+k+1)
                            pe.wait_ge(s_ve,g*3+k+1)
                            for t in range(3):
                                for j in range(4):
                                    last=nc.tensor.matmul(bank[i][:,t,:],wp[:,i,t,j].rearrange("p g c -> p (g c)"),ident[:,:],start=(j==0),stop=(j==3))
                            last.then_inc(s_v,1)
                        def project(k):
                            i=(q*3+k)%2
                            pe.wait_ge(s_ve,g*3+k+3)
                            for t in range(3):
                                last=nc.tensor.matmul(bank[2+q][:,0,:],vT[:,i,t,:],wdT[:,3*k+t,:],start=(k+t==0),stop=(k==2 and t==2))
                            last.then_inc(s_pj,1)
                            if k==2:
                                pe.wait_ge(s_xs,g+1)
                                last=nc.tensor.transpose(bank[4+q][:,0,:],xs[:,q,:],ident[:,:])
                                last.then_inc(s_conv,1)
                        pe.wait_ge(s_t,g+1)
                        sample(0); sample(1); project(0); sample(2); project(1); project(2)
                with pe.Fori(0,NT//2) as m2:
                    for q in range(2):
                        pe.wait_ge(s_tn,b*NT+m2*2+q+1)
                        pe.wait_ge(s_tte,b*NT+m2*2+q+1)
                        nc.tensor.transpose(bank[q][:,0,:],tn[:,q,:],ident[:,:]).then_inc(s_tt,1)
                pe.wait_ge(s_tte,b*NT+NT+2)
                for n,(w,h) in enumerate(((WkT,0),(WkT,1),(WvT,0),(WvT,1))):
                    nc.tensor.matmul(bank[2+n][:,:,:],w[:,:],tnT[:,h*512:(h+1)*512],start=True,stop=True).then_inc(s_kv,1)
                pe.wait_ge(s_kve,b*4+4)
                pe.sem_inc(s_go,1)
                with pe.Fori(0,HEADS) as h:
                    hh=b*HEADS+h
                    pe.wait_ge(s_a,hh+1)
                    pe.wait_ge(s_wqh,hh+1)
                    for i in range(2):
                        nc.tensor.matmul(bank[6+i][:,:,:],wqh[:,:],tnT[:,i*512:(i+1)*512],start=True,stop=True).then_inc(s_q,1)
                    pe.wait_ge(s_qe,hh*2+2)
                    def scores(i):
                        pe.wait_ge(s_p,hh*NT+i+1)
                        for k in range(2):
                            last=nc.tensor.matmul(bank[2*(i%2)+k][:,:,:],QT[:,i*P:(i+1)*P],KT[:,4*k:4*k+4,:],start=True,stop=True)
                        last.then_inc(s_s,1)
                    def gather(i):
                        pe.wait_ge(s_p,hh*NT+i+3); pe.wait_ge(s_wo,hh*NT+i+1)
                        for k in range(2):
                            last=nc.tensor.matmul(bank[4+k][:,:,:],wos[:,i%2,:],pr[:,i%2,k*512:(k+1)*512],start=(i==0),stop=(i==NT-1))
                        last.then_inc(s_g,1)
                    scores(0); scores(1)
                    for i in range(NT):
                        gather(i)
                        if i+2<NT: scores(i+2)
                    for k in range(2):
                        pe.wait_ge(s_ge,hh*2+k+1)
                        for j in range(4):
                            last=nc.tensor.transpose(bank[6+k][:,j,:],GT[:,(4*k+j)*P:(4*k+j+1)*P],ident[:,:])
                        last.then_inc(s_gt,1)
                    for j in range(8):
                        if j%4==0: pe.wait_ge(s_gs,hh*2+j//4+1)
                        last=nc.tensor.matmul(bank[0][:,0,:],V[:,j,:],Gs[:,j,:],start=(j==0),stop=(j==7))
                    last.then_inc(s_o,1)
        @block.scalar
        def _(act):
            for n,(src,dst) in enumerate(wts):
                act.wait_ge(s_wt,n+1)
                nc.scalar.copy(dst,bank[n%4][:,0,:]).then_inc(s_wte,1)
            act.sem_inc(s_ve,2); act.sem_inc(s_tte,2); act.sem_inc(s_p,2)
            with act.Fori(0,B) as b:
                with act.Fori(0,NT//2) as m2:
                    for q in range(2):
                        g=b*NT+m2*2+q
                        for k in range(3):
                            i=(q*3+k)%2
                            act.wait_ge(s_v,g*3+k+3)
                            act.wait_ge(s_pj,g*3+k+1)
                            nc.scalar.activation(vT[:,i],bank[i][:,0:3,:],ACT.Identity).then_inc(s_ve,1)
                        act.wait_ge(s_conv,g+3)
                        act.wait_ge(s_t,g+1)
                        nc.scalar.activation(rl[:,q,:],bank[2+q][:,0,:],ACT.Relu).then_inc(s_rl,1)
                act.wait_ge(s_var,b+1)
                nc.scalar.activation(rs[:,:],rs[:,:],ACT.Sqrt).then_inc(s_sd,1)
                with act.Fori(0,NT//2) as m2:
                    for q in range(2):
                        act.wait_ge(s_tt,b*NT+m2*2+q+3)
                        nc.scalar.activation(tnT[:,ds((m2*2+q)*P,P)],bank[q][:,0,:],ACT.Identity).then_inc(s_tte,1)
                for n in range(4):
                    act.wait_ge(s_kv,b*4+n+1)
                    if n<2:
                        nc.scalar.activation(KT[:,:,n*64:(n+1)*64],bank[2+n][:,:,:].rearrange("p a b -> p (a b)").rearrange("p (o j) -> p j o",j=8),ACT.Identity).then_inc(s_kve,1)
                    else:
                        nc.scalar.activation(V[:,4*(n-2):4*(n-2)+4,:],bank[2+n][:,:,:],ACT.Identity).then_inc(s_kve,1)
                with act.Fori(0,HEADS) as h:
                    hh=b*HEADS+h
                    act.wait_ge(s_q,hh*2+2)
                    nc.scalar.activation(wqh[:,:],WqT[:,ds(h,1),:].rearrange("p a c -> p (a c)"),ACT.Identity).then_inc(s_wqh,1)
                    for i in range(2):
                        act.wait_ge(s_q,hh*2+i+3)
                        nc.scalar.activation(QT[:,i*512:(i+1)*512],bank[6+i][:,:,:].rearrange("p a b -> p (a b)"),ACT.Identity).then_inc(s_qe,1)
                    for i in range(NT):
                        q=i%2
                        act.wait_ge(s_m,hh*NT+i+1)
                        act.wait_ge(s_g,hh*NT+i+1)
                        for k in range(2):
                            last=nc.scalar.activation(pr[:,q,k*512:(k+1)*512],bank[2*q+k][:,:,:].rearrange("p a b -> p (a b)"),ACT.Exp,bias=nmx[:,q:q+1],scale=0.25,accum_out=sm2[:,q,k:k+1])
                        last.then_inc(s_p,1)
                    for k in range(2):
                        act.wait_ge(s_g,hh*NT+NT+2)
                        nc.scalar.activation(GT[:,k*512:(k+1)*512],bank[4+k][:,:,:].rearrange("p a b -> p (a b)"),ACT.Identity).then_inc(s_ge,1)
                    for k in range(2):
                        act.wait_ge(s_gt,hh*2+k+1)
                        nc.scalar.activation(Gs[:,4*k:4*k+4,:],bank[6+k][:,:,:],ACT.Identity).then_inc(s_gs,1)
        idx_v=idx_all[:,:]
        @block.vector
        def _(dve):
            dve.sem_inc(s_t,2); dve.sem_inc(s_a,1); 
            for k in range(3):
                nc.vector.tensor_copy(stage[:,k,:],idx_all[:,12*k:12*k+12]).then_inc(s_stage[k],1)
            lc=Chain(dve,s_l,LKM); hc=Chain(dve,s_ch,HKM)
            with dve.Fori(0,B) as b:
                with dve.Fori(0,NT//2) as m2:
                    for q in range(2):
                        g=b*NT+m2*2+q
                        dve.wait_ge(s_conv,g+1)
                        nc.vector.tensor_copy(xs[:,q,:],x_all[:,ds(b,1),ds((m2*2+q)*P,P)].rearrange("p a n -> p (a n)")).then_inc(s_xs,1)
                        for k in range(3):
                            i=(q*3+k)%2
                            dve.wait_ge(s_patch[k],g*192+192)
                            dve.wait_ge(s_v,g*3+k+1)
                            for t in range(3):
                                last=nc.vector.tensor_tensor(wp[:,i,t].rearrange("p j g c -> p g j c"),
                                    patch[:,k,t].rearrange("p g (j c) -> p g j c",j=4),
                                    w4_all[:,ds((g)*144+(3*k+t)*16,16)].rearrange("p (g j) -> p g j",j=4).unsqueeze(3).to_broadcast([P,DG,4,CG]),ALU.mult)
                            last.then_inc(s_wp,1)
                            dve.wait_ge(s_wp,g*3+k+1)
                            nc.vector.tensor_copy(stage[:,k,:],idx_all[:,ds((g+1)*36+12*k,12)]).then_inc(s_stage[k],1)
                        dve.wait_ge(s_rl,g+1)
                        nc.vector.tensor_tensor(t_all[:,ds(g,1),:].rearrange("p a c -> p (a c)"),bank[4+q][:,0,:],rl[:,q,:],ALU.add).then_inc(s_t,1)
                dve.wait_ge(s_t,b*NT+NT+2)
                lc.body(b)
                for m in range(NT):
                    lc.mark(nc.vector.bn_stats(st[:,m,:],t_all[:,ds(b*NT+m,1),:].rearrange("p a c -> p (a c)")))
                lc.sync()
                dve.sem_inc(s_go,1)
                for m in range(NT): lc.mark(nc.vector.bn_aggr(mv[:,m,:],st[:,m,:]))
                lc.sync()
                nc.vector.tensor_scalar_add(rs[:,:],mv[:,:,1],1e-5).then_inc(s_var,1)
                dve.wait_ge(s_sd,b+1)
                lc(nc.vector.reciprocal(rs[:,:],rs[:,:]))
                for m in range(NT):
                    dve.wait_ge(s_tt,b*NT+m+1)
                    nc.vector.tensor_scalar(tn[:,m%2,:],t_all[:,ds(b*NT+m,1),:].rearrange("p a c -> p (a c)"),mv[:,m,0:1],rs[:,m:m+1],ALU.subtract,ALU.mult).then_inc(s_tn,1)
                lc.end()
                with dve.Fori(0,HEADS) as h:
                    hh=b*HEADS+h
                    hc.body(hh)
                    def maximum(i):
                        q=i%2
                        dve.wait_ge(s_s,hh*NT+i+1)
                        hc.mark(nc.vector.reduce_max(mx2[:,q,0:1],bank[2*q][:,:,:].rearrange("p a b -> p (a b)"),AX.X))
                        hc(nc.vector.reduce_max(mx2[:,q,1:2],bank[2*q+1][:,:,:].rearrange("p a b -> p (a b)"),AX.X))
                        hc(nc.vector.tensor_tensor(mx[:,q:q+1],mx2[:,q,0:1],mx2[:,q,1:2],ALU.max))
                        nc.vector.tensor_scalar_mul(nmx[:,q:q+1],mx[:,q:q+1],-0.25).then_inc(s_m,1)
                    def scale_wo(i):
                        q=i%2
                        dve.wait_ge(s_p,hh*NT+i+3)
                        hc(nc.vector.tensor_tensor(sm[:,q:q+1],sm2[:,q,0:1],sm2[:,q,1:2],ALU.add))
                        hc(nc.vector.reciprocal(ri[:,q:q+1],sm[:,q:q+1]))
                        nc.vector.tensor_scalar(wos[:,q,:],WoT[:,i,:],ri[:,q:q+1],None,ALU.mult).then_inc(s_wo,1)
                    maximum(0)
                    for i in range(NT):
                        if i+1<NT: maximum(i+1)
                        scale_wo(i)
                    dve.wait_ge(s_o,hh+1)
                    nc.vector.tensor_tensor(t_all[:,ds(hh,1),:].rearrange("p a c -> p (a c)"),bank[0][:,0,:],t_all[:,ds(hh,1),:].rearrange("p a c -> p (a c)"),ALU.add).then_inc(s_a,1)
                    hc.end()
LKM=17; HKM=8*5
def gat_phase(nc,A,O,t_all,start_f,end_f,srclist,seg,pay_d,res_d,car_d,ident):
    with ExitStack() as ctx:
        sb=lambda n,s,d: ctx.enter_context(nc.sbuf_tensor(n,s,d))
        sem=lambda n: ctx.enter_context(nc.semaphore("g_"+n))
        bank=[ctx.enter_context(nc.psum_tensor(f"gb{i}",[P,4,P],f32)) for i in range(8)]
        W=sb("Wg",[P,HF],f32); att=sb("att",[P,2,HF],f32); cst=sb("lncst",[P,3,HF],f32)
        b1=sb("b1f",[P,EXP,2],f32); b2=sb("b2f",[P,EXP*P],f32)
        W1=sb("W1s",[P,EXP,2*P],f32); W2=sb("W2s",[P,EXP,2,P],f32)
        st=sb("st2",[P,NT,6],f32); mv=sb("mv2",[P,NT,2],f32); rs=sb("rs2",[P,NT],f32)
        tn=sb("tn_2",[P,2,P],f32); tT=sb("tT",[P,2,P],f32); tnT=sb("tn2T",[P,NODES],f32)
        h_all=sb("h_all",[P,HI,HF],f32); pm=sb("pm",[P,HI,HF],f32)
        pay=sb("pay",[P,HI,PAY],f32); seg_row=sb("seg_row",[P,HI,5],f32)
        sti=sb("sti",[P,HI],u32); eni=sb("eni",[P,HI],u32)
        idx=sb("g_idx",[P,2,CHK],i32); G=sb("G_in",[P,2,CHK,PAY],f32); D=sb("D_in",[P,2,CHK,5],f32)
        ns=sb("ns",[P,CHK],f32); ng=sb("ng",[P,CHK],f32); ad=sb("ad",[P,EXP,CHK],f32); adc=sb("adc",[P,EXP],f32)
        e=sb("e",[P,EXP,CHK],f32); ex=sb("ex",[P,2,EXP,CHK],f32); nm=sb("nm",[P,HF,CHK],f32)
        res=sb("res",[P,2,CHK+1,RES],f32); anys=sb("anys",[P,2],f32)
        s_w=sem("weights"); s_ch=sem("dve_chain"); s_l=sem("dve_ln"); s_var=sem("var"); s_sd=sem("sd"); s_tn=sem("tn"); s_tt=sem("tt"); s_te=sem("tT"); s_h=sem("h"); s_he=sem("h_out")
        s_pay=sem("pay_ready"); s_payd=sem("pay_written"); s_segr=sem("seg_ready"); s_segd=sem("seg_written")
        s_in=[sem(f"chunk_in{i}") for i in range(2)]; s_D=[sem(f"seg_in{i}") for i in range(2)]; s_G=[sem(f"payload{i}") for i in range(2)]; s_used=sem("chunk_used"); s_go=sem("go")
        s_c=sem("dve_scan_chain"); s_e=sem("exp_in"); s_ex=sem("exp_out"); s_r=sem("res_ready"); s_rd=[sem(f"res_written{i}") for i in range(2)]
        s_x=sem("expand"); s_xt=sem("expand_T"); s_x1=sem("x1"); s_x2=sem("x2"); s_cr=sem("carry"); s_crT=sem("carryT"); s_cd=sem("carry_written"); s_ci=sem("carry_sb")
        s_en=sem("ends"); s_gr=sem("ends_in"); s_y1=sem("y1"); s_y2=sem("y2"); s_gate=sem("gate"); s_f=sem("ffn_h"); s_fe=sem("ffn_he"); s_y=sem("ffn_y"); s_ye=sem("ffn_ye"); s_o=sem("oT"); s_oe=sem("oTe"); s_out=[sem(f"out{i}") for i in range(2)]
        resv=res_d.rearrange("(p j) c -> p j c",p=P); segv=seg.rearrange("(p j) c -> p j c",p=P); srcv=srclist.rearrange("(p j) one -> p (j one)",p=P)
        y=sb("y",[P,2,EXP*P],f32); acc=sb("accf",[P,2,P],f32); 
        qi=sb("qi",[P,HI],u32)
        carry=sb("carry",[P,2*PAY],f32)
        rloc=sb("rloc",[P,HI,RES],f32); rcar=sb("rcar",[P,HI,2*PAY],f32)
        ms=sb("mS_",[P,3,PAY],f32); mT=sb("mT",[PAY,3,P],f32); cm=sb("cm",[PAY,2,P+1],f32); xt=sb("xt",[PAY,2,P],f32)
        gate=sb("gate",[P,HI,EXP],f32)
        hT=sb("hT",[P,EXP,2,512],f32); oT=sb("oT",[P,2,512],f32)
        acc4=sb("acc4",[P,4,P],f32)
        s_yd=sem("ffn_used")
        abx=sb("abx",[P,HI,8],f32); vv=sb("vv",[P,HI],f32)
        q4=sb("q4",[P,4,HI],f32); mm=sb("mm",[P,HI,EXP],f32); num=sb("num",[P,HI,PAY],f32); tmp=sb("tmp",[P,HI,PAY],f32)
        mu=sb("mu",[P,HI],f32); sc=sb("sc",[P,HI,EXP],f32); rk=sb("rk",[P,HI,EXP],f32); cc=sb("cc",[P,HI],f32)
        s_fc=sem("ffn_chain")
        block=ctx.enter_context(nc.Block())
        @block.sync
        def _(sp):
            bc=lambda ap,n: ap.to_broadcast([P,n])
            sp.dma_start(W[:,:],A['L1_ffn_W_gat']).then_inc(s_w,16)
            sp.dma_start(att[:,0,:],bc(A['L1_ffn_att_src'].rearrange("(a h) k -> a (h k)",a=1),HF)).then_inc(s_w,16)
            sp.dma_start(att[:,1,:],bc(A['L1_ffn_att_dst'].rearrange("(a h) k -> a (h k)",a=1),HF)).then_inc(s_w,16)
            for i,n in enumerate(('b_gat','ln_gamma','ln_beta')):
                sp.dma_start(cst[:,i,:],bc(A['L1_ffn_'+n].rearrange("(a k) -> a k",a=1),HF)).then_inc(s_w,16)
            sp.dma_start(b1[:,:,:],A['L1_ffn_b1'].rearrange("e (f p) -> p e f",p=P),allow_slow_non_contiguous=True).then_inc(s_w,16)
            sp.dma_start(b2[:,:],bc(A['L1_ffn_b2'].rearrange("(a e) c -> a (e c)",a=1),EXP*P)).then_inc(s_w,16)
            sp.dma_start(W1[:,:,:],A['L1_ffn_W1'].rearrange("e c f -> c e f")).then_inc(s_w,16)
            for ee in range(EXP): sp.dma_start(W2[:,ee],A['L1_ffn_W2'][ee].rearrange("(f p) c -> p f c",p=P)).then_inc(s_w,16)
            sp.wait_ge(s_pay,1)
            sp.dma_start(pay_d.rearrange("(i p) c -> p i c",p=P),pay[:,:,:]).then_inc(s_payd,16)
            sp.wait_ge(s_segd,16*HI)
            with sp.Fori(0,NCH//2) as it:
                for q in range(2):
                    c=it*2+q
                    sp.wait_ge(s_used,c+1)
                    sp.dma_start(idx[:,q,:],srcv[:,ds(c*CHK,CHK)]).then_inc(s_in[q],16)
                    sp.dma_start(D[:,q],segv[:,ds(c*CHK,CHK),:]).then_inc(s_D[q],16)
            sp.wait_ge(s_ci,1)
            sp.dma_start(car_d,carry[:,:]).then_inc(s_cd,16)
        @block.gpsimd
        def _(pool):
            pool.wait_ge(s_segr,1)
            for i in range(HI):
                nc.gpsimd.indirect_dma_start(out=seg,out_offset=bass.IndirectOffsetOnAxis(ap=sti[:,i:i+1],axis=0),in_=seg_row[:,i,:],in_offset=None).then_inc(s_segd,16)
            pool.wait_ge(s_payd,16)
            with pool.Fori(0,NCH//2) as it:
                for q in range(2):
                    pool.wait_ge(s_used,it*2+q+1)
                    pool.sem_inc(s_go,1)
                    pool.wait_ge(s_in[q],it*16+16)
                    pool.sem_inc(s_go,1)
                    for i in range(CHK):
                        nc.gpsimd.indirect_dma_start(out=G[:,q,i,:],out_offset=None,in_=pay_d,in_offset=bass.IndirectOffsetOnAxis(ap=idx[:,q,i:i+1],axis=0)).then_inc(s_G[q],16)
            for q in range(2): pool.wait_ge(s_rd[q],16*NCH//2)
            pool.wait_ge(s_cd,16); pool.wait_ge(s_en,1)
            for i in range(HI):
                nc.gpsimd.indirect_dma_start(out=rloc[:,i,:],out_offset=None,in_=res_d,in_offset=bass.IndirectOffsetOnAxis(ap=eni[:,i:i+1],axis=0)).then_inc(s_gr,16)
                nc.gpsimd.indirect_dma_start(out=rcar[:,i,:],out_offset=None,in_=car_d,in_offset=bass.IndirectOffsetOnAxis(ap=qi[:,i:i+1],axis=0)).then_inc(s_gr,16)
        @block.tensor
        def _(pe):
            pe.wait_ge(s_w,16*13)
            pe.sem_inc(s_tt,2); pe.sem_inc(s_h,2)
            with pe.Fori(0,HI//2) as it:
                for q in range(2):
                    g=it*2+q
                    pe.wait_ge(s_tn,g+1)
                    pe.wait_ge(s_te,g+1)
                    nc.tensor.transpose(bank[q][:,0,:],tn[:,q,:],ident[:,:]).then_inc(s_tt,1)
                    pe.wait_ge(s_te,g+3)
                    pe.wait_ge(s_he,g+1)
                    nc.tensor.matmul(bank[2+q][:,0,0:HF],tT[:,q,:],W[:,:],start=True,stop=True).then_inc(s_h,1)
            pe.wait_ge(s_x,1)
            for i in range(3):
                last=nc.tensor.transpose(bank[4+i][0:PAY,0,:],ms[:,i,:],ident[:,:])
            last.then_inc(s_xt,1)
            pe.wait_ge(s_cr,1)
            for i in range(2):
                last=nc.tensor.transpose(bank[i][:,0,0:PAY],cm[:,i,0:P],ident[0:PAY,0:PAY])
            last.then_inc(s_crT,1)
            pe.wait_ge(s_ci,1)
            pe.wait_ge(s_gate,1)
            with pe.Fori(0,NODES//512) as it:
                for ef in range(8):
                    pe.wait_ge(s_fe,it*8+ef+1)
                    nc.tensor.matmul(bank[ef%2][:,:,:],W1[:,ef//2,(ef%2)*P:(ef%2+1)*P],tnT[:,ds(it*512,512)],start=True,stop=True).then_inc(s_f,1)
                for m in range(4):
                    pe.wait_ge(s_ye,it*4+m+1)
                    pe.wait_ge(s_fe,it*8+10)
                    for ee in range(EXP):
                        for f in range(2):
                            last=nc.tensor.matmul(bank[2+m%2][:,ee,:],hT[:,ee,f,m*P:(m+1)*P],W2[:,ee,f,:],start=(f==0),stop=(f==1))
                    last.then_inc(s_y,1)
                for m in range(4):
                    pe.wait_ge(s_ye,it*4+m+3)
                    if m==0: pe.wait_ge(s_oe,it+1)
                    last=nc.tensor.transpose(bank[4][:,m,:],acc4[:,m,:],ident[:,:])
                last.then_inc(s_o,1)
        @block.scalar
        def _(act):
            act.sem_inc(s_te,2); act.sem_inc(s_fe,2); act.sem_inc(s_oe,1)
            with act.Fori(0,B) as b:
                act.wait_ge(s_var,b+1)
                nc.scalar.activation(rs[:,:],rs[:,:],ACT.Sqrt).then_inc(s_sd,1)
                for m in range(NT):
                    g=b*NT+m; q=m%2
                    act.wait_ge(s_tt,g+3)
                    act.wait_ge(s_h,g+1)
                    nc.scalar.activation(tnT[:,ds(g*P,P)],bank[q][:,0,:],ACT.Identity)
                    nc.scalar.activation(tT[:,q,:],bank[q][:,0,:],ACT.Identity).then_inc(s_te,1)
            with act.Fori(0,NCH//2) as it:
                for q in range(2):
                    c=it*2+q
                    act.wait_ge(s_e,c+1)
                    nc.scalar.activation(ex[:,:,:,:],ex[:,:,:,:],ACT.Exp).then_inc(s_ex,1)
                    act.wait_ge(s_r,c+1)
                    act.dma_start(resv[:,ds(c*CHK,CHK),:],res[:,q,1:CHK+1,:]).then_inc(s_rd[q],16)
            act.wait_ge(s_x1,1)
            nc.scalar.activation(xt[:,:,:],xt[:,:,:],ACT.Exp).then_inc(s_x2,1)
            act.wait_ge(s_y1,1)
            nc.scalar.activation(abx[:,:,:],abx[:,:,:],ACT.Exp).then_inc(s_y2,1)
            act.wait_ge(s_y1,2)
            nc.scalar.activation(vv[:,:],vv[:,:],ACT.Sqrt).then_inc(s_y2,1)
            act.wait_ge(s_y1,3)
            nc.scalar.activation(gate[:,:,:],gate[:,:,:],ACT.Exp).then_inc(s_y2,1)
            with act.Fori(0,NODES//1024) as it2:
                for q in range(2):
                    it=it2*2+q
                    for ef in range(8):
                        act.wait_ge(s_f,it*8+ef+1)
                        if ef==0: act.wait_ge(s_y,it*4)
                        nc.scalar.activation(hT[:,ef//2,ef%2,:],bank[ef%2][:,:,:].rearrange("p a b -> p (a b)"),ACT.Gelu,bias=b1[:,ef//2,ef%2:ef%2+1]).then_inc(s_fe,1)
                    act.wait_ge(s_o,it+1)
                    act.wait_ge(s_out[q],it2*16)
                    nc.scalar.activation(oT[:,q,:],bank[4][:,:,:].rearrange("p a b -> p (a b)"),ACT.Identity).then_inc(s_oe,1)
                    act.wait_ge(s_oe,it+2)
                    act.dma_start(O['out'].rearrange("b c h w -> c b (h w)")[:,ds(it2,1),q*512:(q+1)*512].rearrange("c b n -> c (b n)"),oT[:,q,:]).then_inc(s_out[q],16)
            for q in range(2): act.wait_ge(s_out[q],16*(NODES//1024))
        @block.vector
        def _(dve):
            ch=Chain(dve,s_ch)
            dve.sem_inc(s_he,2); dve.sem_inc(s_used,2); dve.sem_inc(s_ye,2)
            ch.mark(nc.vector.tensor_copy(sti[:,:],start_f[:,:])); ch.mark(nc.vector.tensor_copy(eni[:,:],end_f[:,:]))
            lc=Chain(dve,s_l,17)
            dve.wait_ge(s_w,16*13)
            with dve.Fori(0,B) as b:
                lc.body(b)
                for m in range(NT):
                    lc.mark(nc.vector.bn_stats(st[:,m,:],t_all[:,ds(b*NT+m,1),:].rearrange("p a c -> p (a c)")))
                lc.sync(); dve.sem_inc(s_go,1)
                for m in range(NT): lc.mark(nc.vector.bn_aggr(mv[:,m,:],st[:,m,:]))
                lc.sync()
                nc.vector.tensor_scalar_add(rs[:,:],mv[:,:,1],1e-5).then_inc(s_var,1)
                dve.wait_ge(s_sd,b+1)
                lc(nc.vector.reciprocal(rs[:,:],rs[:,:]))
                def take_h(m):
                    g=b*NT+m
                    dve.wait_ge(s_h,g+3)
                    nc.vector.tensor_copy(h_all[:,ds(g,1),:].rearrange("p a k -> p (a k)"),bank[2+m%2][:,0,0:HF]).then_inc(s_he,1)
                for m in range(NT):
                    dve.wait_ge(s_tt,b*NT+m+1)
                    nc.vector.tensor_scalar(tn[:,m%2,:],t_all[:,ds(b*NT+m,1),:].rearrange("p a c -> p (a c)"),mv[:,m,0:1],rs[:,m:m+1],ALU.subtract,ALU.mult).then_inc(s_tn,1)
                    if m>=1: take_h(m-1)
                take_h(NT-1)
                lc.end()
            dve.wait_ge(s_he,HI+2)
            for i in range(2):
                ch(nc.vector.tensor_tensor(pm[:,:,:],h_all[:,:,:],att[:,i:i+1,:].to_broadcast([P,HI,HF]),ALU.mult))
                dst=(pay[:,:,0:4],seg_row[:,:,1:5])[i]
                ch(nc.vector.tensor_reduce(dst,pm[:,:,:].rearrange("p n (h k) -> p n h k",h=4),axis=AX.X,op=ALU.add))
            nc.vector.tensor_copy(pay[:,:,4:PAY],h_all[:,:,:]).then_inc(s_pay,1)
            nc.vector.memset(seg_row[:,:,0:1],1.0).then_inc(s_segr,1)
            ch.mark(nc.vector.memset(adc[:,:],0.0)); ch.mark(nc.vector.memset(anys[:,:],0.0))
            ch.mark(nc.vector.memset(res[:,1,CHK,:],0.0)); ch.sync()
            ch(nc.vector.memset(res[:,1,CHK,0:4],NEG))
            sc_=Chain(dve,s_c,2*SCK)
            with dve.Fori(0,NCH//2) as it:
                sc_.body(it)
                for q in range(2):
                    c=it*2+q
                    Dq=D[:,q]; Gq=G[:,q]; R=res[:,q]; Rp=res[:,1-q]
                    dve.wait_ge(s_D[q],it*16+16)
                    f=Dq[:,:,0]
                    sc_.mark(nc.vector.tensor_scalar(ns[:,:],f,-1.0,1.0,ALU.mult,ALU.add))
                    sc_.mark(nc.vector.tensor_scalar(ng[:,:],f,NEG,None,ALU.mult))
                    sc_(nc.vector.reduce_max(anys[:,1:2],f,AX.X))
                    sc_.mark(nc.vector.tensor_tensor(anys[:,0:1],anys[:,0:1],anys[:,1:2],ALU.max))
                    for h in range(4):
                        sc_.mark(nc.vector.tensor_tensor_scan(out=ad[:,h,:],data0=ns[:,:],data1=Dq[:,:,1+h],initial=adc[:,h:h+1],op0=ALU.mult,op1=ALU.add))
                    sc_.sync()
                    sc_.mark(nc.vector.tensor_copy(adc[:,:],ad[:,:,CHK-1]))
                    dve.wait_ge(s_rd[q],it*16)
                    sc_.mark(nc.vector.tensor_copy(R[:,0,:],Rp[:,CHK,:]))
                    dve.wait_ge(s_G[q],it*16*CHK+16*CHK)
                    sc_(nc.vector.tensor_tensor(e[:,:,:],Gq[:,:,0:4].rearrange("p j h -> p h j"),ad[:,:,:],ALU.add))
                    sc_(nc.vector.scalar_tensor_tensor(e[:,:,:],e[:,:,:],0.2,e[:,:,:],ALU.mult,ALU.max))
                    for h in range(4):
                        sc_.mark(nc.vector.tensor_tensor_scan(out=R[:,1:CHK+1,h],data0=ng[:,:],data1=e[:,h,:],initial=R[:,0:1,h],op0=ALU.add,op1=ALU.max))
                    sc_.sync()
                    Rh=R.rearrange("p j c -> p c j")
                    sc_.mark(nc.vector.tensor_tensor(ex[:,0],Rh[:,0:4,0:CHK],ng[:,:].unsqueeze(1).to_broadcast([P,4,CHK]),ALU.add))
                    sc_.mark(nc.vector.tensor_tensor(ex[:,1],e[:,:,:],Rh[:,0:4,1:CHK+1],ALU.subtract))
                    sc_.sync()
                    nc.vector.tensor_tensor(ex[:,0],ex[:,0],Rh[:,0:4,1:CHK+1],ALU.subtract).then_inc(s_e,1)
                    dve.wait_ge(s_ex,c+1)
                    sc_(nc.vector.tensor_tensor(nm[:,:,:].rearrange("p (h k) j -> p h k j",h=4),ex[:,1].unsqueeze(2).to_broadcast([P,4,4,CHK]),
                        Gq[:,:,4:PAY].rearrange("p j (h k) -> p h k j",h=4),ALU.mult))
                    for h in range(4):
                        sc_.mark(nc.vector.tensor_tensor_scan(out=R[:,1:CHK+1,4+h],data0=ex[:,0,h,:],data1=ex[:,1,h,:],initial=R[:,0:1,4+h],op0=ALU.mult,op1=ALU.add))
                    for k in range(HF):
                        sc_.mark(nc.vector.tensor_tensor_scan(out=R[:,1:CHK+1,8+k],data0=ex[:,0,k//4,:],data1=nm[:,k,:],initial=R[:,0:1,8+k],op0=ALU.mult,op1=ALU.add))
                    sc_.sync()
                    dve.sem_inc(s_used,1)
                    dve.sem_inc(s_r,1)
                sc_.end()
            last=res[:,1,CHK,:]
            ch.mark(nc.vector.tensor_copy(ms[:,0,0:4],last[:,0:4]))
            ch.mark(nc.vector.tensor_copy(ms[:,0,4:PAY].rearrange("p (h k) -> p h k",h=4),last[:,0:4].unsqueeze(2).to_broadcast([P,4,4])))
            ch.mark(nc.vector.tensor_copy(ms[:,1,:],last[:,4:RES]))
            ch.mark(nc.vector.tensor_copy(ms[:,2,:],anys[:,0:1].to_broadcast([P,PAY])))
            ch.sync()
            dve.sem_inc(s_x,1)
            dve.wait_ge(s_xt,1)
            for i in range(3): ch.mark(nc.vector.tensor_copy(mT[:,i,:],bank[4+i][0:PAY,0,:]))
            ch.mark(nc.vector.memset(cm[:,0,0:1],NEG)); ch.mark(nc.vector.memset(cm[:,1,0:1],0.0)); ch.sync()
            ch(nc.vector.tensor_scalar(mT[:,2,:],mT[:,2,:],NEG,None,ALU.mult))
            ch(nc.vector.tensor_tensor_scan(out=cm[:,0,1:P+1],data0=mT[:,2,:],data1=mT[:,0,:],initial=cm[:,0,0:1],op0=ALU.add,op1=ALU.max))
            ch.mark(nc.vector.tensor_tensor(xt[:,0,:],cm[:,0,0:P],mT[:,2,:],ALU.add))
            ch.mark(nc.vector.tensor_tensor(xt[:,1,:],mT[:,0,:],cm[:,0,1:P+1],ALU.subtract)); ch.sync()
            nc.vector.tensor_tensor(xt[:,0,:],xt[:,0,:],cm[:,0,1:P+1],ALU.subtract).then_inc(s_x1,1)
            dve.wait_ge(s_x2,1)
            ch(nc.vector.tensor_tensor(mT[:,1,:],mT[:,1,:],xt[:,1,:],ALU.mult))
            nc.vector.tensor_tensor_scan(out=cm[:,1,1:P+1],data0=xt[:,0,:],data1=mT[:,1,:],initial=cm[:,1,0:1],op0=ALU.mult,op1=ALU.add).then_inc(s_cr,1)
            dve.wait_ge(s_crT,1)
            ch.mark(nc.vector.tensor_copy(carry[:,0:PAY],bank[0][:,0,0:PAY]))
            nc.vector.tensor_copy(carry[:,PAY:2*PAY],bank[1][:,0,0:PAY]).then_inc(s_ci,1)
            qf,back,t1,need=(q4[:,i,:] for i in range(4))
            ch(nc.vector.tensor_scalar(qf,end_f[:,:],1.0/PCOLS,None,ALU.mult))
            ch(nc.vector.tensor_copy(qi[:,:],qf))
            ch(nc.vector.tensor_copy(qf,qi[:,:]))
            ch(nc.vector.scalar_tensor_tensor(back,qf,float(-PCOLS),end_f[:,:],ALU.mult,ALU.add))
            ch(nc.vector.tensor_scalar(t1,back,0.0,None,ALU.is_lt))
            ch(nc.vector.tensor_tensor(qf,qf,t1,ALU.subtract))
            ch(nc.vector.tensor_scalar(t1,back,float(PCOLS),None,ALU.is_ge))
            ch(nc.vector.tensor_tensor(qf,qf,t1,ALU.add))
            ch(nc.vector.scalar_tensor_tensor(back,qf,float(PCOLS),start_f[:,:],ALU.mult,ALU.subtract))
            ch(nc.vector.tensor_scalar(need,back,0.0,None,ALU.is_gt))
            ch(nc.vector.tensor_scalar(need,need,-1.0,-NEG,ALU.add,ALU.mult))
            nc.vector.tensor_copy(qi[:,:],qf).then_inc(s_en,1)
            dve.wait_ge(s_gr,32*HI)
            ch(nc.vector.tensor_tensor(tmp[:,:,0:4],rcar[:,:,0:4],need.unsqueeze(2).to_broadcast([P,HI,4]),ALU.add))
            ch(nc.vector.tensor_tensor(mm[:,:,:],tmp[:,:,0:4],rloc[:,:,0:4],ALU.max))
            ch.mark(nc.vector.tensor_tensor(abx[:,:,0:4],rloc[:,:,0:4],mm[:,:,:],ALU.subtract))
            ch(nc.vector.tensor_tensor(abx[:,:,4:8],tmp[:,:,0:4],mm[:,:,:],ALU.subtract))
            dve.sem_inc(s_y1,1); dve.wait_ge(s_y2,1)
            for o,src,dst in ((0,rloc[:,:,4:RES],num),(4,rcar[:,:,PAY:2*PAY],tmp)):
                ch.mark(nc.vector.tensor_tensor(dst[:,:,0:4],src[:,:,0:4],abx[:,:,o:o+4],ALU.mult))
                for h in range(4):
                    ch.mark(nc.vector.tensor_tensor(dst[:,:,4+4*h:8+4*h],src[:,:,4+4*h:8+4*h],abx[:,:,o+h:o+h+1].to_broadcast([P,HI,4]),ALU.mult))
            ch.sync()
            ch(nc.vector.tensor_tensor(num[:,:,:],num[:,:,:],tmp[:,:,:],ALU.add))
            ch(nc.vector.tensor_scalar_add(num[:,:,0:4],num[:,:,0:4],1e-16))
            ch(nc.vector.reciprocal(mm[:,:,:],num[:,:,0:4]))
            agg=tmp[:,:,0:HF]
            for h in range(4): ch.mark(nc.vector.tensor_tensor(tmp[:,:,4*h:4*h+4],num[:,:,4+4*h:8+4*h],mm[:,:,h:h+1].to_broadcast([P,HI,4]),ALU.mult))
            ch.sync()
            row=lambda i: cst[:,i:i+1,:].to_broadcast([P,HI,HF])
            ch(nc.vector.tensor_tensor(agg,agg,row(0),ALU.add))
            ch(nc.vector.tensor_reduce(mu[:,:],agg,axis=AX.X,op=ALU.add))
            ch(nc.vector.tensor_scalar(mu[:,:],mu[:,:],1.0/HF,None,ALU.mult))
            ch(nc.vector.tensor_tensor(agg,agg,mu[:,:].unsqueeze(2).to_broadcast([P,HI,HF]),ALU.subtract))
            ch(nc.vector.tensor_tensor(pm[:,:,:],agg,agg,ALU.mult))
            ch(nc.vector.tensor_reduce(vv[:,:],pm[:,:,:],axis=AX.X,op=ALU.add))
            ch(nc.vector.tensor_scalar(vv[:,:],vv[:,:],1.0/HF,1e-5,ALU.mult,ALU.add))
            dve.sem_inc(s_y1,1); dve.wait_ge(s_y2,2)
            ch(nc.vector.reciprocal(vv[:,:],vv[:,:]))
            ch(nc.vector.tensor_tensor(agg,agg,vv[:,:].unsqueeze(2).to_broadcast([P,HI,HF]),ALU.mult))
            ch(nc.vector.tensor_tensor(agg,agg,row(1),ALU.mult))
            ch(nc.vector.tensor_tensor(agg,agg,row(2),ALU.add))
            ch(nc.vector.tensor_reduce(sc[:,:,:],agg.rearrange("p n (h e) -> p n e h",h=4),axis=AX.X,op=ALU.add))
            ch(nc.vector.tensor_scalar(sc[:,:,:],sc[:,:,:],0.25,None,ALU.mult))
            ch(nc.vector.memset(rk[:,:,:],0.0))
            for i in range(EXP):
                for j in range(i+1,EXP):
                    ch(nc.vector.tensor_tensor(cc[:,:],sc[:,:,j],sc[:,:,i],ALU.is_gt))
                    ch.mark(nc.vector.tensor_tensor(rk[:,:,i],rk[:,:,i],cc[:,:],ALU.add))
                    ch(nc.vector.scalar_tensor_tensor(rk[:,:,j],rk[:,:,j],1.0,cc[:,:],ALU.add,ALU.subtract))
            ch(nc.vector.tensor_reduce(cc[:,:],sc[:,:,:],axis=AX.X,op=ALU.max))
            ch(nc.vector.tensor_tensor(gate[:,:,:],sc[:,:,:],cc[:,:].unsqueeze(2).to_broadcast([P,HI,EXP]),ALU.subtract))
            ch(nc.vector.tensor_scalar(rk[:,:,:],rk[:,:,:],2.0,None,ALU.is_lt))
            dve.sem_inc(s_y1,1); dve.wait_ge(s_y2,3)
            ch(nc.vector.tensor_tensor(gate[:,:,:],gate[:,:,:],rk[:,:,:],ALU.mult))
            ch(nc.vector.tensor_reduce(cc[:,:],gate[:,:,:],axis=AX.X,op=ALU.add))
            ch(nc.vector.reciprocal(cc[:,:],cc[:,:]))
            ch(nc.vector.tensor_tensor(gate[:,:,:],gate[:,:,:],cc[:,:].unsqueeze(2).to_broadcast([P,HI,EXP]),ALU.mult))
            dve.sem_inc(s_gate,1)
            fc=Chain(dve,s_fc,4*4)
            with dve.Fori(0,NODES//512) as it:
                fc.body(it)
                for m in range(4):
                    g=it*4+m
                    dve.wait_ge(s_y,g+1)
                    if m==0: dve.wait_ge(s_oe,it+1)
                    fc(nc.vector.tensor_tensor(y[:,m%2,:],bank[2+m%2][:,:,:].rearrange("p a b -> p (a b)"),b2[:,:],ALU.add))
                    fc(nc.vector.scalar_tensor_tensor(acc4[:,m,:],y[:,m%2,0:P],gate[:,ds(g,1),0:1].rearrange("p a b -> p (a b)"),t_all[:,ds(g,1),:].rearrange("p a c -> p (a c)"),ALU.mult,ALU.add))
                    for ee in range(1,EXP):
                        ins=nc.vector.scalar_tensor_tensor(acc4[:,m,:],y[:,m%2,ee*P:(ee+1)*P],gate[:,ds(g,1),ee:ee+1].rearrange("p a b -> p (a b)"),acc4[:,m,:],ALU.mult,ALU.add)
                        if ee<EXP-1: fc(ins)
                        else: ins.then_inc(s_ye,1)
                fc.end()

SCK=39
LKM=17; HKM=40

def program(nc, A, O):
    with ExitStack() as ctx:
        keep = lambda n, s, d: ctx.enter_context(nc.sbuf_tensor(n, s, d))
        dram = lambda n, s, d: nc.dram_tensor(n, s, d, kind="Internal").ap()
        srclist = dram("sorted_sources", [NPOS, 1], i32)
        seg = dram("segment_starts", [NPOS, 5], f32)
        pay_d = dram("node_payload", [NODES, PAY], f32)
        res_d = dram("running_softmax", [NPOS, RES], f32)
        car_d = dram("carried", [P, 2 * PAY], f32)
        table = dram("patches", [B * DG * TROWS, P], f32)
        ident = keep("ident", [P, P], f32)
        start_f = keep("start_f", [P, HI], f32)
        end_f = keep("end_f", [P, HI], f32)
        t_all = keep("t_all", [P, B * NT, C], f32)
        rank_phase(nc, A, srclist, seg, start_f, end_f, ident)
        with ExitStack() as images:
            hold = lambda n, s, d: images.enter_context(nc.sbuf_tensor(n, s, d))
            x_all = hold("x_all", [P, B, HW], f32)
            idx_all = hold("idx_all", [P, (B * NT + 1) * 36], u32)
            w4_all = hold("w4_all", [P, B * 1152], f32)
            wdT = hold("wdT", [P, TAPS, P], f32)
            conv_phase(nc, A, table, x_all, idx_all, w4_all, wdT, ident)
            mix_phase(nc, A, table, x_all, t_all, idx_all, w4_all, wdT, ident)
        gat_phase(nc, A, O, t_all, start_f, end_f, srclist, seg, pay_d, res_d, car_d, ident)


def kernel(**inputs):
    import numpy as np
    import concourse.bacc as bacc
    from concourse.bass_utils import run_bass_kernel_spmd

    nc = bacc.Bacc("TRN2", target_bir_lowering=False, num_devices=1)
    arrays = {name: np.ascontiguousarray(a) for name, a in inputs.items()}
    A = {name: nc.dram_tensor(name, a.shape, mybir.dt.from_np(a.dtype), kind="ExternalInput").ap()
         for name, a in arrays.items()}
    O = {"out": nc.dram_tensor("out", (B, C, WID, WID), f32, kind="ExternalOutput").ap()}
    program(nc, A, O)
    result = run_bass_kernel_spmd(nc, [arrays], core_ids=[0])
    return result.results[0]["out"]
```

```python
import concourse.bass as bass
from concourse import mybir
from contextlib import ExitStack

ds = bass.ds
f32 = mybir.dt.float32
bf16 = mybir.dt.bfloat16
i32 = mybir.dt.int32
u32 = mybir.dt.uint32
ALU = mybir.AluOpType
ACT = mybir.ActivationFunctionType
AX = mybir.AxisListType

P = 128
B, C, WID = 8, 128, 32
HW = WID * WID
NT = HW // P
DG, TAPS = 4, 9
CG = C // DG
NOFF = 2 * DG * TAPS
PITCH = WID + 2
PADN = 1280
BASE = 2 * PITCH + 2
CORNER = (0, 1, PITCH, PITCH + 1)
FRONT = 40
TROWS = PADN + FRONT
HEADS = 8
NODES = B * HW
HI = NODES // P
M = NODES
E = 524288
EXP, HF, PAY, RES = 4, 16, 20, 24
NPOS = 66 * 8192
PCOLS = NPOS // P
ROW = 64
ROWBITS = 6
NCH = NPOS // (P * ROW)
NGRP = NODES // 512
NEG = -1e30
E_UNIT, E_CH = 8, 32
E_NU = E_CH // E_UNIT
C_CH, C_GK = 27, 8
C_NCH = -(-E // P // C_CH)
C_GRP = C_NCH // C_GK
C_GC = C_CH * C_GK
C_COLS = C_NCH * C_CH
C_HALVES = C_NCH * E_UNIT // E_CH // 2
C_POOL = 21

class Chain:
    def __init__(self,eng,sem,per=0): self.eng,self.sem,self.per,self.n,self.base=eng,sem,per,0,0
    def body(self,i): self.base=i*self.per; self.n=0
    def end(self): assert self.n==self.per,(self.n,self.per)
    def mark(self,ins): self.n+=1; return ins.then_inc(self.sem,1)
    def sync(self): self.eng.wait_ge(self.sem,self.base+self.n)
    def __call__(self,ins): self.mark(ins); self.sync()

def conv_phase(nc,A,table,x_all,idx_all,w4_all,wdT,ident,dbg=None):
    with ExitStack() as ctx:
        sb=lambda n,s,d: ctx.enter_context(nc.sbuf_tensor(n,s,d))
        pb=lambda n,s,d: ctx.enter_context(nc.psum_tensor(n,s,d))
        sem=lambda n: ctx.enter_context(nc.semaphore("c_"+n))
        w1n=sb("w1n",[P,C*TAPS],f32); w2n=sb("w2n",[NOFF,C*TAPS],f32); wdn=sb("wdn",[P,C*TAPS],f32)
        w1T=sb("w1T",[P,TAPS,P],f32); w2T=sb("w2T",[P,TAPS,NOFF],f32)
        b1=sb("b1c",[P,1],f32); b2=sb("b2c",[P,NOFF],f32)
        gavg=sb("gavg",[P,P],f32)
        bst=sb("bst",[P,B,2,6],f32); mv=sb("mv",[P,B,2],f32)
        mean=sb("mean",[P,B],f32); rstd=sb("rstd",[P,B],f32); dev=sb("dev",[P,B],f32)
        xpad=sb("xpad",[P,2,PADN],f32); hpad=sb("hpad",[P,2,PADN],f32)
        off=sb("off",[NOFF,2,512],f32)
        Fs=sb("Fs",[P,2,10,P],f32)
        pxi=sb("pxi",[P,NT],i32); pyx=sb("pyx",[P,NT,2],f32); yi=sb("yi",[P,NT],i32); xi=sb("xi",[P,NT],i32)
        kyx=sb("kyx",[P,DG*TAPS,2],f32); kyi=sb("kyi",[P,TAPS],i32); kxi=sb("kxi",[P,TAPS],i32)
        gbase=sb("gbase",[P,DG],i32); gbf=sb("gbf",[P,DG],f32)
        basec=sb("basec",[P,NT,NOFF],f32)
        pos=sb("posyx",[P,NT,NOFF],f32); fli=sb("fli",[P,NT,NOFF],i32); fl=sb("fl",[P,NT,NOFF],f32); gt=sb("gt",[P,NT,NOFF],f32)
        whi=sb("whi",[P,NT,NOFF],f32); wlo=sb("wlo",[P,NT,NOFF],f32)
        ixf=sb("ixf",[P,NT,DG*TAPS],f32)
        tp=[pb(f"tp{i}",[P,4,P],f32) for i in range(3)]
        st_ps=pb("st_ps",[P,B],f32)
        c1=[pb(f"c1_{i}",[P,512],f32) for i in range(2)]
        c2=[pb(f"c2_{i}",[P,4,NOFF],f32) for i in range(2)]
        s_const=sem("const"); s_x=sem("x"); s_w=sem("w"); s_b=sem("b"); s_wt=sem("wt"); s_wt_ev=sem("wt_ev")
        s_mean=sem("mean_in"); s_gm=sem("group_mean"); s_var=sem("var_in"); s_gv=sem("group_var"); s_sq=sem("sqrt")
        s_pad=sem("padded"); s_zero=sem("zeroed"); s_c1=sem("conv1_done"); s_h=sem("hidden_ready"); s_c2=sem("conv2_done")
        ztile=sb("ztile",[P,FRONT*DG],f32); s_edge=sem("table_edges")
        s_off=sem("offsets_out"); s_ot=sem("offsets_transposed")
        s_c2r=sem("conv2_read"); s_F=sem("pixels_transposed"); s_Fe=sem("pixels_ready"); s_T=[sem(f"table_written{i}") for i in range(2)]
        s_ch=sem("dve_chain"); s_lp=sem("dve_loop_chain"); s_xfree=sem("xpad_free"); s_base=sem("base_ready"); s_pc=sem("pool_chain")
        T5=table.rearrange("(b rg) (j c) -> b rg j c",b=B,j=4)
        block=ctx.enter_context(nc.Block())
        @block.sync
        def _(sp):
            for b in range(B):
                sp.dma_start(x_all[:,b,:],A['x'][b].rearrange("c h w -> c (h w)")).then_inc(s_x,16)
            sp.dma_start(w1n[:,:],A['L0_conv_w1'].rearrange("o c a b -> o (c a b)")).then_inc(s_w,16)
            sp.dma_start(w2n[:,:],A['L0_conv_w2'].rearrange("o c a b -> o (c a b)")).then_inc(s_w,16)
            sp.dma_start(wdn[:,:],A['L0_conv_wd'].rearrange("o c a b -> o (c a b)")).then_inc(s_w,16)
            sp.dma_start(b1[:,:],A['L0_conv_b1'].rearrange("(p a) -> p a",a=1)).then_inc(s_b,16)
            sp.dma_start(b2[:,:],A['L0_conv_b2'].rearrange("(a n) -> a n",a=1).to_broadcast([P,NOFF])).then_inc(s_b,16)
            sp.wait_ge(s_zero,1)
            for b in range(B):
                for r0 in (0,PADN):
                    sp.dma_start(table[(b*TROWS+r0)*DG:(b*TROWS+r0+FRONT)*DG,:].rearrange("r c -> (r c)").rearrange("(p n) -> p n",p=P),ztile[:,:]).then_inc(s_edge,16)
            sp.wait_ge(s_edge,16*2*B)
            with sp.Fori(0,B//2) as it:
                for q in range(2):
                    b=it*2+q
                    sp.wait_ge(s_Fe,3*b+6)
                    for j in range(4):
                        o=FRONT-CORNER[j]
                        sp.dma_start(T5[ds(b,1),o*DG:(o+PADN)*DG,j,:].rearrange("b (p rg) c -> (b p) rg c",p=P),
                                     Fs[:,q].rearrange("p r (g c) -> p (r g) c",g=DG)).then_inc(s_T[q],16)
            for q in range(2): sp.wait_ge(s_T[q],16*4*B//2)
        @block.gpsimd
        def _(pool):
            pc=Chain(pool,s_pc)
            pc.mark(nc.gpsimd.memset(ident[:,:],0.0)); pc.mark(nc.gpsimd.memset(gavg[:,:],0.25))
            pc(nc.gpsimd.iota(pxi[:,:],pattern=[[P,NT]],base=0,channel_multiplier=1))
            nc.gpsimd.iota(kyi[:,:],pattern=[[1,3],[0,3]],base=-1,channel_multiplier=0)
            nc.gpsimd.iota(kxi[:,:],pattern=[[0,3],[1,3]],base=-1,channel_multiplier=0)
            nc.gpsimd.iota(gbase[:,:],pattern=[[1,DG]],base=DG*(BASE+FRONT),channel_multiplier=0).then_inc(s_const,1)
            nc.gpsimd.affine_select(out=ident[:,:],in_=ident[:,:],compare_op=ALU.not_equal,fill=1.0,base=0,pattern=[[-1,P]],channel_multiplier=1)
            pc(nc.gpsimd.affine_select(out=gavg[:,:],in_=gavg[:,:],compare_op=ALU.is_ge,fill=0.0,base=0,pattern=[[-4,32],[0,4]],channel_multiplier=1))
            nc.gpsimd.affine_select(out=gavg[:,:],in_=gavg[:,:],compare_op=ALU.is_ge,fill=0.0,base=3,pattern=[[4,32],[0,4]],channel_multiplier=-1).then_inc(s_const,1)
        def trs():
            for t in range(TAPS): yield w1n[:,t::TAPS],w1T[:,t,:],P
            for t in range(TAPS): yield w2n[:,t::TAPS],w2T[:,t,:],NOFF
            for t in range(TAPS): yield wdn[:,t::TAPS],wdT[:,t,:],P
        @block.tensor
        def _(pe):
            pe.wait_ge(s_const,2); pe.wait_ge(s_w,48)
            for n,(src,dst,m) in enumerate(trs()):
                if n>=3: pe.wait_ge(s_wt_ev,n-2)
                nc.tensor.transpose(tp[n%3][:,0,0:m],src,ident[0:m,0:m]).then_inc(s_wt,1)
            pe.wait_ge(s_mean,1)
            nc.tensor.matmul(st_ps[:,:],gavg[:,:],mean[:,:],start=True,stop=True).then_inc(s_gm,1)
            pe.wait_ge(s_var,1)
            nc.tensor.matmul(st_ps[:,:],gavg[:,:],dev[:,:],start=True,stop=True).then_inc(s_gv,1)
            pe.wait_ge(s_wt_ev,27)
            pe.sem_inc(s_c1,4); pe.sem_inc(s_F,6); pe.sem_inc(s_c2,4); pe.sem_inc(s_ot,2)
            with pe.Fori(0,B//2) as it:
                for q in range(2):
                    b=it*2+q
                    pe.wait_ge(s_pad,b+1)
                    xv=xpad[:,q]
                    for r in range(3):
                        nt=min(4,10-4*r)
                        pe.wait_ge(s_Fe,3*b+r)
                        for k in range(nt):
                            last=nc.tensor.transpose(tp[r][:,k,:],xv[:,4*r+k::PADN//P],ident[:,:])
                        last.then_inc(s_F,1)
                    for h in range(2):
                        pe.wait_ge(s_off,b*2+h+1)
                        for t in range(TAPS):
                            o=BASE+(16*h+t//3-1)*PITCH+t%3-1
                            last=nc.tensor.matmul(c1[h][:,:],w1T[:,t,:],xv[:,o:o+16*PITCH].rearrange("p (r w) -> p r w",w=PITCH)[:,:,0:WID],start=(t==0),stop=(t==TAPS-1))
                        last.then_inc(s_c1,1)
                    hv=hpad[:,q]
                    pe.wait_ge(s_h,b*2+4)
                    for h in range(2):
                        pe.wait_ge(s_off,b*2+h+1)
                        for t in range(TAPS):
                            o=BASE+(16*h+t//3-1)*PITCH+t%3-1
                            last=nc.tensor.matmul(c1[h][0:NOFF,:],w2T[:,t,:],hv[:,o:o+16*PITCH].rearrange("p (r w) -> p r w",w=PITCH)[:,:,0:WID],start=(t==0),stop=(t==TAPS-1))
                        last.then_inc(s_c2,1)
                    for m in range(NT):
                        if m%4==0:
                            pe.wait_ge(s_off,b*2+m//4+3)
                            pe.wait_ge(s_c2r,b*2+m//4+1)
                        last=nc.tensor.transpose(c2[m//4][:,m%4,:],off[0:NOFF,m//4,(m%4)*P:(m%4+1)*P],ident[0:NOFF,0:NOFF])
                        if m%4==3: last.then_inc(s_ot,1)
        @block.scalar
        def _(act):
            for n,(src,dst,m) in enumerate(trs()):
                act.wait_ge(s_wt,n+1)
                nc.scalar.copy(dst,tp[n%3][:,0,0:m]).then_inc(s_wt_ev,1)
            act.wait_ge(s_var,2)
            nc.scalar.activation(rstd[:,:],rstd[:,:],ACT.Sqrt).then_inc(s_sq,1)
            act.sem_inc(s_Fe,3); act.sem_inc(s_h,2); act.sem_inc(s_off,2)
            act.wait_ge(s_b,32); act.wait_ge(s_zero,1)
            with act.Fori(0,B//2) as it:
                for q in range(2):
                    b=it*2+q
                    act.wait_ge(s_T[q],it*64)
                    for r in range(3):
                        nt=min(4,10-4*r)
                        act.wait_ge(s_F,b*3+r+7)
                        nc.scalar.activation(Fs[:,q,4*r:4*r+nt,:],tp[r][:,0:nt,:],ACT.Identity).then_inc(s_Fe,1)
                    for h in range(2):
                        act.wait_ge(s_c1,b*2+h+5)
                        act.wait_ge(s_c2,b*2+1)
                        o=BASE+16*h*PITCH
                        nc.scalar.activation(hpad[:,q,o:o+16*PITCH].rearrange("p (r w) -> p r w",w=PITCH)[:,:,0:WID],
                            c1[h][:,:].rearrange("p (r w) -> p r w",w=WID),ACT.Identity,bias=b1[:,0:1]).then_inc(s_h,1)
                    for h in range(2):
                        act.wait_ge(s_c2,b*2+h+5)
                        act.wait_ge(s_ot,b*2+h+1)
                        nc.scalar.activation(off[:,h,:],c1[h][0:NOFF,:],ACT.Identity).then_inc(s_off,1)
        @block.vector
        def _(dve):
            ch=Chain(dve,s_ch)
            nc.vector.memset(xpad[:,:,:],0.0)
            ch.mark(nc.vector.memset(ztile[:,:],0.0))
            ch(nc.vector.memset(hpad[:,:,:],0.0))
            dve.sem_inc(s_zero,1)
            ch.mark(nc.vector.memset(idx_all[:,B*NT*36:],0))
            dve.wait_ge(s_const,2)
            nc.vector.tensor_single_scalar(yi[:,:],pxi[:,:],5,op=ALU.logical_shift_right)
            ch(nc.vector.tensor_single_scalar(xi[:,:],pxi[:,:],31,op=ALU.bitwise_and))
            nc.vector.tensor_copy(pyx[:,:,0],yi[:,:])
            nc.vector.tensor_copy(pyx[:,:,1],xi[:,:])
            nc.vector.tensor_copy(gbf[:,:],gbase[:,:])
            kv=kyx[:,:,:].rearrange("p (g k) two -> p g k two",g=DG)
            nc.vector.tensor_copy(kv[:,:,:,0],kyi[:,:].unsqueeze(1).to_broadcast([P,DG,TAPS]))
            ch(nc.vector.tensor_copy(kv[:,:,:,1],kxi[:,:].unsqueeze(1).to_broadcast([P,DG,TAPS])))
            bv=basec[:,:,:].rearrange("p m (k two) -> p m k two",two=2)
            ch(nc.vector.tensor_tensor(bv,pyx[:,:,:].unsqueeze(2).to_broadcast([P,NT,DG*TAPS,2]),kyx[:,:,:].unsqueeze(1).to_broadcast([P,NT,DG*TAPS,2]),ALU.add))
            dve.wait_ge(s_b,32)
            ch(nc.vector.tensor_tensor(basec[:,:,:],basec[:,:,:],b2[:,:].unsqueeze(1).to_broadcast([P,NT,NOFF]),ALU.add))
            dve.wait_ge(s_x,16*B)
            for b in range(B):
                for h in range(2):
                    last=nc.vector.bn_stats(bst[:,b,h,:],x_all[:,b,h*512:(h+1)*512])
            ch(last)
            for b in range(B): last=nc.vector.bn_aggr(mv[:,b,:],bst[:,b,:,:])
            ch(last)
            nc.vector.tensor_copy(mean[:,:],mv[:,:,0]).then_inc(s_mean,1)
            dve.wait_ge(s_gm,1)
            dve.wait_ge(s_mean,1)
            ch(nc.vector.tensor_copy(mean[:,:],st_ps[:,:]))
            ch(nc.vector.tensor_sub(dev[:,:],mv[:,:,0],mean[:,:]))
            ch(nc.vector.tensor_mul(dev[:,:],dev[:,:],dev[:,:]))
            nc.vector.tensor_add(dev[:,:],dev[:,:],mv[:,:,1]).then_inc(s_var,1)
            dve.wait_ge(s_gv,1)
            nc.vector.tensor_scalar_add(rstd[:,:],st_ps[:,:],1e-5).then_inc(s_var,1)
            dve.wait_ge(s_sq,1)
            ch(nc.vector.reciprocal(rstd[:,:],rstd[:,:]))
            dve.sem_inc(s_c2r,2)
            lc=Chain(dve,s_lp,2*LK)
            with dve.Fori(0,B//2) as it:
                lc.body(it)
                for q in range(2):
                    b=it*2+q
                    def normalize(b,q):
                        nc.vector.tensor_scalar(xpad[:,q,BASE:BASE+WID*PITCH].rearrange("p (r w) -> p r w",w=PITCH)[:,:,0:WID],
                            x_all[:,ds(b,1),:].rearrange("p a (r w) -> p (a r) w",w=WID),mean[:,ds(b,1)],rstd[:,ds(b,1)],ALU.subtract,ALU.mult).then_inc(s_pad,1)
                    normalize(b,q)
                    for m in range(2):
                        dve.wait_ge(s_ot,b*2+m+3)
                        ins=nc.vector.tensor_tensor(pos[:,4*m:4*m+4,:],c2[m][:,:,:],basec[:,4*m:4*m+4,:],ALU.add)
                        lc.mark(ins)
                        if m==1: lc.sync()
                    dve.sem_inc(s_c2r,2)
                    lc(nc.vector.tensor_scalar(pos[:,:,:],pos[:,:,:],-3.0,34.0,ALU.max,ALU.min))
                    lc(nc.vector.tensor_copy(fli[:,:,:],pos[:,:,:]))
                    lc(nc.vector.tensor_copy(fl[:,:,:],fli[:,:,:]))
                    lc(nc.vector.tensor_tensor(gt[:,:,:],fl[:,:,:],pos[:,:,:],ALU.is_gt))
                    lc(nc.vector.tensor_tensor(fl[:,:,:],fl[:,:,:],gt[:,:,:],ALU.subtract))
                    lc(nc.vector.tensor_tensor(whi[:,:,:],pos[:,:,:],fl[:,:,:],ALU.subtract))
                    lc.mark(nc.vector.tensor_scalar(wlo[:,:,:],whi[:,:,:],-1.0,1.0,ALU.mult,ALU.add))
                    lc(nc.vector.tensor_scalar(fl[:,:,:],fl[:,:,:],-2.0,32.0,ALU.max,ALU.min))
                    fv=fl[:,:,:].rearrange("p m (k two) -> p m k two",two=2)
                    lc(nc.vector.scalar_tensor_tensor(ixf[:,:,:],fv[:,:,:,0],float(PITCH),fv[:,:,:,1],ALU.mult,ALU.add))
                    for g in range(DG):
                        lc.mark(nc.vector.tensor_scalar(idx_all[:,ds(b*288,288)].rearrange("p (m k g) -> p m k g",m=NT,k=TAPS)[:,:,:,g],
                            ixf[:,:,g*TAPS:(g+1)*TAPS],float(DG),gbf[:,g:g+1],ALU.mult,ALU.add))
                        for jy,jx in ((0,0),(0,1),(1,0),(1,1)):
                            wy=(wlo,whi)[jy][:,:,:].rearrange("p m (g k two) -> p m g k two",g=DG,two=2)[:,:,g,:,0]
                            wx=(wlo,whi)[jx][:,:,:].rearrange("p m (g k two) -> p m g k two",g=DG,two=2)[:,:,g,:,1]
                            lc.mark(nc.vector.tensor_tensor(w4_all[:,ds(b*1152,1152)].rearrange("p (m k c) -> p m k c",m=NT,k=TAPS)[:,:,:,4*g+2*jy+jx],wy,wx,ALU.mult))
                    lc.sync()
                    lc(nc.vector.tensor_scalar_add(gbf[:,:],gbf[:,:],float(DG*TROWS)))
                lc.end()
LK=32
def compact_phase(nc,A,srclist,seg,res_d,car_d,comp,lim,ident):
    edges=A['L1_ffn_edge_index']
    with ExitStack() as ctx:
        sb=lambda n,s,d: ctx.enter_context(nc.sbuf_tensor(n,s,d))
        pb=lambda n,s,d: ctx.enter_context(nc.psum_tensor(n,s,d))
        sem=lambda n: ctx.enter_context(nc.semaphore("k_"+n))
        io_i=sb("k_iota_i",[P,P],i32); io_b=sb("k_iota_b",[P,P],bf16); before=sb("k_before",[P,P],f32)
        before_b=sb("k_before_b",[P,P],bf16); ones_b=sb("k_ones",[P,P],bf16); zeros=sb("zeros",[P,PCOLS],i32)
        dst=sb("k_dst",[P,C_COLS],i32); src=sb("k_src",[P,C_COLS],i32)
        notfirst=sb("notfirst",[P,C_GC],f32)
        ti=sb("k_ti",[P,4,C_GC],i32); tf=sb("k_tf",[P,C_GC],f32); valid=sb("valid",[P,C_GC],bf16)
        V=sb("edge_values",[P,4,C_GC],bf16)
        incl=sb("k_incl",[P,C_GC],f32); si=sb("k_si",[P,3,C_GC],i32); slot_lo=sb("slot_lo",[P,C_GC],bf16); slot_hi=sb("slot_hi",[P,C_GC],bf16)
        vtot=sb("kept",[P,C_NCH],f32); vm=sb("most_kept",[P,1],f32); vmi=sb("most_kept_i",[P,2],i32)
        OS=sb("slot_onehot",[P,2,C_CH,P],bf16); KH=sb("slot_tile",[P,2,C_CH,32],bf16); R=sb("spread",[P,2,C_CH,4,32],bf16)
        pt=pb("k_prefix",[P,2,C_GC],f32); cb=[pb(f"k_slots{i}",[P,4,4,8],f32) for i in range(2)]
        s_cst=sem("const"); s_ld=sem("edges_in"); s_z=sem("zeros"); s_cl=sem("cleared"); s_ch=sem("chain"); s_g=sem("group_chain"); s_b=sem("bf16_const")
        s_valid=sem("valid"); s_pt=sem("prefix"); s_sl=sem("prefix_read"); s_kh=sem("tile_onehot"); s_oh=sem("onehots"); s_rp=sem("spread"); s_cm=sem("placed"); s_cv=sem("compacted")
        mine=(s_cst,s_ld,s_z,s_cl,s_ch,s_g,s_b,s_valid,s_pt,s_sl,s_kh,s_oh,s_rp,s_cm,s_cv)
        ctx.callback(lambda: [nc.gpsimd.sem_clear(x) for x in mine])
        block=ctx.enter_context(nc.Block())
        @block.sync
        def _(sp):
            sp.wait_ge(s_z,1)
            for row,t in ((1,dst),(0,src)):
                sp.dma_start(t[:,0:E//P],edges[row].rearrange("(p c) -> p c",p=P)).then_inc(s_ld,16)
            z=zeros[:,:].bitcast(f32)
            sp.dma_start(srclist.rearrange("(p j) one -> p (j one)",p=P),zeros[:,:]).then_inc(s_cl,16)
            sp.dma_start(car_d.rearrange("(p j) k -> p (j k)",p=P),z[:,0:NCH*2*PAY]).then_inc(s_cl,16)
            with sp.Fori(0,5) as k:
                sp.dma_start(seg.rearrange("(p j) c -> p (j c)",p=P)[:,ds(k*PCOLS,PCOLS)],z).then_inc(s_cl,16)
            with sp.Fori(0,RES) as k:
                sp.dma_start(res_d.rearrange("(p j) c -> p (j c)",p=P)[:,ds(k*PCOLS,PCOLS)],z).then_inc(s_cl,16)
            sp.wait_ge(s_cl,16*(7+RES))
        def spread(eng,q,k,c0,c1):
            return eng.tensor_tensor(R[:,q,c0:c1],KH[:,q,c0:c1,:].unsqueeze(2).to_broadcast([P,c1-c0,4,32]),
                V[:,:,k*C_CH+c0:k*C_CH+c1].rearrange("p v c -> p c v").unsqueeze(3).to_broadcast([P,c1-c0,4,32]),ALU.mult)
        @block.gpsimd
        def _(pool):
            nc.gpsimd.iota(io_i[:,:],pattern=[[1,P]],base=0,channel_multiplier=0).then_inc(s_cst,1)
            nc.gpsimd.memset(before[:,:],1.0).then_inc(s_cst,1)
            pool.wait_ge(s_cst,2)
            nc.gpsimd.affine_select(out=before[:,:],in_=before[:,:],compare_op=ALU.is_gt,fill=0.0,base=0,pattern=[[1,P]],channel_multiplier=-1).then_inc(s_cst,1)
            with pool.Fori(0,C_GRP) as it:
                for k in range(C_GK):
                    n=it*C_GK+k; q=k%2
                    pool.wait_ge(s_kh,n+1)
                    pool.wait_ge(s_cm,n+1)
                    spread(nc.gpsimd,q,k,0,C_POOL).then_inc(s_rp,1)
        @block.tensor
        def _(pe):
            pe.wait_ge(s_b,1)
            pe.sem_inc(s_cm,2)
            with pe.Fori(0,C_GRP) as it:
                pe.wait_ge(s_valid,it+1)
                pe.wait_ge(s_sl,it+1)
                nc.tensor.matmul(pt[:,0,:],before_b[:,:],valid[:,:],start=True,stop=True)
                nc.tensor.matmul(pt[:,1,:],ones_b[:,:],valid[:,:],start=True,stop=True).then_inc(s_pt,1)
                for k in range(C_GK):
                    n=it*C_GK+k; q=k%2
                    pe.wait_ge(s_oh,n+1)
                    pe.wait_ge(s_rp,n+1)
                    pe.wait_ge(s_cv,n+1)
                    for j in range(C_CH):
                        last=nc.tensor.matmul(cb[q][:,:,:,:],OS[:,q,j,:],R[:,q,j],start=(j==0),stop=(j==C_CH-1))
                    last.then_inc(s_cm,1)
        @block.scalar
        def _(act):
            act.sem_inc(s_cv,2)
            with act.Fori(0,C_GRP) as it:
                for k in range(C_GK):
                    n=it*C_GK+k; q=k%2
                    act.wait_ge(s_cm,n+3)
                    nc.scalar.activation(comp[:,:,:,ds(n*8,8)],cb[q][:,:,:,:],ACT.Identity).then_inc(s_cv,1)
            act.wait_ge(s_cv,2+C_NCH)
        @block.vector
        def _(dve):
            ch=Chain(dve,s_ch)
            nc.vector.memset(zeros[:,:],0).then_inc(s_z,1)
            ch.mark(nc.vector.memset(dst[:,E//P:],M)); ch.mark(nc.vector.memset(src[:,E//P:],0))
            ch.mark(nc.vector.memset(ones_b[:,:],1.0)); ch(nc.vector.memset(notfirst[:,:],1.0))
            ch(nc.vector.memset(notfirst[:,::C_CH],0.0))
            dve.wait_ge(s_cst,3)
            ch.mark(nc.vector.tensor_copy(before_b[:,:],before[:,:]))
            ch(nc.vector.tensor_copy(io_b[:,:],io_i[:,:]))
            dve.sem_inc(s_b,1); dve.sem_inc(s_sl,1)
            dve.wait_ge(s_ld,32)
            gc=Chain(dve,s_g,C_GCH)
            with dve.Fori(0,C_GRP) as it:
                gc.body(it)
                d=dst[:,ds(it*C_GC,C_GC)]; s_=src[:,ds(it*C_GC,C_GC)]
                dve.wait_ge(s_oh,it*C_GK); dve.wait_ge(s_rp,it*C_GK)
                gc.mark(nc.vector.tensor_single_scalar(ti[:,0],d,13,op=ALU.logical_shift_right))
                gc.mark(nc.vector.tensor_single_scalar(ti[:,1],d,127,op=ALU.bitwise_and))
                gc.mark(nc.vector.tensor_single_scalar(ti[:,2],d,7,op=ALU.logical_shift_right))
                gc(nc.vector.tensor_scalar_min(ti[:,3],s_,float(M-1)))
                gc.mark(nc.vector.tensor_scalar(tf[:,:],ti[:,0],0.0,None,ALU.is_equal))
                nc.vector.tensor_scalar(valid[:,:],ti[:,0],0.0,None,ALU.is_equal).then_inc(s_valid,1)
                gc.mark(nc.vector.tensor_scalar_add(V[:,0],ti[:,1],1.0))
                gc.mark(nc.vector.tensor_copy(V[:,1],ti[:,2]))
                gc.mark(nc.vector.tensor_single_scalar(si[:,1],ti[:,3],127,op=ALU.bitwise_and))
                gc(nc.vector.tensor_single_scalar(si[:,2],ti[:,3],7,op=ALU.logical_shift_right))
                gc.mark(nc.vector.tensor_copy(V[:,2],si[:,1])); gc.mark(nc.vector.tensor_copy(V[:,3],si[:,2]))
                dve.wait_ge(s_pt,it+1)
                gc(nc.vector.tensor_tensor_scan(out=incl[:,:],data0=notfirst[:,:],data1=pt[:,1,:],initial=0.0,op0=ALU.mult,op1=ALU.add))
                gc(nc.vector.tensor_copy(vtot[:,ds(it*C_GK,C_GK)],incl[:,C_CH-1::C_CH]))
                gc(nc.vector.tensor_tensor(incl[:,:],incl[:,:],pt[:,1,:],ALU.subtract))
                gc(nc.vector.tensor_tensor(si[:,0],incl[:,:],pt[:,0,:],ALU.add))
                dve.sem_inc(s_sl,1)
                gc.mark(nc.vector.tensor_single_scalar(si[:,1],si[:,0],127,op=ALU.bitwise_and))
                gc.mark(nc.vector.tensor_single_scalar(si[:,2],si[:,0],7,op=ALU.logical_shift_right))
                gc(nc.vector.tensor_scalar(tf[:,:],tf[:,:],-64.0,64.0,ALU.mult,ALU.add))
                gc.mark(nc.vector.tensor_copy(slot_lo[:,:],si[:,1]))
                gc(nc.vector.tensor_tensor(slot_hi[:,:],si[:,2],tf[:,:],ALU.add))
                for k in range(C_GK):
                    n=it*C_GK+k; q=k%2; c=slice(k*C_CH,(k+1)*C_CH)
                    dve.wait_ge(s_cm,n+1)
                    nc.vector.tensor_tensor(KH[:,q],slot_hi[:,c].unsqueeze(2).to_broadcast([P,C_CH,32]),io_b[:,0:32].unsqueeze(1).to_broadcast([P,C_CH,32]),ALU.is_equal).then_inc(s_kh,1)
                    nc.vector.tensor_tensor(OS[:,q],slot_lo[:,c].unsqueeze(2).to_broadcast([P,C_CH,P]),io_b[:,:].unsqueeze(1).to_broadcast([P,C_CH,P]),ALU.is_equal)
                    dve.wait_ge(s_kh,n+1)
                    spread(nc.vector,q,k,C_POOL,C_CH).then_inc(s_oh,1)
                gc.end()
            ch(nc.vector.reduce_max(vm[:,:],vtot[:,:],AX.X))
            ch(nc.vector.tensor_scalar(vm[:,:],vm[:,:],1.0,float(8*P-1),ALU.max,ALU.add))
            ch(nc.vector.tensor_copy(vmi[:,0:1],vm[:,:]))
            ch(nc.vector.tensor_single_scalar(vmi[:,1:2],vmi[:,0:1],10,op=ALU.logical_shift_right))
            ch(nc.vector.tensor_scalar(lim[:,:],vmi[:,1:2],float(C_HALVES),None,ALU.mult))

def rank_phase(nc,srclist,comp,lim,start_f,end_f,ident):
    ctx=ExitStack()
    with ctx:
        sb=lambda n,s,d: ctx.enter_context(nc.sbuf_tensor(n,s,d))
        pb=lambda n,s,d: ctx.enter_context(nc.psum_tensor(n,s,d))
        sem=lambda n: ctx.enter_context(nc.semaphore("r_"+n))
        iota_i=sb("iota_i",[P,P],i32); iota_b=sb("iota_b",[P,P],bf16); iota1_b=sb("iota1_b",[P,P],bf16)
        ident_b=sb("ident_b",[P,P],bf16); node=sb("node",[P,HI],i32); sti=sb("r_sti",[P,HI],u32)
        before=sb("before",[P,P],f32)
        dropped=sb("dropped",[P,E_CH],f32)
        OL=sb("OL",[P,2,E_UNIT,P],bf16); OH=sb("OH",[P,2,E_UNIT,HI],bf16)
        OLT=sb("OLT",[P,2,2,4,P],f32)
        Gm=sb("Gm",[P,2,2,4,P],bf16)
        snap=sb("snap",[P,2,E_UNIT+1,HI],f32)
        start1=sb("start1",[P,HI],f32); cnt=sb("cnt",[P,HI],f32); incl=sb("incl",[P,HI],f32); rowb=sb("rowb",[P,1],f32)
        prod=sb("prod",[P,E_UNIT,HI],f32); posf=sb("posf",[P,E_CH],f32)
        pos=sb("pos",[P,2,E_CH],u32); srcs=sb("srcs",[P,2,E_CH],i32)
        D=[pb(f"D{i}",[P,E_UNIT,HI],f32) for i in range(2)]
        OLT16=sb("OLT16",[P,2,2,4,P],bf16); notbefore=sb("notbefore",[P,P],bf16)
        T=[pb(f"T{i}",[P,4,P],bf16) for i in range(2)]
        G=[pb(f"G{i}",[P,4,P],f32) for i in range(2)]
        PP=[pb(f"PP{i}",[P,E_UNIT,HI],f32) for i in range(2)]
        S={n: sem(n) for n in (
            "cst", "node", "self_ready", "self", "pos_ready", "go", "scattered0", "scattered1",
            "t_done", "p_done", "olt_ready", "g_done", "gm_ready", "cst_b", "cnt_used", "zero_r",
            "c_ready", "cnt_done", "rows", "base", "oh_ready", "snap_ready", "d_done", "p_free",
            "dve_chain", "fin", "m_chain", "dropped")}
        def s(n): return S[n]
        compv=comp[:,:,:,:].rearrange("p v u n -> p v (u n)")
        def n_iters(eng): return eng.value_load(lim[0:1,0:1],min_val=C_HALVES,max_val=4*C_HALVES)
        def part_of(v,it,half,u=0,n=E_CH): return compv[:,v,ds((it*2+half)*E_CH+u*E_UNIT,n)]
        ctx.callback(lambda: [nc.gpsimd.sem_clear(x) for x in S.values()])
        block=ctx.enter_context(nc.Block())
        @block.gpsimd
        def _(pool):
            nc.gpsimd.iota(iota_i[:,:],pattern=[[1,P]],base=0,channel_multiplier=0).then_inc(s("cst"),1)
            nc.gpsimd.memset(before[:,:],1.0).then_inc(s("cst"),1)
            nc.gpsimd.memset(ident[:,:],0.0).then_inc(s("cst"),1)
            pool.wait_ge(s("cst"),3)
            nc.gpsimd.affine_select(out=before[:,:],in_=before[:,:],compare_op=ALU.is_gt,fill=0.0,base=0,pattern=[[1,P]],channel_multiplier=-1).then_inc(s("cst"),1)
            nc.gpsimd.affine_select(out=ident[:,:],in_=ident[:,:],compare_op=ALU.not_equal,fill=1.0,base=0,pattern=[[-1,P]],channel_multiplier=1).then_inc(s("cst"),1)
            nc.gpsimd.iota(node[:,:],pattern=[[P,HI]],base=0,channel_multiplier=1).then_inc(s("node"),1)
            pool.wait_ge(s("self_ready"),1); pool.wait_ge(s("node"),1)
            def put(pos_ap,val_ap,done):
                nc.gpsimd.indirect_dma_start(out=srclist,out_offset=bass.IndirectOffsetOnAxis(ap=pos_ap,axis=0),in_=val_ap,in_offset=None,
                    bounds_check=NPOS-1,oob_is_err=False).then_inc(done,16)
            for i in range(HI): put(sti[:,i:i+1],node[:,i:i+1],s("self"))
            iters=n_iters(pool)
            with pool.Fori(0,4*C_HALVES) as it, pool.If(it<iters):
                for half in range(2):
                    pool.wait_ge(s("pos_ready"), it*2+half+1)
                    pool.sem_inc(s("go"),1)
                    for j in range(E_CH): put(pos[:,half,j:j+1],srcs[:,half,j:j+1],s(f"scattered{half}"))
            pool.wait_ge(s("self"),16*HI)
            for half in range(2): pool.wait_ge(s(f"scattered{half}"),pool.snap(iters*(16*E_CH)))
        @block.scalar
        def _(act):
            iters=n_iters(act)
            with act.Fori(0,4*C_HALVES) as it, act.If(it<iters):
                for half in range(2):
                    for u in range(E_NU):
                        n=(it*2+half)*E_NU+u
                        for g in range(2):
                            act.wait_ge(s("t_done"),n*2+g+1)
                            act.wait_ge(s("p_done"),n+1)
                            nc.scalar.activation(OLT[:,u%2,g],T[g][:,:,:],ACT.Relu)
                            nc.scalar.activation(OLT16[:,u%2,g],T[g][:,:,:],ACT.Relu).then_inc(s("olt_ready"),1)
                        for g in range(2):
                            act.wait_ge(s("g_done"),n*2+g+1)
                            nc.scalar.activation(Gm[:,u%2,g],G[g][:,:,:],ACT.Relu).then_inc(s("gm_ready"),1)
        @block.tensor
        def _(pe):
            pe.wait_ge(s("cst_b"),1)
            pe.sem_inc(s("cnt_used"),2)
            pe.wait_ge(s("zero_r"),1)
            nc.tensor.matmul(D[0][:,0,:],ident[:,:],start1[:,:],start=True,stop=False,skip_group_check=True)
            iters=n_iters(pe)
            with pe.Fori(0,4*C_HALVES) as it, pe.If(it<iters):
                for u in range(2*E_NU):
                    q=u%2
                    pe.wait_ge(s("c_ready"),it*2*E_NU+u+1)
                    for j in range(E_UNIT):
                        last=nc.tensor.matmul(D[0][:,0,:],OL[:,q,j,:],OH[:,q,j,:],start=False,stop=False,skip_group_check=True)
                    last.then_inc(s("cnt_used"),1)
            nc.tensor.matmul(D[0][:,0,:],ident[:,:],start1[:,:],start=False,stop=True,skip_group_check=True).then_inc(s("cnt_done"),1)
            pe.wait_ge(s("rows"),1)
            nc.tensor.matmul(PP[0][:,0,0:1],before[:,:],incl[:,HI-1:HI],start=True,stop=True).then_inc(s("base"),1)
            pe.sem_inc(s("p_done"),2); pe.sem_inc(s("olt_ready"),2); pe.sem_inc(s("gm_ready"),2)
            with pe.Fori(0,4*C_HALVES) as it, pe.If(it<iters):
                for half in range(2):
                    def front(u):
                        n=(it*2+half)*E_NU+u
                        q=u%2
                        pe.wait_ge(s("oh_ready"),n+1)
                        for g in range(2):
                            pe.wait_ge(s("olt_ready"),n*2+g+1)
                            for j in range(4):
                                last=nc.tensor.transpose(T[g][:,j,:],OL[:,q,4*g+j,:],ident_b[:,:])
                            last.then_inc(s("t_done"),1)
                        pe.wait_ge(s("snap_ready"),n)
                        for i in range(E_UNIT):
                            last=nc.tensor.matmul(D[q][:,i:E_UNIT,:],OL[:,q,i,:],OH[:,q,i:i+1,:].to_broadcast([P,E_UNIT-i,HI]),start=(i==0),stop=(i==E_UNIT-1))
                        last.then_inc(s("d_done"),1)
                        for g in range(2):
                            pe.wait_ge(s("olt_ready"),n*2+g+3)
                            pe.wait_ge(s("gm_ready"),n*2+g+1)
                            for j in range(4):
                                nc.tensor.matmul(G[g][:,j,:],OLT16[:,q,g,j,:],OLT16[:,q,g,j,:],start=True,stop=False)
                                last=nc.tensor.matmul(G[g][:,j,:],ident_b[:,:],notbefore[:,:],start=False,stop=True)
                            last.then_inc(s("g_done"),1)
                    def back(u):
                        n=(it*2+half)*E_NU+u
                        q=u%2
                        pe.wait_ge(s("snap_ready"),n+2)
                        pe.wait_ge(s("p_free"),n+1)
                        for g in range(2):
                            pe.wait_ge(s("gm_ready"),n*2+g+3)
                            for j in range(4):
                                t=4*g+j
                                prior=snap[:,q,t,:]
                                nc.tensor.matmul(PP[q][:,t,:],OLT[:,q,g,j,:],prior,start=True,stop=False)
                                last=nc.tensor.matmul(PP[q][:,t,:],Gm[:,q,g,j,:],OH[:,q,t,:],start=False,stop=True)
                        last.then_inc(s("p_done"),1)
                    front(0)
                    for u in range(1,E_NU):
                        front(u); back(u-1)
                    back(E_NU-1)
        @block.vector
        def _(dve):
            ch=s("dve_chain"); k=[0]
            def link(ins):
                k[0]+=1; ins.then_inc(ch,1); dve.wait_ge(ch,k[0])
            dve.wait_ge(s("cst"),5)
            nc.vector.tensor_copy(iota_b[:,:],iota_i[:,:])
            nc.vector.tensor_scalar_add(iota1_b[:,:],iota_i[:,:],1.0)
            nc.vector.tensor_scalar(notbefore[:,:],before[:,:],1.0,None,ALU.subtract)
            nc.vector.tensor_copy(ident_b[:,:],ident[:,:]).then_inc(s("cst_b"),1)
            nc.vector.memset(start1[:,:],0.0).then_inc(s("zero_r"),1)
            dve.wait_ge(s("zero_r"),1)
            def onehots(it,half,u):
                q=u%2
                nc.vector.tensor_tensor(OL[:,q],part_of(0,it,half,u,E_UNIT).unsqueeze(2).to_broadcast([P,E_UNIT,P]),
                    iota1_b[:,:].unsqueeze(1).to_broadcast([P,E_UNIT,P]),ALU.is_equal)
                return nc.vector.tensor_tensor(OH[:,q],part_of(1,it,half,u,E_UNIT).unsqueeze(2).to_broadcast([P,E_UNIT,HI]),
                    iota_b[:,0:HI].unsqueeze(1).to_broadcast([P,E_UNIT,HI]),ALU.is_equal)
            iters=n_iters(dve)
            with dve.Fori(0,4*C_HALVES) as it, dve.If(it<iters):
                for half in range(2):
                    for u in range(E_NU):
                        n=it*2*E_NU+half*E_NU+u
                        dve.wait_ge(s("cnt_used"),n+1)
                        onehots(it,half,u).then_inc(s("c_ready"),1)
            dve.wait_ge(s("cnt_done"),1)
            link(nc.vector.tensor_scalar_add(cnt[:,:],D[0][:,0,:],1.0))
            nc.vector.tensor_tensor_scan(out=incl[:,:],data0=cnt[:,:],data1=cnt[:,:],initial=0.0,op0=ALU.add,op1=ALU.bypass).then_inc(s("rows"),1)
            dve.wait_ge(s("rows"),1)
            dve.wait_ge(s("base"),1)
            link(nc.vector.tensor_copy(rowb[:,:],PP[0][:,0,0:1]))
            link(nc.vector.tensor_sub(start1[:,:],incl[:,:],cnt[:,:]))
            nc.vector.tensor_scalar(start1[:,:],start1[:,:],rowb[:,0:1],1.0,ALU.add,ALU.add).then_inc(s("fin"),1)
            dve.wait_ge(s("fin"),1)
            link(nc.vector.tensor_scalar_add(start_f[:,:],start1[:,:],-1.0))
            nc.vector.tensor_copy(sti[:,:],start_f[:,:]).then_inc(s("self_ready"),1)
            link(nc.vector.tensor_tensor(end_f[:,:],start_f[:,:],cnt[:,:],ALU.add))
            link(nc.vector.tensor_scalar_add(end_f[:,:],end_f[:,:],-1.0))
            nc.vector.tensor_copy(snap[:,1,E_UNIT,:],start1[:,:]).then_inc(s("snap_ready"),1)
            dve.sem_inc(s("p_free"),2)
            with dve.Fori(0,4*C_HALVES) as it, dve.If(it<iters):
                for half in range(2):
                    c=[0]
                    K=E_NU+1
                    def sl(ins):
                        c[0]+=1; ins.then_inc(s("m_chain"),1); dve.wait_ge(s("m_chain"),it*2*K+half*K+c[0])
                    def gen(u):
                        n=it*2*E_NU+half*E_NU+u
                        dve.wait_ge(s("p_done"),n+1)
                        onehots(it,half,u).then_inc(s("oh_ready"),1)
                    def snapshot(u):
                        n=it*2*E_NU+half*E_NU+u
                        dve.wait_ge(s("d_done"),n+1)
                        dve.wait_ge(s("p_done"),n+1)
                        dve.wait_ge(s("snap_ready"),n+1)
                        nc.vector.tensor_copy(snap[:,u%2,0],snap[:,1-u%2,E_UNIT])
                        nc.vector.tensor_tensor(snap[:,u%2,1:E_UNIT+1],D[u%2][:,:,:],snap[:,1-u%2,E_UNIT:E_UNIT+1,:].to_broadcast([P,E_UNIT,HI]),ALU.add).then_inc(s("snap_ready"),1)
                    def extract(u):
                        n=it*2*E_NU+half*E_NU+u
                        dve.wait_ge(s("p_done"),n+3)
                        dve.wait_ge(s("p_free"),n+2)
                        sl(nc.vector.tensor_tensor(prod[:,:,:],PP[u%2][:,:,:],OH[:,u%2],ALU.mult))
                        nc.vector.tensor_reduce(posf[:,E_UNIT*u:E_UNIT*(u+1)],prod[:,:,:],axis=AX.X,op=ALU.add).then_inc(s("p_free"),1)
                    gen(0); gen(1); snapshot(0)
                    for u in range(E_NU):
                        if u+1<E_NU: snapshot(u+1)
                        extract(u)
                        if u+2<E_NU: gen(u+2)
                    dve.wait_ge(s("p_free"),(it*2*E_NU+half*E_NU+E_NU)+2)
                    dve.wait_ge(s(f"scattered{half}"),it*16*E_CH)
                    nc.vector.tensor_scalar(dropped[:,:],part_of(0,it,half),0.0,float(1<<20),ALU.is_equal,ALU.mult).then_inc(s("dropped"),1)
                    dve.wait_ge(s("dropped"),it*2+half+1)
                    sl(nc.vector.tensor_tensor(posf[:,:],posf[:,:],dropped[:,:],ALU.add))
                    nc.vector.tensor_copy(pos[:,half,:],posf[:,:])
                    nc.vector.scalar_tensor_tensor(srcs[:,half,:],part_of(3,it,half),float(P),part_of(2,it,half),ALU.mult,ALU.add).then_inc(s("pos_ready"),1)
                    dve.wait_ge(s("pos_ready"),it*2+half+1)
                    dve.sem_inc(s("go"),1)

def mix_phase(nc,A,table,x_all,t_all,idx_all,w4_all,wdT,ident):
    with ExitStack() as ctx:
        sb=lambda n,s,d: ctx.enter_context(nc.sbuf_tensor(n,s,d))
        sem=lambda n: ctx.enter_context(nc.semaphore("m_"+n))
        bank=[ctx.enter_context(nc.psum_tensor(f"bank{i}",[P,4,P],f32)) for i in range(8)]
        stage=sb("stage",[P,3,12],u32)
        patch=sb("patch",[P,3,3,DG,4*CG],f32)
        wp=sb("wp",[P,3,4,DG,CG],f32); wpair=sb("wpair",[P,3,2,P],f32); wsum=sb("wsum",[P,3,3,P],f32)
        vT=sb("vT",[P,3,3,P],f32)
        rl=sb("rl",[P,P],f32)
        tn=sb("tn",[P,2,P],f32); st=sb("lnst",[P,NT,6],f32); mv=sb("lnmv",[P,NT,2],f32); rs=sb("lnrs",[P,NT],f32)
        tnT=sb("tnT",[P,HW],f32)
        WqT=sb("WqT",[P,HEADS,P],f32); WkT=sb("WkT",[P,P],f32); WvT=sb("WvT",[P,P],f32); WoT=sb("WoT",[P,NT,P],f32)
        KT=sb("KT",[P,8,P],f32); V=sb("V",[P,8,P],f32); QT=sb("QT",[P,HW],f32)
        pr=sb("pr",[P,2,HW],f32); mx=sb("mx",[P,2],f32); nmx=sb("nmx",[P,2],f32); sm=sb("sm",[P,2],f32); ri=sb("ri",[P,2],f32)
        wos=sb("wos",[P,2,P],f32); GT=sb("GT",[P,HW],f32); Gs=sb("Gs",[P,8,P],f32)
        wnat=sb("wnat",[P,P],f32)
        sm2=sb("sm2",[P,2,2],f32); mx2=sb("mx2",[P,2,2],f32)
        xs=sb("xs",[P,P],f32); wqh=sb("wqh",[P,P],f32)
        s_stage=[sem(f"staged{i}") for i in range(3)]; s_patch=[sem(f"patches{i}") for i in range(3)]
        s_go=sem("go"); s_xs=sem("x_tile"); s_pj=sem("projected"); s_wqh=sem("wq_head")
        s_w=[sem(f"weights{i}") for i in range(2)]; s_wt=sem("wt"); s_wte=sem("wt_out"); s_wp=sem("weighted"); s_v=sem("sampled"); s_ve=sem("sampled_out"); s_conv=sem("conv_done"); s_rl=sem("relu_out")
        s_t=sem("tokens"); s_ch=sem("head_chain"); s_l=sem("norm_chain"); s_d=sem("sample_chain"); s_var=sem("variance"); s_sd=sem("deviation")
        s_tn=sem("normalized"); s_tt=sem("tn_transposed"); s_tte=sem("tnT_ready"); s_kv=sem("kv_done"); s_kve=sem("kv_ready")
        s_q=sem("q_done"); s_qe=sem("q_ready"); s_s=sem("scores"); s_m=sem("max_ready"); s_p=sem("probs"); s_wo=sem("scaled_wo"); s_g=sem("gathered")
        s_ge=sem("GT_ready"); s_gt=sem("G_transposed"); s_gs=sem("G_ready"); s_o=sem("head_out"); s_a=sem("head_added")
        parts=[(A['L1_attn_Wq'][h*P:(h+1)*P,:],WqT[:,h,:]) for h in range(HEADS)]+[(A['L1_attn_Wk'],WkT[:,:]),(A['L1_attn_Wv'],WvT[:,:])]+[(A['L1_attn_Wo'][:,i*P:(i+1)*P],WoT[:,i,:]) for i in range(NT)]
        wbuf=lambda n: (wnat[:,:],xs[:,:])[n%2]
        flat=lambda ap: ap.rearrange("p a b -> p (a b)")
        block=ctx.enter_context(nc.Block())
        @block.sync
        def _(sp):
            for n,(src,_) in enumerate(parts):
                if n>=2: sp.wait_ge(s_wt,n-1)
                sp.dma_start(wbuf(n),src).then_inc(s_w[n%2],16)
        @block.gpsimd
        def _(pool):
            with pool.Fori(0,B*NT) as g:
                for k in range(3):
                    pool.wait_ge(s_stage[k],g+1)
                    pool.sem_inc(s_go,1)
                    for i in range(12):
                        nc.gpsimd.indirect_dma_start(out=patch[:,k,i//DG,i%DG,:],out_offset=None,in_=table,
                            in_offset=bass.IndirectOffsetOnAxis(ap=stage[:,k,i:i+1],axis=0)).then_inc(s_patch[k],16)
        @block.tensor
        def _(pe):
            for n in range(len(parts)):
                pe.wait_ge(s_w[n%2],16*(n//2)+16)
                if n>=4: pe.wait_ge(s_wte,n-3)
                nc.tensor.transpose(bank[n%4][:,0,:],wbuf(n),ident[:,:]).then_inc(s_wt,1)
            pe.wait_ge(s_wte,len(parts))
            pe.sem_inc(s_v,3); pe.sem_inc(s_pj,3); pe.sem_inc(s_tt,2); pe.sem_inc(s_g,2)
            def sample(g,k):
                pe.wait_ge(s_wp,g*3+k+1)
                pe.wait_ge(s_ve,g*3+k)
                for t in range(3): last=nc.tensor.transpose(bank[6][:,t,:],wsum[:,k,t,:],ident[:,:])
                last.then_inc(s_v,1)
            def project(g,k):
                pe.wait_ge(s_ve,g*3+k+1)
                if k==0: pe.wait_ge(s_rl,g)
                for t in range(3):
                    last=nc.tensor.matmul(bank[7][:,0,:],vT[:,k,t,:],wdT[:,3*k+t,:],start=(k+t==0),stop=(k==2 and t==2))
                last.then_inc(s_pj,1)
                if k==2:
                    pe.wait_ge(s_xs,g+1)
                    pe.wait_ge(s_t,g)
                    nc.tensor.transpose(bank[7][:,1,:],xs[:,:],ident[:,:]).then_inc(s_conv,1)
            def queries(hh):
                pe.wait_ge(s_wqh,hh+1)
                pe.wait_ge(s_p,hh*NT+7)
                for i in range(2):
                    nc.tensor.matmul(bank[i][:,:,:],wqh[:,:],tnT[:,i*512:(i+1)*512],start=True,stop=True).then_inc(s_q,1)
            def scores(hh,i):
                if i==0: pe.wait_ge(s_qe,hh*2+2)
                elif i==1: pe.wait_ge(s_gs,hh*2)
                else: pe.wait_ge(s_p,hh*NT+i+7)
                for k in range(2):
                    last=nc.tensor.matmul(bank[2*(i%2)+k][:,:,:],QT[:,i*P:(i+1)*P],KT[:,4*k:4*k+4,:],start=True,stop=True)
                last.then_inc(s_s,1)
            def gather(hh,i):
                pe.wait_ge(s_p,hh*NT+i+9); pe.wait_ge(s_wo,hh*NT+i+1)
                for k in range(2):
                    last=nc.tensor.matmul(bank[4+k][:,:,:],wos[:,i%2,:],pr[:,i%2,k*512:(k+1)*512],start=(i==0),stop=(i==NT-1))
                last.then_inc(s_g,1)
            def head(b,h,sampling,more):
                hh=b*HEADS+h; g=hh+HEADS
                scores(hh,1)
                for i in range(NT):
                    if i+2<NT: scores(hh,i+2)
                    if i==6 and more: queries(hh+1)
                    gather(hh,i)
                    if sampling and i in (1,3,5): sample(g,i//2)
                    if sampling and i in (2,4,6): project(g,i//2-1)
                if more: scores(hh+1,0)
                for k in range(2):
                    pe.wait_ge(s_ge,hh*2+k+1)
                    for j in range(4):
                        last=nc.tensor.transpose(bank[2+k][:,j,:],GT[:,(4*k+j)*P:(4*k+j+1)*P],ident[:,:])
                    last.then_inc(s_gt,1)
                for j in range(8):
                    if j==0: pe.wait_ge(s_a,hh)
                    if j%4==0: pe.wait_ge(s_gs,hh*2+j//4+1)
                    last=nc.tensor.matmul(bank[6][:,3,:],V[:,j,:],Gs[:,j,:],start=(j==0),stop=(j==7))
                last.then_inc(s_o,1)
            def image(b,sampling):
                for m in range(NT):
                    pe.wait_ge(s_tn,b*NT+m+1)
                    pe.wait_ge(s_tte,b*NT+m+1)
                    nc.tensor.transpose(bank[m%2][:,0,:],tn[:,m%2,:],ident[:,:]).then_inc(s_tt,1)
                pe.wait_ge(s_tte,b*NT+NT+2)
                for n,(w,h) in enumerate(((WkT,0),(WkT,1),(WvT,0),(WvT,1))):
                    nc.tensor.matmul(bank[2+n][:,:,:],w[:,:],tnT[:,h*512:(h+1)*512],start=True,stop=True).then_inc(s_kv,1)
                queries(b*HEADS)
                pe.wait_ge(s_kve,b*4+4)
                scores(b*HEADS,0)
                with pe.Fori(0,HEADS-1) as h: head(b,h,sampling,True)
                head(b,HEADS-1,sampling,False)
            with pe.Fori(0,NT) as g:
                for k in range(3): sample(g,k); project(g,k)
            with pe.Fori(0,B-1) as b: image(b,True)
            image(B-1,False)
        @block.scalar
        def _(act):
            for n,(_,dst) in enumerate(parts):
                act.wait_ge(s_wt,n+1)
                nc.scalar.activation(dst,bank[n%4][:,0,:],ACT.Identity).then_inc(s_wte,1)
            act.sem_inc(s_tte,2); act.sem_inc(s_p,8)
            nc.scalar.activation(wqh[:,:],WqT[:,0,:],ACT.Identity).then_inc(s_wqh,1)
            def samples_out(g,k):
                act.wait_ge(s_v,g*3+k+4)
                act.wait_ge(s_pj,g*3+k+1)
                nc.scalar.activation(vT[:,k],bank[6][:,0:3,:],ACT.Identity).then_inc(s_ve,1)
            def relu(g):
                act.wait_ge(s_conv,g+1)
                act.wait_ge(s_t,g)
                nc.scalar.activation(rl[:,:],bank[7][:,0,:],ACT.Relu).then_inc(s_rl,1)
            def queries_out(hh):
                for i in range(2):
                    act.wait_ge(s_q,hh*2+i+1)
                    nc.scalar.activation(QT[:,i*512:(i+1)*512],flat(bank[i][:,:,:]),ACT.Identity).then_inc(s_qe,1)
            def head(b,h,sampling,more):
                hh=b*HEADS+h; g=hh+HEADS
                for i in range(NT):
                    q=i%2
                    act.wait_ge(s_m,hh*NT+i+1)
                    act.wait_ge(s_g,hh*NT+i+1)
                    for k in range(2):
                        last=nc.scalar.activation(pr[:,q,k*512:(k+1)*512],flat(bank[2*q+k][:,:,:]),ACT.Exp,bias=nmx[:,q:q+1],scale=0.25,accum_out=sm2[:,q,k:k+1])
                    last.then_inc(s_p,1)
                    if sampling and i in (2,4,6): samples_out(g,i//2-1)
                    if i==1:
                        act.wait_ge(s_q,hh*2+2)
                        nc.scalar.activation(wqh[:,:],WqT[:,ds(h+1,1),:].rearrange("p a c -> p (a c)") if more else WqT[:,0,:],ACT.Identity).then_inc(s_wqh,1)
                if more: queries_out(hh+1)
                if sampling: relu(g)
                for k in range(2):
                    act.wait_ge(s_g,hh*NT+NT+2)
                    nc.scalar.activation(GT[:,k*512:(k+1)*512],flat(bank[4+k][:,:,:]),ACT.Identity).then_inc(s_ge,1)
                act.wait_ge(s_o,hh)
                for k in range(2):
                    act.wait_ge(s_gt,hh*2+k+1)
                    nc.scalar.activation(Gs[:,4*k:4*k+4,:],bank[2+k][:,:,:],ACT.Identity).then_inc(s_gs,1)
            def image(b,sampling):
                act.wait_ge(s_var,b+1)
                nc.scalar.activation(rs[:,:],rs[:,:],ACT.Sqrt).then_inc(s_sd,1)
                for m in range(NT):
                    act.wait_ge(s_tt,b*NT+m+3)
                    nc.scalar.activation(tnT[:,m*P:(m+1)*P],bank[m%2][:,0,:],ACT.Identity).then_inc(s_tte,1)
                for n in range(4):
                    act.wait_ge(s_kv,b*4+n+1)
                    if n<2:
                        nc.scalar.activation(KT[:,:,n*64:(n+1)*64],flat(bank[2+n][:,:,:]).rearrange("p (o j) -> p j o",j=8),ACT.Identity).then_inc(s_kve,1)
                    else:
                        nc.scalar.activation(V[:,4*(n-2):4*(n-2)+4,:],bank[2+n][:,:,:],ACT.Identity).then_inc(s_kve,1)
                queries_out(b*HEADS)
                with act.Fori(0,HEADS-1) as h: head(b,h,sampling,True)
                head(b,HEADS-1,sampling,False)
            with act.Fori(0,NT) as g:
                for k in range(3): samples_out(g,k)
                relu(g)
            with act.Fori(0,B-1) as b: image(b,True)
            image(B-1,False)
        @block.vector
        def _(dve):
            for k in range(3):
                nc.vector.tensor_copy(stage[:,k,:],idx_all[:,12*k:12*k+12]).then_inc(s_stage[k],1)
            lc=Chain(dve,s_l,LKM); hc=Chain(dve,s_ch,HKM); dc=Chain(dve,s_d,6)
            dve.wait_ge(s_wt,len(parts))
            def x_tile(b,m,g):
                dve.wait_ge(s_conv,g)
                nc.vector.tensor_copy(xs[:,:],x_all[:,ds(b,1),ds(m*P,P)].rearrange("p a n -> p (a n)")).then_inc(s_xs,1)
            def weigh(g,k):
                dc.base=g*6; dc.n=2*k
                dve.wait_ge(s_patch[k],g*192+192)
                dve.wait_ge(s_wp,g*3+k)
                dve.wait_ge(s_v,g*3+k+1)
                for t in range(3):
                    last=nc.vector.tensor_tensor(wp[:,t].rearrange("p j g c -> p g j c"),
                        patch[:,k,t].rearrange("p g (j c) -> p g j c",j=4),
                        w4_all[:,ds(g*144+(3*k+t)*16,16)].rearrange("p (g j) -> p g j",j=4).unsqueeze(3).to_broadcast([P,DG,4,CG]),ALU.mult)
                dc(last)
                nc.vector.tensor_copy(stage[:,k,:],idx_all[:,ds((g+1)*36+12*k,12)]).then_inc(s_stage[k],1)
                w=wp[:,:,:,:,:].rearrange("p t j g c -> p t j (g c)")
                dc(nc.vector.tensor_tensor(wpair[:,:,:,:],w[:,:,0:2],w[:,:,2:4],ALU.add))
                nc.vector.tensor_tensor(wsum[:,k],wpair[:,:,0],wpair[:,:,1],ALU.add).then_inc(s_wp,1)
            def add_conv(g):
                dve.wait_ge(s_rl,g+1)
                nc.vector.tensor_tensor(t_all[:,ds(g,1),:].rearrange("p a c -> p (a c)"),bank[7][:,1,:],rl[:,:],ALU.add).then_inc(s_t,1)
            def maximum(hh,i):
                q=i%2; hc.base=hh*HKM
                if i==0: hc.n=0
                dve.wait_ge(s_s,hh*NT+i+1)
                hc.mark(nc.vector.reduce_max(mx2[:,q,0:1],flat(bank[2*q][:,:,:]),AX.X))
                hc(nc.vector.reduce_max(mx2[:,q,1:2],flat(bank[2*q+1][:,:,:]),AX.X))
                hc(nc.vector.tensor_tensor(mx[:,q:q+1],mx2[:,q,0:1],mx2[:,q,1:2],ALU.max))
                nc.vector.tensor_scalar_mul(nmx[:,q:q+1],mx[:,q:q+1],-0.25).then_inc(s_m,1)
            def scale_wo(hh,i):
                q=i%2
                dve.wait_ge(s_p,hh*NT+i+9)
                hc(nc.vector.tensor_tensor(sm[:,q:q+1],sm2[:,q,0:1],sm2[:,q,1:2],ALU.add))
                hc(nc.vector.reciprocal(ri[:,q:q+1],sm[:,q:q+1]))
                nc.vector.tensor_scalar(wos[:,q,:],WoT[:,i,:],ri[:,q:q+1],None,ALU.mult).then_inc(s_wo,1)
            def head(b,h,sampling,more):
                hh=b*HEADS+h; g=hh+HEADS
                hc.base=hh*HKM; hc.n=3
                for i in range(NT):
                    if i+1<NT: maximum(hh,i+1)
                    scale_wo(hh,i)
                    if sampling and i in (0,2,4): weigh(g,i//2)
                    if sampling and i==1: x_tile(b+1,h,g)
                hc.end()
                if more: maximum(hh+1,0)
                if sampling: add_conv(g)
                dve.wait_ge(s_o,hh+1)
                nc.vector.tensor_tensor(t_all[:,ds(hh,1),:].rearrange("p a c -> p (a c)"),bank[6][:,3,:],t_all[:,ds(hh,1),:].rearrange("p a c -> p (a c)"),ALU.add).then_inc(s_a,1)
            def image(b,sampling):
                dve.wait_ge(s_t,b*NT+NT)
                lc.body(b)
                for m in range(NT):
                    lc.mark(nc.vector.bn_stats(st[:,m,:],t_all[:,ds(b*NT+m,1),:].rearrange("p a c -> p (a c)")))
                lc.sync()
                dve.sem_inc(s_go,1)
                for m in range(NT): lc.mark(nc.vector.bn_aggr(mv[:,m,:],st[:,m,:]))
                lc.sync()
                nc.vector.tensor_scalar_add(rs[:,:],mv[:,:,1],1e-5).then_inc(s_var,1)
                dve.wait_ge(s_sd,b+1)
                lc(nc.vector.reciprocal(rs[:,:],rs[:,:]))
                for m in range(NT):
                    dve.wait_ge(s_tt,b*NT+m+1)
                    nc.vector.tensor_scalar(tn[:,m%2,:],t_all[:,ds(b*NT+m,1),:].rearrange("p a c -> p (a c)"),mv[:,m,0:1],rs[:,m:m+1],ALU.subtract,ALU.mult).then_inc(s_tn,1)
                lc.end()
                maximum(b*HEADS,0)
                with dve.Fori(0,HEADS-1) as h: head(b,h,sampling,True)
                head(b,HEADS-1,sampling,False)
            with dve.Fori(0,NT) as g:
                x_tile(0,g,g)
                for k in range(3): weigh(g,k)
                add_conv(g)
            with dve.Fori(0,B-1) as b: image(b,True)
            image(B-1,False)
LKM=17; HKM=8*5
def gat_phase(nc,A,O,t_all,start_f,end_f,srclist,seg,pay_d,res_d,car_d,y_d,ident):
    with ExitStack() as ctx:
        sb=lambda n,s,d: ctx.enter_context(nc.sbuf_tensor(n,s,d))
        sem=lambda n: ctx.enter_context(nc.semaphore("g_"+n))
        bank=[ctx.enter_context(nc.psum_tensor(f"gb{i}",[P,4,P],f32)) for i in range(8)]
        W=sb("Wg",[P,HF],f32); att=sb("att",[P,2,HF],f32); cst=sb("lncst",[P,3,HF],f32)
        b1=sb("b1f",[P,EXP,2],f32); b2=sb("b2f",[P,EXP*P],f32)
        W1=sb("W1s",[P,EXP,2*P],f32); W2=sb("W2s",[P,EXP,2,P],f32)
        st=sb("st2",[P,NT,6],f32); mv=sb("mv2",[P,NT,2],f32); rs=sb("rs2",[P,NT],f32)
        tn=sb("tn_2",[P,2,P],f32); tT=sb("tT",[P,2,P],f32)
        sti=sb("sti",[P,HI],u32); eni=sb("eni",[P,HI],u32); rowi=sb("rowi",[P,HI],u32); srow=sb("srow",[P,HI],u32)
        ends=sb("node_ends",[P,1],f32)
        carry=sb("carry",[P,2,2*PAY],f32); gate=sb("gate",[P,HI,EXP],f32)
        rloc=sb("rloc",[P,HI,RES],f32); rcar=sb("rcar",[P,HI,2*PAY],f32)
        s_w=sem("weights"); s_ch=sem("dve_chain"); s_l=sem("dve_ln"); s_var=sem("var"); s_sd=sem("sd"); s_tn=sem("tn"); s_tt=sem("tt"); s_te=sem("tT"); s_h=sem("h"); s_he=sem("h_out")
        s_pay=sem("pay_ready"); s_payd=sem("pay_written"); s_segr=sem("seg_ready"); s_segd=sem("seg_written"); s_eni=sem("ends_ready")
        s_in=[sem(f"chunk_in{i}") for i in range(2)]; s_D=[sem(f"seg_in{i}") for i in range(2)]; s_G=[sem(f"payload{i}") for i in range(2)]; s_used=sem("chunk_used"); s_go=sem("go")
        s_c=sem("dve_scan_chain"); s_e=sem("exp_in"); s_ex=sem("exp_out"); s_r=sem("res_ready"); s_rd=[sem(f"res_written{i}") for i in range(2)]
        s_a1=sem("row_ends"); s_a2=sem("row_ends_T"); s_a3=sem("row_starts_T"); s_a4=sem("row_starts")
        s_x=sem("rows"); s_xt=sem("rows_T"); s_x1=sem("x1"); s_x2=sem("x2"); s_cr=sem("carry"); s_crT=sem("carryT"); s_cd=[sem(f"carry_written{i}") for i in range(2)]; s_ci=sem("carry_sb")
        s_en=sem("ends"); s_gr=sem("ends_in"); s_y1=sem("y1"); s_y2=sem("y2"); s_f=sem("ffn_h"); s_fe=sem("ffn_he"); s_y=sem("ffn_y"); s_ye=sem("ffn_ye"); s_yw=[sem(f"y_written{i}") for i in range(2)]
        s_yl=[sem(f"y_loaded{i}") for i in range(2)]; s_yu=sem("y_used"); s_acc=sem("summed"); s_o=sem("oT"); s_oe=sem("oTe"); s_out=[sem(f"out{i}") for i in range(2)]; s_fc=sem("sum_chain")
        resv=res_d.rearrange("(c p j) k -> c p (j k)",p=P,j=ROW); segv=seg.rearrange("(c p j) k -> c p (j k)",p=P,j=ROW); srcv=srclist.rearrange("(c p j) one -> c p (j one)",p=P,j=ROW)
        carv=car_d.rearrange("(c p) k -> c p k",p=P); yv=y_d.rearrange("(g p) n -> g p n",p=P)
        def n_end(eng):
            eng.wait_ge(s_eni,1)
            return eng.value_load(eni[P-1:P,HI-1:HI],min_val=NODES-1,max_val=NPOS-1)
        def group(c):
            return nc.s_assert_within(c,0,NGRP-1,skip_runtime_bounds_check_because="it stands where the chunk is known to be under NGRP")
        def on(c,end): return c*(P*ROW)<=end
        with ExitStack() as loop:
            lb=lambda n,s,d: loop.enter_context(nc.sbuf_tensor(n,s,d))
            tnT=lb("tn2T",[P,NODES],f32); hT=lb("hT",[P,EXP,2,512],f32); ysb=lb("ysb",[P,2,4,EXP*P],f32)
            h_all=lb("h_all",[P,HI,HF],f32); pm=lb("pm",[P,HI,HF],f32)
            pay=lb("pay",[P,HI,PAY],f32); seg_row=lb("seg_row",[P,HI,5],f32)
            idx=lb("g_idx",[P,2,ROW],i32); G=lb("G_in",[P,2,ROW,PAY],f32); D=lb("D_in",[P,2,ROW,5],f32)
            ns=lb("ns",[P,ROW],f32); ng=lb("ng",[P,ROW],f32); ad=lb("ad",[P,4,ROW],f32); rowe=lb("rowe",[P,8],f32); adin=lb("adin",[P,4],f32)
            aT=lb("aT",[4,P+1],f32); aTv=lb("aTv",[4,2,P],f32)
            e=lb("e",[P,4,ROW],f32); ex=lb("ex",[P,2,4,ROW],f32); nm=lb("nm",[P,HF,ROW],f32)
            res=lb("res",[P,2,ROW+1,RES],f32)
            ms=lb("row_sums",[P,3,PAY],f32); mT=lb("mT",[PAY,3,P],f32); cm=lb("cm",[PAY,2,P+1],f32); xt=lb("xt",[PAY,2,P],f32)
            block=loop.enter_context(nc.Block())
            @block.sync
            def _(sp):
                bc=lambda ap,n: ap.to_broadcast([P,n])
                sp.dma_start(W[:,:],A['L1_ffn_W_gat']).then_inc(s_w,16)
                sp.dma_start(att[:,0,:],bc(A['L1_ffn_att_src'].rearrange("(a h) k -> a (h k)",a=1),HF)).then_inc(s_w,16)
                sp.dma_start(att[:,1,:],bc(A['L1_ffn_att_dst'].rearrange("(a h) k -> a (h k)",a=1),HF)).then_inc(s_w,16)
                for i,n in enumerate(('b_gat','ln_gamma','ln_beta')):
                    sp.dma_start(cst[:,i,:],bc(A['L1_ffn_'+n].rearrange("(a k) -> a k",a=1),HF)).then_inc(s_w,16)
                sp.dma_start(b1[:,:,:],A['L1_ffn_b1'].rearrange("e (f p) -> p e f",p=P),allow_slow_non_contiguous=True).then_inc(s_w,16)
                sp.dma_start(b2[:,:],bc(A['L1_ffn_b2'].rearrange("(a e) c -> a (e c)",a=1),EXP*P)).then_inc(s_w,16)
                sp.dma_start(W1[:,:,:],A['L1_ffn_W1'].rearrange("e c f -> c e f")).then_inc(s_w,16)
                for ee in range(EXP): sp.dma_start(W2[:,ee],A['L1_ffn_W2'][ee].rearrange("(f p) c -> p f c",p=P)).then_inc(s_w,16)
                end=n_end(sp)
                sp.wait_ge(s_pay,1)
                sp.dma_start(pay_d.rearrange("(i p) c -> p i c",p=P),pay[:,:,:]).then_inc(s_payd,16)
                sp.wait_ge(s_segd,16*HI)
                with sp.Fori(0,NCH//2) as it:
                    for q in range(2):
                        c=it*2+q
                        with sp.If(on(c,end)):
                            sp.wait_ge(s_used,c+1)
                            sp.sem_inc(s_go,1)
                            sp.dma_start(idx[:,q,:],srcv[ds(c,1),:,:].rearrange("a p j -> (a p) j")).then_inc(s_in[q],16)
                            sp.dma_start(D[:,q].rearrange("p j k -> p (j k)"),segv[ds(c,1),:,:].rearrange("a p j -> (a p) j")).then_inc(s_D[q],16)
            @block.gpsimd
            def _(pool):
                pool.wait_ge(s_segr,1)
                for i in range(HI):
                    nc.gpsimd.indirect_dma_start(out=seg,out_offset=bass.IndirectOffsetOnAxis(ap=sti[:,i:i+1],axis=0),in_=seg_row[:,i,:],in_offset=None).then_inc(s_segd,16)
                pool.wait_ge(s_payd,16)
                end=n_end(pool)
                with pool.Fori(0,NCH//2) as it:
                    for q in range(2):
                        with pool.If(on(it*2+q,end)):
                            pool.wait_ge(s_used,it*2+q+1)
                            pool.sem_inc(s_go,1)
                            pool.wait_ge(s_in[q],it*16+16)
                            pool.sem_inc(s_go,1)
                            for i in range(ROW):
                                nc.gpsimd.indirect_dma_start(out=G[:,q,i,:],out_offset=None,in_=pay_d,in_offset=bass.IndirectOffsetOnAxis(ap=idx[:,q,i:i+1],axis=0)).then_inc(s_G[q],16)
                for q in range(2):
                    chunks=((end>>13)+2-q)>>1
                    pool.wait_ge(s_rd[q],pool.snap(chunks*16)); pool.sem_inc(s_go,1)
                    pool.wait_ge(s_cd[q],pool.snap(chunks*16)); pool.sem_inc(s_go,1)
                pool.wait_ge(s_en,1)
                for i in range(HI):
                    nc.gpsimd.indirect_dma_start(out=rloc[:,i,:],out_offset=None,in_=res_d,in_offset=bass.IndirectOffsetOnAxis(ap=eni[:,i:i+1],axis=0)).then_inc(s_gr,16)
                    nc.gpsimd.indirect_dma_start(out=rcar[:,i,:],out_offset=None,in_=car_d,in_offset=bass.IndirectOffsetOnAxis(ap=rowi[:,i:i+1],axis=0)).then_inc(s_gr,16)
                pool.wait_ge(s_gr,32*HI)
            @block.tensor
            def _(pe):
                pe.wait_ge(s_w,16*13)
                pe.sem_inc(s_tt,2); pe.sem_inc(s_h,2); pe.sem_inc(s_y,4) 
                with pe.Fori(0,HI//2) as it:
                    for q in range(2):
                        g=it*2+q
                        pe.wait_ge(s_tn,g+1)
                        pe.wait_ge(s_te,g+1)
                        nc.tensor.transpose(bank[q][:,0,:],tn[:,q,:],ident[:,:]).then_inc(s_tt,1)
                        pe.wait_ge(s_te,g+3)
                        pe.wait_ge(s_he,g+1)
                        nc.tensor.matmul(bank[2+q][:,0,0:HF],tT[:,q,:],W[:,:],start=True,stop=True).then_inc(s_h,1)
                end=n_end(pe)
                with pe.Fori(0,NCH//2) as it:
                    for q in range(2):
                        c=it*2+q
                        with pe.If(on(c,end)):
                            pe.wait_ge(s_a1,c+1)
                            pe.sem_inc(s_go,1)
                            for i in range(2): last=nc.tensor.transpose(bank[4][0:4,i,:],rowe[:,4*i:4*i+4],ident[:,:])
                            last.then_inc(s_a2,1)
                            pe.wait_ge(s_a3,c+1)
                            pe.sem_inc(s_go,1)
                            nc.tensor.transpose(bank[5][:,0,0:4],aT[:,0:P],ident[0:4,0:4]).then_inc(s_a4,1)
                            pe.wait_ge(s_x,c+1)
                            for i in range(3): last=nc.tensor.transpose(bank[6][0:PAY,i,:],ms[:,i,:],ident[:,:])
                            last.then_inc(s_xt,1)
                            pe.wait_ge(s_cr,c+1)
                            pe.sem_inc(s_go,1)
                            for i in range(2): last=nc.tensor.transpose(bank[7][:,i,0:PAY],cm[:,i,0:P],ident[0:PAY,0:PAY])
                            last.then_inc(s_crT,1)
                        with pe.If(it*2+q<NGRP):
                            for ef in range(8):
                                pe.wait_ge(s_fe,c*8+ef+1)
                                nc.tensor.matmul(bank[ef%2][:,:,:],W1[:,ef//2,(ef%2)*P:(ef%2+1)*P],tnT[:,ds(group(c)*512,512)],start=True,stop=True).then_inc(s_f,1)
                            for m in range(4):
                                pe.wait_ge(s_ye,c*4+m+1)
                                if m==0: pe.wait_ge(s_fe,c*8+10)
                                for ee in range(EXP):
                                    for f in range(2):
                                        last=nc.tensor.matmul(bank[2+m%2][:,ee,:],hT[:,ee,f,m*P:(m+1)*P],W2[:,ee,f,:],start=(f==0),stop=(f==1))
                                last.then_inc(s_y,1)
                pe.wait_ge(s_w,16*13)
            @block.scalar
            def _(act):
                act.sem_inc(s_te,2); act.sem_inc(s_fe,2)
                with act.Fori(0,B) as b:
                    act.wait_ge(s_var,b+1)
                    nc.scalar.activation(rs[:,:],rs[:,:],ACT.Sqrt).then_inc(s_sd,1)
                    for m in range(NT):
                        g=b*NT+m; q=m%2
                        act.wait_ge(s_tt,g+3)
                        act.wait_ge(s_h,g+1)
                        nc.scalar.activation(tnT[:,ds(g*P,P)],bank[q][:,0,:],ACT.Identity)
                        nc.scalar.activation(tT[:,q,:],bank[q][:,0,:],ACT.Identity).then_inc(s_te,1)
                end=n_end(act)
                with act.Fori(0,NCH//2) as it:
                    for q in range(2):
                        c=it*2+q
                        with act.If(on(c,end)):
                            act.wait_ge(s_e,c+1)
                            nc.scalar.activation(ex[:,:,:,:],ex[:,:,:,:],ACT.Exp).then_inc(s_ex,1)
                            act.wait_ge(s_r,c+1)
                            act.dma_start(resv[ds(c,1),:,:].rearrange("a p j -> (a p) j"),res[:,q,1:ROW+1,:].rearrange("p j k -> p (j k)")).then_inc(s_rd[q],16)
                            act.wait_ge(s_x1,c+1)
                            nc.scalar.activation(xt[:,:,:],xt[:,:,:],ACT.Exp).then_inc(s_x2,1)
                            act.wait_ge(s_ci,c+1)
                            act.dma_start(carv[ds(c,1),:,:].rearrange("a p k -> (a p) k"),carry[:,q,:]).then_inc(s_cd[q],16)
                        with act.If(it*2+q<NGRP):
                            for ef in range(8):
                                act.wait_ge(s_f,c*8+ef+1)
                                if ef==0: act.wait_ge(s_y,c*4+4)
                                nc.scalar.activation(hT[:,ef//2,ef%2,:],bank[ef%2][:,:,:].rearrange("p a b -> p (a b)"),ACT.Gelu,bias=b1[:,ef//2,ef%2:ef%2+1]).then_inc(s_fe,1)
                            act.wait_ge(s_ye,c*4+6)
                            act.dma_start(yv[ds(group(c),1),:,:].rearrange("a p n -> (a p) n"),ysb[:,q].rearrange("p m n -> p (m n)")).then_inc(s_yw[q],16)
                for q in range(2): act.wait_ge(s_yw[q],16*NGRP//2)
            @block.vector
            def _(dve):
                ch=Chain(dve,s_ch)
                dve.sem_inc(s_he,2); dve.sem_inc(s_used,2); dve.sem_inc(s_ye,2)
                ch.mark(nc.vector.tensor_copy(sti[:,:],start_f[:,:]))
                ch(nc.vector.tensor_copy(eni[:,:],end_f[:,:]))
                dve.sem_inc(s_eni,1)
                lc=Chain(dve,s_l,17)
                dve.wait_ge(s_w,16*13)
                with dve.Fori(0,B) as b:
                    lc.body(b)
                    for m in range(NT):
                        lc.mark(nc.vector.bn_stats(st[:,m,:],t_all[:,ds(b*NT+m,1),:].rearrange("p a c -> p (a c)")))
                    lc.sync(); dve.sem_inc(s_go,1)
                    for m in range(NT): lc.mark(nc.vector.bn_aggr(mv[:,m,:],st[:,m,:]))
                    lc.sync()
                    nc.vector.tensor_scalar_add(rs[:,:],mv[:,:,1],1e-5).then_inc(s_var,1)
                    dve.wait_ge(s_sd,b+1)
                    lc(nc.vector.reciprocal(rs[:,:],rs[:,:]))
                    def take_h(m):
                        g=b*NT+m
                        dve.wait_ge(s_h,g+3)
                        nc.vector.tensor_copy(h_all[:,ds(g,1),:].rearrange("p a k -> p (a k)"),bank[2+m%2][:,0,0:HF]).then_inc(s_he,1)
                    for m in range(NT):
                        dve.wait_ge(s_tt,b*NT+m+1)
                        nc.vector.tensor_scalar(tn[:,m%2,:],t_all[:,ds(b*NT+m,1),:].rearrange("p a c -> p (a c)"),mv[:,m,0:1],rs[:,m:m+1],ALU.subtract,ALU.mult).then_inc(s_tn,1)
                        if m>=1: take_h(m-1)
                    take_h(NT-1)
                    lc.end()
                dve.wait_ge(s_he,HI+2)
                for i in range(2):
                    ch(nc.vector.tensor_tensor(pm[:,:,:],h_all[:,:,:],att[:,i:i+1,:].to_broadcast([P,HI,HF]),ALU.mult))
                    dst=(pay[:,:,0:4],seg_row[:,:,1:5])[i]
                    ch(nc.vector.tensor_reduce(dst,pm[:,:,:].rearrange("p n (h k) -> p n h k",h=4),axis=AX.X,op=ALU.add))
                nc.vector.tensor_copy(pay[:,:,4:PAY],h_all[:,:,:]).then_inc(s_pay,1)
                nc.vector.memset(seg_row[:,:,0:1],1.0).then_inc(s_segr,1)
                ch.mark(nc.vector.memset(aT[:,:],0.0)); ch.mark(nc.vector.memset(cm[:,1,:],0.0)); ch.mark(nc.vector.memset(cm[:,0,:],NEG))
                ch.mark(nc.vector.memset(res[:,:,0,:],0.0)); ch.sync()
                ch(nc.vector.memset(res[:,:,0,0:4],NEG))
                end=n_end(dve)
                sc_=Chain(dve,s_c,2*SCK)
                with dve.Fori(0,NCH//2) as it:
                    sc_.body(it)
                    for q in range(2):
                        c=it*2+q
                        sc_.n=q*SCK
                        Dq=D[:,q]; Gq=G[:,q]; R=res[:,q]; Rh=R.rearrange("p j c -> p c j")
                        with dve.If(on(c,end)):
                            dve.wait_ge(s_D[q],it*16+16)
                            f=Dq[:,:,0]
                            sc_.mark(nc.vector.tensor_scalar(ns[:,:],f,-1.0,1.0,ALU.mult,ALU.add))
                            sc_.mark(nc.vector.tensor_scalar(ng[:,:],f,NEG,None,ALU.mult))
                            sc_(nc.vector.reduce_max(rowe[:,4:5],f,AX.X))
                            for h in range(4):
                                sc_.mark(nc.vector.tensor_tensor_scan(out=ad[:,h,:],data0=ns[:,:],data1=Dq[:,:,1+h],initial=0.0,op0=ALU.mult,op1=ALU.add))
                            sc_.mark(nc.vector.tensor_copy(rowe[:,5:8],rowe[:,4:5].to_broadcast([P,3])))
                            sc_.mark(nc.vector.tensor_copy(aT[:,0:1],aT[:,P:P+1]))
                            sc_.sync()
                            nc.vector.tensor_copy(rowe[:,0:4],ad[:,:,ROW-1]).then_inc(s_a1,1)
                            dve.wait_ge(s_a2,c+1)
                            sc_.mark(nc.vector.tensor_copy(aTv[:,0,:],bank[4][0:4,0,:]))
                            sc_(nc.vector.tensor_scalar(aTv[:,1,:],bank[4][0:4,1,:],-1.0,1.0,ALU.mult,ALU.add))
                            nc.vector.tensor_tensor_scan(out=aT[:,1:P+1],data0=aTv[:,1,:],data1=aTv[:,0,:],initial=aT[:,0:1],op0=ALU.mult,op1=ALU.add).then_inc(s_a3,1)
                            dve.wait_ge(s_a4,c+1)
                            sc_(nc.vector.tensor_copy(adin[:,:],bank[5][:,0,0:4]))
                            for h in range(4):
                                sc_.mark(nc.vector.tensor_tensor_scan(out=ad[:,h,:],data0=ns[:,:],data1=Dq[:,:,1+h],initial=adin[:,h:h+1],op0=ALU.mult,op1=ALU.add))
                            sc_.sync()
                            dve.wait_ge(s_rd[q],it*16)
                            dve.wait_ge(s_G[q],it*16*ROW+16*ROW)
                            sc_(nc.vector.tensor_tensor(e[:,:,:],Gq[:,:,0:4].rearrange("p j h -> p h j"),ad[:,:,:],ALU.add))
                            sc_(nc.vector.scalar_tensor_tensor(e[:,:,:],e[:,:,:],0.2,e[:,:,:],ALU.mult,ALU.max))
                            for h in range(4):
                                sc_.mark(nc.vector.tensor_tensor_scan(out=R[:,1:ROW+1,h],data0=ng[:,:],data1=e[:,h,:],initial=NEG,op0=ALU.add,op1=ALU.max))
                            sc_.sync()
                            sc_.mark(nc.vector.tensor_tensor(ex[:,0],Rh[:,0:4,0:ROW],ng[:,:].unsqueeze(1).to_broadcast([P,4,ROW]),ALU.add))
                            sc_.mark(nc.vector.tensor_tensor(ex[:,1],e[:,:,:],Rh[:,0:4,1:ROW+1],ALU.subtract))
                            sc_.sync()
                            nc.vector.tensor_tensor(ex[:,0],ex[:,0],Rh[:,0:4,1:ROW+1],ALU.subtract).then_inc(s_e,1)
                            dve.wait_ge(s_ex,c+1)
                            sc_(nc.vector.tensor_tensor(nm[:,:,:].rearrange("p (h k) j -> p h k j",h=4),ex[:,1].unsqueeze(2).to_broadcast([P,4,4,ROW]),
                                Gq[:,:,4:PAY].rearrange("p j (h k) -> p h k j",h=4),ALU.mult))
                            for h in range(4):
                                sc_.mark(nc.vector.tensor_tensor_scan(out=R[:,1:ROW+1,4+h],data0=ex[:,0,h,:],data1=ex[:,1,h,:],initial=0.0,op0=ALU.mult,op1=ALU.add))
                            for k in range(HF):
                                sc_.mark(nc.vector.tensor_tensor_scan(out=R[:,1:ROW+1,8+k],data0=ex[:,0,k//4,:],data1=nm[:,k,:],initial=0.0,op0=ALU.mult,op1=ALU.add))
                            sc_.sync()
                            dve.sem_inc(s_r,1)
                            dve.sem_inc(s_used,1)
                            last=R[:,ROW,:]
                            sc_.mark(nc.vector.tensor_copy(ms[:,0,0:4],last[:,0:4]))
                            sc_.mark(nc.vector.tensor_copy(ms[:,0,4:PAY].rearrange("p (h k) -> p h k",h=4),last[:,0:4].unsqueeze(2).to_broadcast([P,4,4])))
                            sc_.mark(nc.vector.tensor_copy(ms[:,1,:],last[:,4:RES]))
                            sc_.mark(nc.vector.tensor_copy(cm[:,:,0:1],cm[:,:,P:P+1]))
                            sc_(nc.vector.tensor_copy(ms[:,2,:],rowe[:,4:5].to_broadcast([P,PAY])))
                            dve.sem_inc(s_x,1)
                            dve.wait_ge(s_xt,c+1)
                            sc_.mark(nc.vector.tensor_copy(mT[:,0:2,:],bank[6][0:PAY,0:2,:]))
                            sc_(nc.vector.tensor_scalar(mT[:,2,:],bank[6][0:PAY,2,:],NEG,None,ALU.mult))
                            sc_(nc.vector.tensor_tensor_scan(out=cm[:,0,1:P+1],data0=mT[:,2,:],data1=mT[:,0,:],initial=cm[:,0,0:1],op0=ALU.add,op1=ALU.max))
                            sc_.mark(nc.vector.tensor_tensor(xt[:,0,:],cm[:,0,0:P],mT[:,2,:],ALU.add))
                            sc_(nc.vector.tensor_tensor(xt[:,1,:],mT[:,0,:],cm[:,0,1:P+1],ALU.subtract))
                            nc.vector.tensor_tensor(xt[:,0,:],xt[:,0,:],cm[:,0,1:P+1],ALU.subtract).then_inc(s_x1,1)
                            dve.wait_ge(s_x2,c+1)
                            sc_(nc.vector.tensor_tensor(mT[:,1,:],mT[:,1,:],xt[:,1,:],ALU.mult))
                            nc.vector.tensor_tensor_scan(out=cm[:,1,1:P+1],data0=xt[:,0,:],data1=mT[:,1,:],initial=cm[:,1,0:1],op0=ALU.mult,op1=ALU.add).then_inc(s_cr,1)
                            dve.wait_ge(s_crT,c+1)
                            dve.wait_ge(s_cd[q],it*16)
                            sc_(nc.vector.tensor_copy(carry[:,q,:].rearrange("p (a k) -> p a k",a=2),bank[7][:,0:2,0:PAY]))
                            dve.sem_inc(s_ci,1)
                        assert sc_.n==(q+1)*SCK,sc_.n
                        with dve.If(it*2+q<NGRP):
                            for m in range(4):
                                dve.wait_ge(s_y,c*4+m+5)
                                if m==0: dve.wait_ge(s_yw[q],it*16)
                                nc.vector.tensor_tensor(ysb[:,q,m,:],bank[2+m%2][:,:,:].rearrange("p a b -> p (a b)"),b2[:,:],ALU.add).then_inc(s_ye,1)
                ch.mark(nc.vector.tensor_single_scalar(srow[:,:],sti[:,:],ROWBITS,op=ALU.logical_shift_right))
                ch(nc.vector.tensor_single_scalar(rowi[:,:],eni[:,:],ROWBITS,op=ALU.logical_shift_right))
                dve.sem_inc(s_en,1)
        with ExitStack() as tail:
            lb=lambda n,s,d: tail.enter_context(nc.sbuf_tensor(n,s,d))
            q4=lb("q4",[P,3,HI],f32); mm=lb("mm",[P,HI,EXP],f32); num=lb("num",[P,HI,PAY],f32); tmp=lb("tmp",[P,HI,PAY],f32); pm=lb("pm2",[P,HI,HF],f32)
            abx=lb("abx",[P,HI,8],f32); vv=lb("vv",[P,HI],f32)
            mu=lb("mu",[P,HI],f32); sc=lb("sc",[P,HI,EXP],f32); rk=lb("rk",[P,HI,EXP],f32); cc=lb("cc",[P,HI],f32)
            ysb=lb("ysb2",[P,2,4,EXP*P],f32); acc4=lb("acc4",[P,2,4,P],f32); oT=lb("oT",[P,2,512],f32)
            s_ch=tail.enter_context(nc.semaphore("g_tail_chain"))
            block=tail.enter_context(nc.Block())
            @block.sync
            def _(sp):
                with sp.Fori(0,NGRP//2) as it:
                    for q in range(2):
                        sp.wait_ge(s_yu,it*2+q+1)
                        sp.sem_inc(s_go,1)
                        sp.dma_start(ysb[:,q].rearrange("p m n -> p (m n)"),yv[ds(it*2+q,1),:,:].rearrange("a p n -> (a p) n")).then_inc(s_yl[q],16)
            @block.tensor
            def _(pe):
                with pe.Fori(0,NGRP//2) as it:
                    for q in range(2):
                        c=it*2+q
                        pe.wait_ge(s_acc,c+1)
                        pe.wait_ge(s_oe,c+1)
                        for m in range(4): last=nc.tensor.transpose(bank[q][:,m,:],acc4[:,q,m,:],ident[:,:])
                        last.then_inc(s_o,1)
            @block.scalar
            def _(act):
                act.wait_ge(s_y1,1)
                nc.scalar.activation(abx[:,:,:],abx[:,:,:],ACT.Exp).then_inc(s_y2,1)
                act.wait_ge(s_y1,2)
                nc.scalar.activation(vv[:,:],vv[:,:],ACT.Sqrt).then_inc(s_y2,1)
                act.wait_ge(s_y1,3)
                nc.scalar.activation(gate[:,:,:],gate[:,:,:],ACT.Exp).then_inc(s_y2,1)
                act.sem_inc(s_oe,2)
                with act.Fori(0,NGRP//2) as it:
                    for q in range(2):
                        c=it*2+q
                        act.wait_ge(s_o,c+1)
                        act.wait_ge(s_out[q],it*16)
                        nc.scalar.activation(oT[:,q,:],bank[q][:,:,:].rearrange("p a b -> p (a b)"),ACT.Identity).then_inc(s_oe,1)
                        act.wait_ge(s_oe,c+3)
                        act.dma_start(O['out'].rearrange("b c h w -> c b (h w)")[:,ds(it,1),q*512:(q+1)*512].rearrange("c b n -> c (b n)"),oT[:,q,:]).then_inc(s_out[q],16)
                for q in range(2): act.wait_ge(s_out[q],16*(NGRP//2))
            @block.vector
            def _(dve):
                ch=Chain(dve,s_ch)
                dve.sem_inc(s_yu,2)
                a_,b_,need=(q4[:,i,:] for i in range(3))
                ch.mark(nc.vector.tensor_copy(a_,srow[:,:])); ch(nc.vector.tensor_copy(b_,rowi[:,:]))
                ch(nc.vector.tensor_tensor(need,a_,b_,ALU.is_equal))
                ch(nc.vector.tensor_scalar(need,need,NEG,None,ALU.mult))
                ch(nc.vector.tensor_tensor(tmp[:,:,0:4],rcar[:,:,0:4],need.unsqueeze(2).to_broadcast([P,HI,4]),ALU.add))
                ch(nc.vector.tensor_tensor(mm[:,:,:],tmp[:,:,0:4],rloc[:,:,0:4],ALU.max))
                ch.mark(nc.vector.tensor_tensor(abx[:,:,0:4],rloc[:,:,0:4],mm[:,:,:],ALU.subtract))
                ch(nc.vector.tensor_tensor(abx[:,:,4:8],tmp[:,:,0:4],mm[:,:,:],ALU.subtract))
                dve.sem_inc(s_y1,1); dve.wait_ge(s_y2,1)
                for o,src,dst in ((0,rloc[:,:,4:RES],num),(4,rcar[:,:,PAY:2*PAY],tmp)):
                    ch.mark(nc.vector.tensor_tensor(dst[:,:,0:4],src[:,:,0:4],abx[:,:,o:o+4],ALU.mult))
                    for h in range(4):
                        ch.mark(nc.vector.tensor_tensor(dst[:,:,4+4*h:8+4*h],src[:,:,4+4*h:8+4*h],abx[:,:,o+h:o+h+1].to_broadcast([P,HI,4]),ALU.mult))
                ch.sync()
                ch(nc.vector.tensor_tensor(num[:,:,:],num[:,:,:],tmp[:,:,:],ALU.add))
                ch(nc.vector.tensor_scalar_add(num[:,:,0:4],num[:,:,0:4],1e-16))
                ch(nc.vector.reciprocal(mm[:,:,:],num[:,:,0:4]))
                agg=tmp[:,:,0:HF]
                for h in range(4): ch.mark(nc.vector.tensor_tensor(tmp[:,:,4*h:4*h+4],num[:,:,4+4*h:8+4*h],mm[:,:,h:h+1].to_broadcast([P,HI,4]),ALU.mult))
                ch.sync()
                row=lambda i: cst[:,i:i+1,:].to_broadcast([P,HI,HF])
                ch(nc.vector.tensor_tensor(agg,agg,row(0),ALU.add))
                ch(nc.vector.tensor_reduce(mu[:,:],agg,axis=AX.X,op=ALU.add))
                ch(nc.vector.tensor_scalar(mu[:,:],mu[:,:],1.0/HF,None,ALU.mult))
                ch(nc.vector.tensor_tensor(agg,agg,mu[:,:].unsqueeze(2).to_broadcast([P,HI,HF]),ALU.subtract))
                ch(nc.vector.tensor_tensor(pm[:,:,:],agg,agg,ALU.mult))
                ch(nc.vector.tensor_reduce(vv[:,:],pm[:,:,:],axis=AX.X,op=ALU.add))
                ch(nc.vector.tensor_scalar(vv[:,:],vv[:,:],1.0/HF,1e-5,ALU.mult,ALU.add))
                dve.sem_inc(s_y1,1); dve.wait_ge(s_y2,2)
                ch(nc.vector.reciprocal(vv[:,:],vv[:,:]))
                ch(nc.vector.tensor_tensor(agg,agg,vv[:,:].unsqueeze(2).to_broadcast([P,HI,HF]),ALU.mult))
                ch(nc.vector.tensor_tensor(agg,agg,row(1),ALU.mult))
                ch(nc.vector.tensor_tensor(agg,agg,row(2),ALU.add))
                ch(nc.vector.tensor_reduce(sc[:,:,:],agg.rearrange("p n (h e) -> p n e h",h=4),axis=AX.X,op=ALU.add))
                ch(nc.vector.tensor_scalar(sc[:,:,:],sc[:,:,:],0.25,None,ALU.mult))
                ch(nc.vector.memset(rk[:,:,:],0.0))
                for i in range(EXP):
                    for j in range(i+1,EXP):
                        ch(nc.vector.tensor_tensor(cc[:,:],sc[:,:,j],sc[:,:,i],ALU.is_gt))
                        ch.mark(nc.vector.tensor_tensor(rk[:,:,i],rk[:,:,i],cc[:,:],ALU.add))
                        ch(nc.vector.scalar_tensor_tensor(rk[:,:,j],rk[:,:,j],1.0,cc[:,:],ALU.add,ALU.subtract))
                ch(nc.vector.tensor_reduce(cc[:,:],sc[:,:,:],axis=AX.X,op=ALU.max))
                ch(nc.vector.tensor_tensor(gate[:,:,:],sc[:,:,:],cc[:,:].unsqueeze(2).to_broadcast([P,HI,EXP]),ALU.subtract))
                ch(nc.vector.tensor_scalar(rk[:,:,:],rk[:,:,:],2.0,None,ALU.is_lt))
                dve.sem_inc(s_y1,1); dve.wait_ge(s_y2,3)
                ch(nc.vector.tensor_tensor(gate[:,:,:],gate[:,:,:],rk[:,:,:],ALU.mult))
                ch(nc.vector.tensor_reduce(cc[:,:],gate[:,:,:],axis=AX.X,op=ALU.add))
                ch(nc.vector.reciprocal(cc[:,:],cc[:,:]))
                ch(nc.vector.tensor_tensor(gate[:,:,:],gate[:,:,:],cc[:,:].unsqueeze(2).to_broadcast([P,HI,EXP]),ALU.mult))
                fc=Chain(dve,s_fc,2*4*3)
                with dve.Fori(0,NGRP//2) as it:
                    fc.body(it)
                    for q in range(2):
                        dve.wait_ge(s_yl[q],it*16+16)
                        dve.wait_ge(s_o,it*2+q) if q else dve.wait_ge(s_o,it*2)
                        for m in range(4):
                            tok=(it*2+q)*4+m
                            acc=acc4[:,q,m,:]
                            fc.mark(nc.vector.scalar_tensor_tensor(acc,ysb[:,q,m,0:P],gate[:,ds(tok,1),0:1].rearrange("p a b -> p (a b)"),t_all[:,ds(tok,1),:].rearrange("p a c -> p (a c)"),ALU.mult,ALU.add))
                        for ee in range(1,EXP):
                            fc.sync()
                            for m in range(4):
                                tok=(it*2+q)*4+m
                                acc=acc4[:,q,m,:]
                                ins=nc.vector.scalar_tensor_tensor(acc,ysb[:,q,m,ee*P:(ee+1)*P],gate[:,ds(tok,1),ee:ee+1].rearrange("p a b -> p (a b)"),acc,ALU.mult,ALU.add)
                                if ee<EXP-1: fc.mark(ins)
                        ins.then_inc(s_acc,1)
                        dve.wait_ge(s_acc,it*2+q+1)
                        dve.sem_inc(s_yu,1)
                    fc.end()

C_GCH=20
SCK=57
LKM=17; HKM=40

def program(nc, A, O):
    with ExitStack() as ctx:
        keep = lambda n, s, d: ctx.enter_context(nc.sbuf_tensor(n, s, d))
        dram = lambda n, s, d: nc.dram_tensor(n, s, d, kind="Internal").ap()
        srclist = dram("sorted_sources", [NPOS, 1], i32)
        seg = dram("segment_starts", [NPOS, 5], f32)
        pay_d = dram("node_payload", [NODES, PAY], f32)
        res_d = dram("running_softmax", [NPOS, RES], f32)
        car_d = dram("carried", [NCH * P, 2 * PAY], f32)
        y_d = dram("expert_outputs", [NGRP * P, 4 * EXP * P], f32)
        table = dram("patches", [B * DG * TROWS, P], f32)
        ident = keep("ident", [P, P], f32)
        start_f = keep("start_f", [P, HI], f32)
        end_f = keep("end_f", [P, HI], f32)
        t_all = keep("t_all", [P, B * NT, C], f32)
        with ExitStack() as edges:
            comp = edges.enter_context(nc.sbuf_tensor("kept_edges", [P, 4, 4, C_NCH * E_UNIT], bf16))
            lim = edges.enter_context(nc.sbuf_tensor("iterations", [P, 1], i32))
            compact_phase(nc, A, srclist, seg, res_d, car_d, comp, lim, ident)
            rank_phase(nc, srclist, comp, lim, start_f, end_f, ident)
        with ExitStack() as images:
            hold = lambda n, s, d: images.enter_context(nc.sbuf_tensor(n, s, d))
            x_all = hold("x_all", [P, B, HW], f32)
            idx_all = hold("idx_all", [P, (B * NT + 1) * 36], u32)
            w4_all = hold("w4_all", [P, B * 1152], f32)
            wdT = hold("wdT", [P, TAPS, P], f32)
            conv_phase(nc, A, table, x_all, idx_all, w4_all, wdT, ident)
            mix_phase(nc, A, table, x_all, t_all, idx_all, w4_all, wdT, ident)
        gat_phase(nc, A, O, t_all, start_f, end_f, srclist, seg, pay_d, res_d, car_d, y_d, ident)


def kernel(**inputs):
    import numpy as np
    import concourse.bacc as bacc
    from concourse.bass_utils import run_bass_kernel_spmd

    nc = bacc.Bacc("TRN2", target_bir_lowering=False, num_devices=1)
    arrays = {name: np.ascontiguousarray(a) for name, a in inputs.items()}
    A = {name: nc.dram_tensor(name, a.shape, mybir.dt.from_np(a.dtype), kind="ExternalInput").ap()
         for name, a in arrays.items()}
    O = {"out": nc.dram_tensor("out", (B, C, WID, WID), f32, kind="ExternalOutput").ap()}
    program(nc, A, O)
    result = run_bass_kernel_spmd(nc, [arrays], core_ids=[0])
    return result.results[0]["out"]
```

```python
import concourse.bass as bass
from concourse import mybir
from contextlib import ExitStack

ds = bass.ds
f32 = mybir.dt.float32
bf16 = mybir.dt.bfloat16
i32 = mybir.dt.int32
u32 = mybir.dt.uint32
ALU = mybir.AluOpType
ACT = mybir.ActivationFunctionType
AX = mybir.AxisListType

P = 128
B, C, WID = 8, 128, 32
HW = WID * WID
NT = HW // P
DG, TAPS = 4, 9
CG = C // DG
NOFF = 2 * DG * TAPS
PITCH = WID + 2
PADN = 1280
BASE = 2 * PITCH + 2
CORNER = (0, 1, PITCH, PITCH + 1)
FRONT = 40
TROWS = PADN + FRONT
HEADS = 8
NODES = B * HW
HI = NODES // P
M = NODES
E = 524288
EXP, HF = 4, 16
PAY, RES = HF + 4, HF + 8
NPOS = 66 * 8192
PCOLS = NPOS // P
ROW = 64
ROWBITS = ROW.bit_length() - 1
NCH = NPOS // (P * ROW)
NGRP = NODES // 512
NEG = -1e30
E_UNIT, E_CH = 8, 32
LATE = 6
E_NU = E_CH // E_UNIT
C_CH, C_GK = 29, 8
C_GRP = -(-E // P // (C_CH * C_GK))
C_NCH = C_GRP * C_GK
C_GC = C_CH * C_GK
C_COLS = C_NCH * C_CH
C_HALVES = C_NCH * E_UNIT // E_CH // 2

def wait_later(eng,go,i,sem,n):
    eng.sem_inc(go,1)
    with eng.If(i>0):
        eng.wait_ge(sem,n)
        eng.sem_inc(go,1)

class Chain:
    def __init__(self,eng,sem,per=0): self.eng,self.sem,self.per,self.n,self.base=eng,sem,per,0,0
    def body(self,i): self.base=i*self.per; self.n=0
    def end(self): assert self.n==self.per,(self.n,self.per)
    def mark(self,ins): self.n+=1; return ins.then_inc(self.sem,1)
    def sync(self): self.eng.wait_ge(self.sem,self.base+self.n)
    def __call__(self,ins): self.mark(ins); self.sync()

def conv_phase(nc,A,table,x_all,idx_all,w4_all,wdT,ident,srclist,ring):
    with ExitStack() as ctx:
        sb=lambda n,s,d: ctx.enter_context(nc.sbuf_tensor(n,s,d))
        pb=lambda n,s,d: ctx.enter_context(nc.psum_tensor(n,s,d))
        sem=lambda n: ctx.enter_context(nc.semaphore("c_"+n))
        w1n=sb("w1n",[P,C*TAPS],f32); w2n=sb("w2n",[NOFF,C*TAPS],f32); wdn=sb("wdn",[P,C*TAPS],f32)
        w1T=sb("w1T",[P,TAPS,P],f32); w2T=sb("w2T",[P,TAPS,NOFF],f32)
        b1=sb("b1c",[P,1],f32); b2=sb("b2c",[P,NOFF],f32)
        gavg=sb("gavg",[P,P],f32)
        bst=sb("bst",[P,B,2,6],f32); mv=sb("mv",[P,B,2],f32)
        mean=sb("mean",[P,B],f32); rstd=sb("rstd",[P,B],f32); dev=sb("dev",[P,B],f32)
        xpad=sb("xpad",[P,2,PADN],f32); hpad=sb("hpad",[P,2,PADN],f32)
        off=sb("off",[NOFF,2,512],f32)
        Fs=sb("Fs",[P,2,10,P],f32)
        pxi=sb("pxi",[P,NT],i32); pyx=sb("pyx",[P,NT,2],f32); yi=sb("yi",[P,NT],i32); xi=sb("xi",[P,NT],i32)
        kyx=sb("kyx",[P,DG*TAPS,2],f32); kyi=sb("kyi",[P,TAPS],i32); kxi=sb("kxi",[P,TAPS],i32)
        gbase=sb("gbase",[P,DG],i32); gbf=sb("gbf",[P,DG],f32)
        basec=sb("basec",[P,NT,NOFF],f32)
        pos=sb("posyx",[P,NT,NOFF],f32); fli=sb("fli",[P,NT,NOFF],i32); fl=sb("fl",[P,NT,NOFF],f32); gt=sb("gt",[P,NT,NOFF],f32)
        whi=sb("whi",[P,NT,NOFF],f32); wlo=sb("wlo",[P,NT,NOFF],f32)
        ixf=sb("ixf",[P,NT,DG*TAPS],f32)
        tp=[pb(f"tp{i}",[P,4,P],f32) for i in range(3)]
        st_ps=pb("st_ps",[P,B],f32)
        c1=[pb(f"c1_{i}",[P,512],f32) for i in range(2)]
        c2=[pb(f"c2_{i}",[P,4,NOFF],f32) for i in range(2)]
        s_const=sem("const"); s_x=sem("x"); s_w=sem("w"); s_b=sem("b"); s_wt=sem("wt"); s_wt_ev=sem("wt_ev")
        s_mean=sem("mean_in"); s_gm=sem("group_mean"); s_var=sem("var_in"); s_gv=sem("group_var"); s_sq=sem("sqrt")
        s_pad=sem("padded"); s_zero=sem("zeroed"); s_c1=sem("conv1_done"); s_h=sem("hidden_ready"); s_c2=sem("conv2_done")
        ztile=sb("ztile",[P,FRONT*DG],f32); s_edge=sem("table_edges")
        s_off=sem("offsets_out"); s_ot=sem("offsets_transposed")
        s_c2r=sem("conv2_read"); s_F=sem("pixels_transposed"); s_Fe=sem("pixels_ready"); s_T=[sem(f"table_written{i}") for i in range(2)]
        s_ch=sem("dve_chain"); s_lp=sem("dve_loop_chain"); s_xfree=sem("xpad_free"); s_base=sem("base_ready"); s_go=sem("go"); s_pc=sem("pool_chain")
        T5=table.rearrange("(b rg) (j c) -> b rg j c",b=B,j=4)
        sc=Scatter(nc,ctx,"late",srclist,ring)
        block=ctx.enter_context(nc.Block())
        @block.sync
        def _(sp):
            for b in range(B):
                sp.dma_start(x_all[:,b,:],A['x'][b].rearrange("c h w -> c (h w)")).then_inc(s_x,16)
            sp.dma_start(w1n[:,:],A['L0_conv_w1'].rearrange("o c a b -> o (c a b)")).then_inc(s_w,16)
            sp.dma_start(w2n[:,:],A['L0_conv_w2'].rearrange("o c a b -> o (c a b)")).then_inc(s_w,16)
            sp.dma_start(wdn[:,:],A['L0_conv_wd'].rearrange("o c a b -> o (c a b)")).then_inc(s_w,16)
            sp.dma_start(b1[:,:],A['L0_conv_b1'].rearrange("(p a) -> p a",a=1)).then_inc(s_b,16)
            sp.dma_start(b2[:,:],A['L0_conv_b2'].rearrange("(a n) -> a n",a=1).to_broadcast([P,NOFF])).then_inc(s_b,16)
            sp.wait_ge(s_zero,1)
            for b in range(B):
                for r0 in (0,PADN):
                    sp.dma_start(table[(b*TROWS+r0)*DG:(b*TROWS+r0+FRONT)*DG,:].rearrange("r c -> (r c)").rearrange("(p n) -> p n",p=P),ztile[:,:]).then_inc(s_edge,16)
            sp.wait_ge(s_edge,16*2*B)
            with sp.Fori(0,B//2) as it:
                for q in range(2):
                    b=it*2+q
                    sp.wait_ge(s_Fe,3*b+6)
                    for j in range(4):
                        o=FRONT-CORNER[j]
                        sp.dma_start(T5[ds(b,1),o*DG:(o+PADN)*DG,j,:].rearrange("b (p rg) c -> (b p) rg c",p=P),
                                     Fs[:,q].rearrange("p r (g c) -> p (r g) c",g=DG)).then_inc(s_T[q],16)
            for q in range(2): sp.wait_ge(s_T[q],16*4*B//2)
        @block.gpsimd
        def _(pool):
            pc=Chain(pool,s_pc)
            pc.mark(nc.gpsimd.memset(ident[:,:],0.0)); pc.mark(nc.gpsimd.memset(gavg[:,:],0.25))
            pc(nc.gpsimd.iota(pxi[:,:],pattern=[[P,NT]],base=0,channel_multiplier=1))
            nc.gpsimd.iota(kyi[:,:],pattern=[[1,3],[0,3]],base=-1,channel_multiplier=0)
            nc.gpsimd.iota(kxi[:,:],pattern=[[0,3],[1,3]],base=-1,channel_multiplier=0)
            nc.gpsimd.iota(gbase[:,:],pattern=[[1,DG]],base=DG*(BASE+FRONT),channel_multiplier=0).then_inc(s_const,1)
            nc.gpsimd.affine_select(out=ident[:,:],in_=ident[:,:],compare_op=ALU.not_equal,fill=1.0,base=0,pattern=[[-1,P]],channel_multiplier=1)
            pc(nc.gpsimd.affine_select(out=gavg[:,:],in_=gavg[:,:],compare_op=ALU.is_ge,fill=0.0,base=0,pattern=[[-4,32],[0,4]],channel_multiplier=1))
            nc.gpsimd.affine_select(out=gavg[:,:],in_=gavg[:,:],compare_op=ALU.is_ge,fill=0.0,base=3,pattern=[[4,32],[0,4]],channel_multiplier=-1).then_inc(s_const,1)
            with pool.Fori(0,LATE) as i:
                for half in range(2): sc.half(pool,i,half,((i+C_HALVES-LATE)*2+half)*E_CH)
            sc.finish(pool,16*E_CH*LATE)
        def trs():
            for t in range(TAPS): yield w1n[:,t::TAPS],w1T[:,t,:],P
            for t in range(TAPS): yield w2n[:,t::TAPS],w2T[:,t,:],NOFF
            for t in range(TAPS): yield wdn[:,t::TAPS],wdT[:,t,:],P
        @block.tensor
        def _(pe):
            pe.wait_ge(s_const,2); pe.wait_ge(s_w,48)
            for n,(src,dst,m) in enumerate(trs()):
                if n>=3: pe.wait_ge(s_wt_ev,n-2)
                nc.tensor.transpose(tp[n%3][:,0,0:m],src,ident[0:m,0:m]).then_inc(s_wt,1)
            pe.wait_ge(s_mean,1)
            nc.tensor.matmul(st_ps[:,:],gavg[:,:],mean[:,:],start=True,stop=True).then_inc(s_gm,1)
            pe.wait_ge(s_var,1)
            nc.tensor.matmul(st_ps[:,:],gavg[:,:],dev[:,:],start=True,stop=True).then_inc(s_gv,1)
            pe.wait_ge(s_wt_ev,27)
            pe.sem_inc(s_c1,4); pe.sem_inc(s_F,6); pe.sem_inc(s_c2,4); pe.sem_inc(s_ot,2)
            with pe.Fori(0,B//2) as it:
                for q in range(2):
                    b=it*2+q
                    pe.wait_ge(s_pad,b+1)
                    xv=xpad[:,q]
                    for r in range(3):
                        nt=min(4,10-4*r)
                        pe.wait_ge(s_Fe,3*b+r)
                        for k in range(nt):
                            last=nc.tensor.transpose(tp[r][:,k,:],xv[:,4*r+k::PADN//P],ident[:,:])
                        last.then_inc(s_F,1)
                    for h in range(2):
                        pe.wait_ge(s_off,b*2+h+1)
                        for t in range(TAPS):
                            o=BASE+(16*h+t//3-1)*PITCH+t%3-1
                            last=nc.tensor.matmul(c1[h][:,:],w1T[:,t,:],xv[:,o:o+16*PITCH].rearrange("p (r w) -> p r w",w=PITCH)[:,:,0:WID],start=(t==0),stop=(t==TAPS-1))
                        last.then_inc(s_c1,1)
                    hv=hpad[:,q]
                    pe.wait_ge(s_h,b*2+4)
                    for h in range(2):
                        pe.wait_ge(s_off,b*2+h+1)
                        for t in range(TAPS):
                            o=BASE+(16*h+t//3-1)*PITCH+t%3-1
                            last=nc.tensor.matmul(c1[h][0:NOFF,:],w2T[:,t,:],hv[:,o:o+16*PITCH].rearrange("p (r w) -> p r w",w=PITCH)[:,:,0:WID],start=(t==0),stop=(t==TAPS-1))
                        last.then_inc(s_c2,1)
                    for m in range(NT):
                        if m%4==0:
                            pe.wait_ge(s_off,b*2+m//4+3)
                            pe.wait_ge(s_c2r,b*2+m//4+1)
                        last=nc.tensor.transpose(c2[m//4][:,m%4,:],off[0:NOFF,m//4,(m%4)*P:(m%4+1)*P],ident[0:NOFF,0:NOFF])
                        if m%4==3: last.then_inc(s_ot,1)
        @block.scalar
        def _(act):
            for n,(src,dst,m) in enumerate(trs()):
                act.wait_ge(s_wt,n+1)
                nc.scalar.copy(dst,tp[n%3][:,0,0:m]).then_inc(s_wt_ev,1)
            act.wait_ge(s_var,2)
            nc.scalar.activation(rstd[:,:],rstd[:,:],ACT.Sqrt).then_inc(s_sq,1)
            act.sem_inc(s_Fe,3); act.sem_inc(s_h,2); act.sem_inc(s_off,2)
            act.wait_ge(s_b,32); act.wait_ge(s_zero,1)
            with act.Fori(0,B//2) as it:
                for q in range(2):
                    b=it*2+q
                    wait_later(act,s_go,it,s_T[q],it*64)
                    for r in range(3):
                        nt=min(4,10-4*r)
                        act.wait_ge(s_F,b*3+r+7)
                        nc.scalar.activation(Fs[:,q,4*r:4*r+nt,:],tp[r][:,0:nt,:],ACT.Identity).then_inc(s_Fe,1)
                    for h in range(2):
                        act.wait_ge(s_c1,b*2+h+5)
                        act.wait_ge(s_c2,b*2+1)
                        o=BASE+16*h*PITCH
                        nc.scalar.activation(hpad[:,q,o:o+16*PITCH].rearrange("p (r w) -> p r w",w=PITCH)[:,:,0:WID],
                            c1[h][:,:].rearrange("p (r w) -> p r w",w=WID),ACT.Identity,bias=b1[:,0:1]).then_inc(s_h,1)
                    for h in range(2):
                        act.wait_ge(s_c2,b*2+h+5)
                        act.wait_ge(s_ot,b*2+h+1)
                        nc.scalar.activation(off[:,h,:],c1[h][0:NOFF,:],ACT.Identity).then_inc(s_off,1)
        @block.vector
        def _(dve):
            ch=Chain(dve,s_ch)
            nc.vector.memset(xpad[:,:,:],0.0)
            ch.mark(nc.vector.memset(ztile[:,:],0.0))
            ch(nc.vector.memset(hpad[:,:,:],0.0))
            dve.sem_inc(s_zero,1)
            ch.mark(nc.vector.memset(idx_all[:,B*NT*36:],0))
            dve.wait_ge(s_const,2)
            nc.vector.tensor_single_scalar(yi[:,:],pxi[:,:],5,op=ALU.logical_shift_right)
            ch(nc.vector.tensor_single_scalar(xi[:,:],pxi[:,:],31,op=ALU.bitwise_and))
            nc.vector.tensor_copy(pyx[:,:,0],yi[:,:])
            nc.vector.tensor_copy(pyx[:,:,1],xi[:,:])
            nc.vector.tensor_copy(gbf[:,:],gbase[:,:])
            kv=kyx[:,:,:].rearrange("p (g k) two -> p g k two",g=DG)
            nc.vector.tensor_copy(kv[:,:,:,0],kyi[:,:].unsqueeze(1).to_broadcast([P,DG,TAPS]))
            ch(nc.vector.tensor_copy(kv[:,:,:,1],kxi[:,:].unsqueeze(1).to_broadcast([P,DG,TAPS])))
            bv=basec[:,:,:].rearrange("p m (k two) -> p m k two",two=2)
            ch(nc.vector.tensor_tensor(bv,pyx[:,:,:].unsqueeze(2).to_broadcast([P,NT,DG*TAPS,2]),kyx[:,:,:].unsqueeze(1).to_broadcast([P,NT,DG*TAPS,2]),ALU.add))
            dve.wait_ge(s_b,32)
            ch(nc.vector.tensor_tensor(basec[:,:,:],basec[:,:,:],b2[:,:].unsqueeze(1).to_broadcast([P,NT,NOFF]),ALU.add))
            dve.wait_ge(s_x,16*B)
            for b in range(B):
                for h in range(2):
                    last=nc.vector.bn_stats(bst[:,b,h,:],x_all[:,b,h*512:(h+1)*512])
            ch(last)
            for b in range(B): last=nc.vector.bn_aggr(mv[:,b,:],bst[:,b,:,:])
            ch(last)
            nc.vector.tensor_copy(mean[:,:],mv[:,:,0]).then_inc(s_mean,1)
            dve.wait_ge(s_gm,1)
            dve.wait_ge(s_mean,1)
            ch(nc.vector.tensor_copy(mean[:,:],st_ps[:,:]))
            ch(nc.vector.tensor_sub(dev[:,:],mv[:,:,0],mean[:,:]))
            ch(nc.vector.tensor_mul(dev[:,:],dev[:,:],dev[:,:]))
            nc.vector.tensor_add(dev[:,:],dev[:,:],mv[:,:,1]).then_inc(s_var,1)
            dve.wait_ge(s_gv,1)
            nc.vector.tensor_scalar_add(rstd[:,:],st_ps[:,:],1e-5).then_inc(s_var,1)
            dve.wait_ge(s_sq,1)
            ch(nc.vector.reciprocal(rstd[:,:],rstd[:,:]))
            dve.sem_inc(s_c2r,2)
            lc=Chain(dve,s_lp,2*LK)
            with dve.Fori(0,B//2) as it:
                lc.body(it)
                for q in range(2):
                    b=it*2+q
                    def normalize(b,q):
                        nc.vector.tensor_scalar(xpad[:,q,BASE:BASE+WID*PITCH].rearrange("p (r w) -> p r w",w=PITCH)[:,:,0:WID],
                            x_all[:,ds(b,1),:].rearrange("p a (r w) -> p (a r) w",w=WID),mean[:,ds(b,1)],rstd[:,ds(b,1)],ALU.subtract,ALU.mult).then_inc(s_pad,1)
                    normalize(b,q)
                    for m in range(2):
                        dve.wait_ge(s_ot,b*2+m+3)
                        ins=nc.vector.tensor_tensor(pos[:,4*m:4*m+4,:],c2[m][:,:,:],basec[:,4*m:4*m+4,:],ALU.add)
                        lc.mark(ins)
                        if m==1: lc.sync()
                    dve.sem_inc(s_c2r,2)
                    lc(nc.vector.tensor_scalar(pos[:,:,:],pos[:,:,:],-3.0,34.0,ALU.max,ALU.min))
                    lc(nc.vector.tensor_copy(fli[:,:,:],pos[:,:,:]))
                    lc(nc.vector.tensor_copy(fl[:,:,:],fli[:,:,:]))
                    lc(nc.vector.tensor_tensor(gt[:,:,:],fl[:,:,:],pos[:,:,:],ALU.is_gt))
                    lc(nc.vector.tensor_tensor(fl[:,:,:],fl[:,:,:],gt[:,:,:],ALU.subtract))
                    lc(nc.vector.tensor_tensor(whi[:,:,:],pos[:,:,:],fl[:,:,:],ALU.subtract))
                    lc.mark(nc.vector.tensor_scalar(wlo[:,:,:],whi[:,:,:],-1.0,1.0,ALU.mult,ALU.add))
                    lc(nc.vector.tensor_scalar(fl[:,:,:],fl[:,:,:],-2.0,32.0,ALU.max,ALU.min))
                    fv=fl[:,:,:].rearrange("p m (k two) -> p m k two",two=2)
                    lc(nc.vector.scalar_tensor_tensor(ixf[:,:,:],fv[:,:,:,0],float(PITCH),fv[:,:,:,1],ALU.mult,ALU.add))
                    for g in range(DG):
                        lc.mark(nc.vector.tensor_scalar(idx_all[:,ds(b*288,288)].rearrange("p (m k g) -> p m k g",m=NT,k=TAPS)[:,:,:,g],
                            ixf[:,:,g*TAPS:(g+1)*TAPS],float(DG),gbf[:,g:g+1],ALU.mult,ALU.add))
                        for jy,jx in ((0,0),(0,1),(1,0),(1,1)):
                            wy=(wlo,whi)[jy][:,:,:].rearrange("p m (g k two) -> p m g k two",g=DG,two=2)[:,:,g,:,0]
                            wx=(wlo,whi)[jx][:,:,:].rearrange("p m (g k two) -> p m g k two",g=DG,two=2)[:,:,g,:,1]
                            lc.mark(nc.vector.tensor_tensor(w4_all[:,ds(b*1152,1152)].rearrange("p (m k c) -> p m k c",m=NT,k=TAPS)[:,:,:,4*g+2*jy+jx],wy,wx,ALU.mult))
                    lc.sync()
                    lc(nc.vector.tensor_scalar_add(gbf[:,:],gbf[:,:],float(DG*TROWS)))
                lc.end()
LK=32
def compact_phase(nc,A,srclist,seg,res_d,car_d,comp,lim,ident):
    edges=A['L1_ffn_edge_index']
    with ExitStack() as ctx:
        sb=lambda n,s,d: ctx.enter_context(nc.sbuf_tensor(n,s,d))
        pb=lambda n,s,d: ctx.enter_context(nc.psum_tensor(n,s,d))
        sem=lambda n: ctx.enter_context(nc.semaphore("k_"+n))
        io_i=sb("k_iota_i",[P,P],i32); io_b=sb("k_iota_b",[P,P],bf16); before=sb("k_before",[P,P],f32)
        before_b=sb("k_before_b",[P,P],bf16); ones_b=sb("k_ones",[P,P],bf16); zeros=sb("zeros",[P,PCOLS],i32)
        dst=sb("k_dst",[P,C_COLS],i32); src=sb("k_src",[P,C_COLS],i32)
        notfirst=sb("notfirst",[P,C_GC],f32)
        ti=sb("k_ti",[P,4,C_GC],i32); tf=sb("k_tf",[P,C_GC],f32); valid=sb("valid",[P,C_GC],bf16)
        V=sb("edge_values",[P,4,C_COLS],bf16)
        incl=sb("k_incl",[P,C_GC],f32); si=sb("k_si",[P,3,C_GC],i32); slot_lo=sb("slot_lo",[P,C_COLS],bf16); slot_hi=sb("slot_hi",[P,C_COLS],bf16)
        vtot=sb("kept",[P,C_NCH],f32); vm=sb("most_kept",[P,1],f32); vmi=sb("most_kept_i",[P,2],i32)
        OS=sb("slot_onehot",[P,2,C_CH,P],bf16); KH=sb("slot_tile",[P,2,C_CH,8],bf16); R=sb("spread",[P,2,C_CH,4,8],bf16)
        pt=pb("k_prefix",[P,2,C_GC],f32); cb=[pb(f"k_slots{i}",[P,4,8],f32) for i in range(2)]
        s_cst=sem("const"); s_ld=sem("edges_in"); s_z=sem("zeros"); s_cl=sem("cleared"); s_ch=sem("chain"); s_g=sem("group_chain"); s_b=sem("bf16_const")
        s_valid=sem("valid"); s_pt=sem("prefix"); s_sl=sem("prefix_read"); s_kh=sem("tile_onehot"); s_oh=sem("onehots"); s_rp=sem("spread"); s_cm=sem("placed"); s_cv=sem("compacted"); s_lim=sem("lim_ready"); s_go=sem("go"); s_cz=sem("kept_zero")
        mine=(s_cst,s_ld,s_z,s_cl,s_ch,s_g,s_b,s_valid,s_pt,s_sl,s_kh,s_oh,s_rp,s_cm,s_cv,s_lim,s_go,s_cz)
        ctx.callback(lambda: [nc.gpsimd.sem_clear(x) for x in mine])
        block=ctx.enter_context(nc.Block())
        @block.sync
        def _(sp):
            sp.wait_ge(s_z,1)
            for row,t in ((1,dst),(0,src)):
                sp.dma_start(t[:,0:E//P],edges[row].rearrange("(p c) -> p c",p=P)).then_inc(s_ld,16)
            z=zeros[:,:].bitcast(f32)
            sp.dma_start(srclist.rearrange("(p j) one -> p (j one)",p=P),zeros[:,:]).then_inc(s_cl,16)
            sp.dma_start(car_d.rearrange("(p j) k -> p (j k)",p=P),z[:,0:NCH*2*PAY]).then_inc(s_cl,16)
            with sp.Fori(0,5) as k:
                sp.dma_start(seg.rearrange("(p j) c -> p (j c)",p=P)[:,ds(k*PCOLS,PCOLS)],z).then_inc(s_cl,16)
            with sp.Fori(0,RES) as k:
                sp.dma_start(res_d.rearrange("(p j) c -> p (j c)",p=P)[:,ds(k*PCOLS,PCOLS)],z).then_inc(s_cl,16)
            sp.wait_ge(s_cl,16*(7+RES))
        def n_iters(eng):
            eng.wait_ge(s_lim,1)
            return eng.value_load(lim[0:1,0:1],min_val=C_HALVES,max_val=4*C_HALVES)
        def slot_onehots(eng,it,k,c0,c1):
            return eng.tensor_tensor(OS[:,k%2,c0:c1],slot_lo[:,ds(it*C_GC+k*C_CH+c0,c1-c0)].unsqueeze(2).to_broadcast([P,c1-c0,P]),io_b[:,:].unsqueeze(1).to_broadcast([P,c1-c0,P]),ALU.is_equal)
        @block.gpsimd
        def _(pool):
            nc.gpsimd.iota(io_i[:,:],pattern=[[1,P]],base=0,channel_multiplier=0).then_inc(s_cst,1)
            nc.gpsimd.memset(before[:,:],1.0).then_inc(s_cst,1)
            pool.wait_ge(s_cst,2)
            nc.gpsimd.affine_select(out=before[:,:],in_=before[:,:],compare_op=ALU.is_gt,fill=0.0,base=0,pattern=[[1,P]],channel_multiplier=-1).then_inc(s_cst,1)
            nc.gpsimd.memset(comp[:,:,:],0.0).then_inc(s_cz,1)
            iters=n_iters(pool)
            with pool.Fori(0,4) as u, pool.Fori(0,C_GRP) as it, pool.If(u*C_GRP+it<iters):
                for k in range(C_GK):
                    n=(u*C_GRP+it)*C_GK+k; q=k%2
                    pool.wait_ge(s_cm,n+1)
                    pool.wait_ge(s_kh,n+1)
                    nc.gpsimd.tensor_tensor(R[:,q],KH[:,q].unsqueeze(2).to_broadcast([P,C_CH,4,8]),
                        V[:,:,ds(it*C_GC+k*C_CH,C_CH)].rearrange("p v c -> p c v").unsqueeze(3).to_broadcast([P,C_CH,4,8]),ALU.mult).then_inc(s_rp,1)
        @block.tensor
        def _(pe):
            pe.wait_ge(s_b,1)
            pe.sem_inc(s_cm,2)
            with pe.Fori(0,C_GRP) as it:
                pe.wait_ge(s_valid,it+1)
                pe.wait_ge(s_sl,it+1)
                nc.tensor.matmul(pt[:,0,:],before_b[:,:],valid[:,:],start=True,stop=True)
                nc.tensor.matmul(pt[:,1,:],ones_b[:,:],valid[:,:],start=True,stop=True).then_inc(s_pt,1)
            iters=n_iters(pe)
            with pe.Fori(0,4) as u, pe.Fori(0,C_GRP) as it, pe.If(u*C_GRP+it<iters):
                for k in range(C_GK):
                    n=(u*C_GRP+it)*C_GK+k; q=k%2
                    pe.wait_ge(s_oh,n+1)
                    pe.wait_ge(s_rp,n+1)
                    pe.wait_ge(s_cv,n+1)
                    for j in range(C_CH):
                        last=nc.tensor.matmul(cb[q][:,:,:],OS[:,q,j,:],R[:,q,j],start=(j==0),stop=(j==C_CH-1))
                    last.then_inc(s_cm,1)
        @block.scalar
        def _(act):
            act.sem_inc(s_cv,2); act.wait_ge(s_cz,1)
            iters=n_iters(act)
            with act.Fori(0,4) as u, act.Fori(0,C_GRP) as it, act.If(u*C_GRP+it<iters):
                for k in range(C_GK):
                    n=(u*C_GRP+it)*C_GK+k; q=k%2
                    act.wait_ge(s_cm,n+3)
                    nc.scalar.activation(comp[:,:,ds(n*8,8)],cb[q][:,:,:],ACT.Identity).then_inc(s_cv,1)
        @block.vector
        def _(dve):
            ch=Chain(dve,s_ch)
            nc.vector.memset(zeros[:,:],0).then_inc(s_z,1)
            ch.mark(nc.vector.memset(dst[:,E//P:],M)); ch.mark(nc.vector.memset(src[:,E//P:],0))
            ch.mark(nc.vector.memset(ones_b[:,:],1.0)); ch(nc.vector.memset(notfirst[:,:],1.0))
            ch(nc.vector.memset(notfirst[:,::C_CH],0.0))
            dve.wait_ge(s_cst,3)
            ch.mark(nc.vector.tensor_copy(before_b[:,:],before[:,:]))
            ch(nc.vector.tensor_copy(io_b[:,:],io_i[:,:]))
            dve.sem_inc(s_b,1); dve.sem_inc(s_sl,1)
            gv=lambda v: V[:,v,ds(it*C_GC,C_GC)]
            dve.wait_ge(s_ld,32)
            gc=Chain(dve,s_g,C_GCH)
            with dve.Fori(0,C_GRP) as it:
                gc.body(it)
                d=dst[:,ds(it*C_GC,C_GC)]; s_=src[:,ds(it*C_GC,C_GC)]
                gc.mark(nc.vector.tensor_single_scalar(ti[:,0],d,13,op=ALU.logical_shift_right))
                gc.mark(nc.vector.tensor_single_scalar(ti[:,1],d,127,op=ALU.bitwise_and))
                gc.mark(nc.vector.tensor_single_scalar(ti[:,2],d,7,op=ALU.logical_shift_right))
                gc(nc.vector.tensor_scalar_min(ti[:,3],s_,float(M-1)))
                gc.mark(nc.vector.tensor_scalar(tf[:,:],ti[:,0],0.0,None,ALU.is_equal))
                nc.vector.tensor_scalar(valid[:,:],ti[:,0],0.0,None,ALU.is_equal).then_inc(s_valid,1)
                gc.mark(nc.vector.tensor_scalar_add(gv(0),ti[:,1],1.0))
                gc.mark(nc.vector.tensor_copy(gv(1),ti[:,2]))
                gc.mark(nc.vector.tensor_single_scalar(si[:,1],ti[:,3],127,op=ALU.bitwise_and))
                gc(nc.vector.tensor_single_scalar(si[:,2],ti[:,3],7,op=ALU.logical_shift_right))
                gc.mark(nc.vector.tensor_copy(gv(2),si[:,1])); gc.mark(nc.vector.tensor_copy(gv(3),si[:,2]))
                dve.wait_ge(s_pt,it+1)
                gc(nc.vector.tensor_tensor_scan(out=incl[:,:],data0=notfirst[:,:],data1=pt[:,1,:],initial=0.0,op0=ALU.mult,op1=ALU.add))
                gc(nc.vector.tensor_copy(vtot[:,ds(it*C_GK,C_GK)],incl[:,C_CH-1::C_CH]))
                gc(nc.vector.tensor_tensor(incl[:,:],incl[:,:],pt[:,1,:],ALU.subtract))
                gc(nc.vector.tensor_tensor(si[:,0],incl[:,:],pt[:,0,:],ALU.add))
                dve.sem_inc(s_sl,1)
                gc.mark(nc.vector.tensor_single_scalar(si[:,1],si[:,0],127,op=ALU.bitwise_and))
                gc.mark(nc.vector.tensor_single_scalar(si[:,2],si[:,0],7,op=ALU.logical_shift_right))
                gc(nc.vector.tensor_scalar(tf[:,:],tf[:,:],-64.0,64.0,ALU.mult,ALU.add))
                gc.mark(nc.vector.tensor_copy(slot_lo[:,ds(it*C_GC,C_GC)],si[:,1]))
                gc(nc.vector.tensor_tensor(slot_hi[:,ds(it*C_GC,C_GC)],si[:,2],tf[:,:],ALU.add))
                gc.end()
            ch(nc.vector.reduce_max(vm[:,:],vtot[:,:],AX.X))
            ch(nc.vector.tensor_scalar(vm[:,:],vm[:,:],1.0,float(8*P-1),ALU.max,ALU.add))
            ch(nc.vector.tensor_copy(vmi[:,0:1],vm[:,:]))
            ch(nc.vector.tensor_single_scalar(vmi[:,1:2],vmi[:,0:1],10,op=ALU.logical_shift_right))
            ch.mark(nc.vector.tensor_scalar(lim[:,0:1],vmi[:,1:2],float(C_HALVES),None,ALU.mult))
            ch(nc.vector.tensor_scalar(lim[:,1:2],vmi[:,1:2],float(C_HALVES),float(-LATE),ALU.mult,ALU.add))
            dve.sem_inc(s_lim,1)
            iters=n_iters(dve)
            with dve.Fori(0,4) as u, dve.Fori(0,C_GRP) as it, dve.If(u*C_GRP+it<iters):
                for k in range(C_GK):
                    n=(u*C_GRP+it)*C_GK+k; q=k%2
                    dve.wait_ge(s_cm,n+1)
                    nc.vector.tensor_tensor(KH[:,q],slot_hi[:,ds(it*C_GC+k*C_CH,C_CH)].unsqueeze(2).to_broadcast([P,C_CH,8]),io_b[:,ds(u*8,8)].unsqueeze(1).to_broadcast([P,C_CH,8]),ALU.is_equal).then_inc(s_kh,1)
                    slot_onehots(nc.vector,it,k,0,C_CH).then_inc(s_oh,1)

class Scatter:
    def __init__(self,nc,ctx,name,srclist,ring):
        self.nc,self.srclist,self.ring=nc,srclist,ring
        self.pos=ctx.enter_context(nc.sbuf_tensor(name+"_pos",[P,2,E_CH],i32)); self.src=ctx.enter_context(nc.sbuf_tensor(name+"_src",[P,2,E_CH],i32))
        sem=lambda n: ctx.enter_context(nc.semaphore(name+"_"+n))
        self.done=[sem("scattered0"),sem("scattered1")]; self.copied=sem("copied"); self.go=sem("go"); self.sems=self.done+[self.copied,self.go]
    def put(self,pos_ap,src_ap,done):
        self.nc.gpsimd.indirect_dma_start(out=self.srclist,out_offset=bass.IndirectOffsetOnAxis(ap=pos_ap,axis=0),in_=src_ap,in_offset=None,
            bounds_check=NPOS-1,oob_is_err=False).then_inc(done,16)
    def half(self,pool,i,half,slot):
        nc=self.nc
        wait_later(pool,self.go,i,self.done[half],i*(16*E_CH))
        nc.gpsimd.tensor_copy(self.pos[:,half,:],self.ring[:,0,ds(slot,E_CH)]).then_inc(self.copied,1)
        nc.gpsimd.tensor_copy(self.src[:,half,:],self.ring[:,1,ds(slot,E_CH)]).then_inc(self.copied,1)
        pool.wait_ge(self.copied,i*4+half*2+2)
        pool.sem_inc(self.go,1)
        for j in range(E_CH): self.put(self.pos[:,half,j:j+1].bitcast(u32),self.src[:,half,j:j+1],self.done[half])
    def finish(self,pool,n):
        for half in range(2):
            pool.wait_ge(self.done[half],n)
            pool.sem_inc(self.go,1)

def rank_phase(nc,srclist,comp,lim,ring,start_f,end_f,ident):
    ctx=ExitStack()
    with ctx:
        sb=lambda n,s,d: ctx.enter_context(nc.sbuf_tensor(n,s,d))
        pb=lambda n,s,d: ctx.enter_context(nc.psum_tensor(n,s,d))
        sem=lambda n: ctx.enter_context(nc.semaphore("r_"+n))
        iota_i=sb("iota_i",[P,P],i32); iota_b=sb("iota_b",[P,P],bf16); iota1_b=sb("iota1_b",[P,P],bf16)
        ident_b=sb("ident_b",[P,P],bf16); node=sb("node",[P,HI],i32); sti=sb("r_sti",[P,HI],u32)
        before=sb("before",[P,P],f32)
        dropped=sb("dropped",[P,E_CH],f32)
        OL=sb("OL",[P,E_NU,E_UNIT,P],bf16); OH=sb("OH",[P,E_NU,E_UNIT,HI],bf16)
        OLT=sb("OLT",[P,E_NU,2,4,P],f32)
        Gm=sb("Gm",[P,E_NU,2,4,P],bf16)
        snap=sb("snap",[P,E_NU,E_UNIT+1,HI],f32)
        start1=sb("start1",[P,HI],f32); cnt=sb("cnt",[P,HI],f32); incl=sb("incl",[P,HI],f32); rowb=sb("rowb",[P,1],f32)
        prod=sb("prod",[P,E_UNIT,HI],f32); posf=sb("posf",[P,E_CH],f32)
        sc=Scatter(nc,ctx,"rank",srclist,ring)
        D=[pb(f"D{i}",[P,E_UNIT,HI],f32) for i in range(2)]
        OLT16=sb("OLT16",[P,E_NU,2,4,P],bf16); notbefore=sb("notbefore",[P,P],bf16)
        T=[pb(f"T{i}",[P,4,P],bf16) for i in range(2)]
        G=[pb(f"G{i}",[P,4,P],f32) for i in range(2)]
        PP=[pb(f"PP{i}",[P,E_UNIT,HI],f32) for i in range(2)]
        S={n: sem(n) for n in (
            "cst", "node", "self_ready", "self", "pos_ready", "go", "ring_free",
            "t_done", "p_done", "olt_ready", "g_done", "gm_ready", "cst_b", "cnt_used", "zero_r",
            "c_ready", "cnt_done", "rows", "base", "oh_ready", "snap_ready", "d_done", "p_free",
            "dve_chain", "fin", "m_chain", "dropped")}
        def s(n): return S[n]
        def n_iters(eng): return eng.value_load(lim[0:1,0:1],min_val=C_HALVES,max_val=4*C_HALVES)
        def part_of(v,it,half,u=0,n=E_CH): return comp[:,v,ds((it*2+half)*E_CH+u*E_UNIT,n)]
        ctx.callback(lambda: [nc.gpsimd.sem_clear(x) for x in list(S.values())+sc.sems])
        block=ctx.enter_context(nc.Block())
        @block.gpsimd
        def _(pool):
            nc.gpsimd.iota(iota_i[:,:],pattern=[[1,P]],base=0,channel_multiplier=0).then_inc(s("cst"),1)
            nc.gpsimd.memset(before[:,:],1.0).then_inc(s("cst"),1)
            nc.gpsimd.memset(ident[:,:],0.0).then_inc(s("cst"),1)
            pool.wait_ge(s("cst"),3)
            nc.gpsimd.affine_select(out=before[:,:],in_=before[:,:],compare_op=ALU.is_gt,fill=0.0,base=0,pattern=[[1,P]],channel_multiplier=-1).then_inc(s("cst"),1)
            nc.gpsimd.affine_select(out=ident[:,:],in_=ident[:,:],compare_op=ALU.not_equal,fill=1.0,base=0,pattern=[[-1,P]],channel_multiplier=1).then_inc(s("cst"),1)
            nc.gpsimd.iota(node[:,:],pattern=[[P,HI]],base=0,channel_multiplier=1).then_inc(s("node"),1)
            pool.wait_ge(s("self_ready"),1); pool.wait_ge(s("node"),1)
            for i in range(HI): sc.put(sti[:,i:i+1],node[:,i:i+1],s("self"))
            iters=n_iters(pool)
            early=pool.value_load(lim[0:1,1:2],min_val=C_HALVES-LATE,max_val=4*C_HALVES-LATE)
            with pool.Fori(0,4) as u:
                with pool.Fori(0,C_HALVES) as step, pool.If(u*C_HALVES+step<early):
                    it=u*C_HALVES+step
                    for half in range(2):
                        pool.wait_ge(s("pos_ready"), it*2+half+1)
                        pool.sem_inc(s("go"),1)
                        sc.half(pool,it,half,(step*2+half)*E_CH)
                with pool.If((u+1)*C_HALVES<iters):
                    for half in range(2):
                        pool.wait_ge(sc.done[half],(u+1)*(C_HALVES*16*E_CH)); pool.sem_inc(s("go"),1)
                    pool.sem_inc(s("ring_free"),1)
            pool.wait_ge(s("self"),16*HI)
            sc.finish(pool,pool.snap(early*(16*E_CH)))
        @block.scalar
        def _(act):
            iters=n_iters(act)
            def transposed(it,u):
                n=it*2*E_NU+u; m=u%E_NU
                for g in range(2):
                    act.wait_ge(s("t_done"),n*2+g+1)
                    act.wait_ge(s("p_done"),n+1)
                    nc.scalar.activation(OLT16[:,m,g],T[g][:,:,:],ACT.Relu)
                    nc.scalar.activation(OLT[:,m,g],T[g][:,:,:],ACT.Relu).then_inc(s("olt_ready"),1)
                for g in range(2):
                    act.wait_ge(s("g_done"),n*2+g+1)
                    nc.scalar.activation(Gm[:,m,g],G[g][:,:,:],ACT.Relu).then_inc(s("gm_ready"),1)
            transposed(0,0)
            with act.Fori(0,4*C_HALVES) as it, act.If(it<iters):
                for u in range(2*E_NU): transposed(it,u+1)
        @block.tensor
        def _(pe):
            pe.wait_ge(s("cst_b"),1)
            pe.sem_inc(s("cnt_used"),4)
            pe.wait_ge(s("zero_r"),1)
            nc.tensor.matmul(D[0][:,0,:],ident[:,:],start1[:,:],start=True,stop=False,skip_group_check=True)
            iters=n_iters(pe)
            with pe.Fori(0,4*C_HALVES) as it, pe.If(it<iters):
                for u in range(2*E_NU):
                    q=u%E_NU
                    pe.wait_ge(s("c_ready"),it*2*E_NU+u+1)
                    for j in range(E_UNIT):
                        last=nc.tensor.matmul(D[0][:,0,:],OL[:,q,j,:],OH[:,q,j,:],start=False,stop=False,skip_group_check=True)
                    last.then_inc(s("cnt_used"),1)
            nc.tensor.matmul(D[0][:,0,:],ident[:,:],start1[:,:],start=False,stop=True,skip_group_check=True).then_inc(s("cnt_done"),1)
            pe.wait_ge(s("rows"),1)
            nc.tensor.matmul(PP[0][:,0,0:1],before[:,:],incl[:,HI-1:HI],start=True,stop=True).then_inc(s("base"),1)
            pe.sem_inc(s("p_done"),4); pe.sem_inc(s("olt_ready"),2); pe.sem_inc(s("gm_ready"),2)
            def front(it,u):
                n=it*2*E_NU+u; q=u%2; m=u%E_NU
                pe.wait_ge(s("oh_ready"),n+1)
                for g in range(2):
                    pe.wait_ge(s("olt_ready"),n*2+g+1)
                    for j in range(4):
                        last=nc.tensor.transpose(T[g][:,j,:],OL[:,m,4*g+j,:],ident_b[:,:])
                    last.then_inc(s("t_done"),1)
                pe.wait_ge(s("snap_ready"),n)
                for i in range(E_UNIT):
                    last=nc.tensor.matmul(D[q][:,i:E_UNIT,:],OL[:,m,i,:],OH[:,m,i:i+1,:].to_broadcast([P,E_UNIT-i,HI]),start=(i==0),stop=(i==E_UNIT-1))
                last.then_inc(s("d_done"),1)
                for g in range(2):
                    pe.wait_ge(s("olt_ready"),n*2+g+3)
                    pe.wait_ge(s("gm_ready"),n*2+g+1)
                    for j in range(4):
                        nc.tensor.matmul(G[g][:,j,:],OLT16[:,m,g,j,:],OLT16[:,m,g,j,:],start=True,stop=False)
                        last=nc.tensor.matmul(G[g][:,j,:],ident_b[:,:],notbefore[:,:],start=False,stop=True)
                    last.then_inc(s("g_done"),1)
            def back(it,u):
                n=it*2*E_NU+u; q=u%2; m=u%E_NU
                pe.wait_ge(s("snap_ready"),n+2)
                pe.wait_ge(s("p_free"),n+1)
                for g in range(2):
                    pe.wait_ge(s("gm_ready"),n*2+g+3)
                    for j in range(4):
                        t=4*g+j
                        nc.tensor.matmul(PP[q][:,t,:],OLT[:,m,g,j,:],snap[:,m,t,:],start=True,stop=False)
                        last=nc.tensor.matmul(PP[q][:,t,:],Gm[:,m,g,j,:],OH[:,m,t,:],start=False,stop=True)
                last.then_inc(s("p_done"),1)
            front(0,0)
            with pe.Fori(0,4*C_HALVES) as it, pe.If(it<iters):
                for u in range(2*E_NU): front(it,u+1); back(it,u)
        @block.vector
        def _(dve):
            ch=s("dve_chain"); k=[0]
            def link(ins):
                k[0]+=1; ins.then_inc(ch,1); dve.wait_ge(ch,k[0])
            dve.wait_ge(s("cst"),5)
            nc.vector.tensor_copy(iota_b[:,:],iota_i[:,:])
            nc.vector.tensor_scalar_add(iota1_b[:,:],iota_i[:,:],1.0)
            nc.vector.tensor_scalar(notbefore[:,:],before[:,:],1.0,None,ALU.subtract)
            nc.vector.tensor_copy(ident_b[:,:],ident[:,:]).then_inc(s("cst_b"),1)
            nc.vector.memset(start1[:,:],0.0).then_inc(s("zero_r"),1)
            dve.wait_ge(s("zero_r"),1)
            def onehots(it,half,u):
                q=u%E_NU
                nc.vector.tensor_tensor(OL[:,q],part_of(0,it,half,u,E_UNIT).unsqueeze(2).to_broadcast([P,E_UNIT,P]),
                    iota1_b[:,:].unsqueeze(1).to_broadcast([P,E_UNIT,P]),ALU.is_equal)
                return nc.vector.tensor_tensor(OH[:,q],part_of(1,it,half,u,E_UNIT).unsqueeze(2).to_broadcast([P,E_UNIT,HI]),
                    iota_b[:,0:HI].unsqueeze(1).to_broadcast([P,E_UNIT,HI]),ALU.is_equal)
            iters=n_iters(dve)
            with dve.Fori(0,4*C_HALVES) as it, dve.If(it<iters):
                for half in range(2):
                    for u in range(E_NU):
                        n=it*2*E_NU+half*E_NU+u
                        dve.wait_ge(s("cnt_used"),n+1)
                        onehots(it,half,u).then_inc(s("c_ready"),1)
            dve.wait_ge(s("cnt_done"),1)
            link(nc.vector.tensor_scalar_add(cnt[:,:],D[0][:,0,:],1.0))
            nc.vector.tensor_tensor_scan(out=incl[:,:],data0=cnt[:,:],data1=cnt[:,:],initial=0.0,op0=ALU.add,op1=ALU.bypass).then_inc(s("rows"),1)
            dve.wait_ge(s("rows"),1)
            dve.wait_ge(s("base"),1)
            link(nc.vector.tensor_copy(rowb[:,:],PP[0][:,0,0:1]))
            link(nc.vector.tensor_sub(start1[:,:],incl[:,:],cnt[:,:]))
            nc.vector.tensor_scalar(start1[:,:],start1[:,:],rowb[:,0:1],1.0,ALU.add,ALU.add).then_inc(s("fin"),1)
            dve.wait_ge(s("fin"),1)
            link(nc.vector.tensor_scalar_add(start_f[:,:],start1[:,:],-1.0))
            nc.vector.tensor_copy(sti[:,:],start_f[:,:]).then_inc(s("self_ready"),1)
            link(nc.vector.tensor_tensor(end_f[:,:],start_f[:,:],cnt[:,:],ALU.add))
            link(nc.vector.tensor_scalar_add(end_f[:,:],end_f[:,:],-1.0))
            nc.vector.tensor_copy(snap[:,E_NU-1,E_UNIT,:],start1[:,:]).then_inc(s("snap_ready"),1)
            dve.sem_inc(s("ring_free"),1); dve.sem_inc(s("p_free"),2)
            def gen(it,u):
                dve.wait_ge(s("p_done"),it*2*E_NU+u+1)
                onehots(it,0,u).then_inc(s("oh_ready"),1)
            def snapshot(it,u):
                n=it*2*E_NU+u; m=u%E_NU; before_=(u-1)%E_NU
                dve.wait_ge(s("d_done"),n+1)
                dve.wait_ge(s("p_done"),n+1)
                dve.wait_ge(s("snap_ready"),n+1)
                nc.vector.tensor_copy(snap[:,m,0],snap[:,before_,E_UNIT])
                nc.vector.tensor_tensor(snap[:,m,1:E_UNIT+1],D[u%2][:,:,:],snap[:,before_,E_UNIT:E_UNIT+1,:].to_broadcast([P,E_UNIT,HI]),ALU.add).then_inc(s("snap_ready"),1)
            def extract(it,u,sl):
                n=it*2*E_NU+u
                dve.wait_ge(s("p_done"),n+5)
                dve.wait_ge(s("p_free"),n+2)
                sl(nc.vector.tensor_tensor(prod[:,:,:],PP[u%2][:,:,:],OH[:,u%E_NU],ALU.mult))
                nc.vector.tensor_reduce(posf[:,E_UNIT*(u%E_NU):E_UNIT*(u%E_NU+1)],prod[:,:,:],axis=AX.X,op=ALU.add).then_inc(s("p_free"),1)
            gen(0,0); gen(0,1); gen(0,2); snapshot(0,0)
            with dve.Fori(0,4) as pass_, dve.Fori(0,C_HALVES) as step, dve.If(pass_*C_HALVES+step<iters):
                it=pass_*C_HALVES+step
                for half in range(2):
                    c=[0]
                    K=E_NU+1
                    def sl(ins):
                        c[0]+=1; ins.then_inc(s("m_chain"),1); dve.wait_ge(s("m_chain"),it*2*K+half*K+c[0])
                    for u in range(half*E_NU,half*E_NU+E_NU):
                        snapshot(it,u+1)
                        extract(it,u,sl)
                        gen(it,u+3)
                    dve.wait_ge(s("p_free"),(it*2*E_NU+half*E_NU+E_NU)+2)
                    dve.wait_ge(s("ring_free"),pass_+1)
                    slot=ds((step*2+half)*E_CH,E_CH)
                    nc.vector.tensor_scalar(dropped[:,:],part_of(0,it,half),0.0,float(1<<20),ALU.is_equal,ALU.mult).then_inc(s("dropped"),1)
                    dve.wait_ge(s("dropped"),it*2+half+1)
                    sl(nc.vector.tensor_tensor(posf[:,:],posf[:,:],dropped[:,:],ALU.add))
                    nc.vector.tensor_copy(ring[:,0,slot],posf[:,:])
                    nc.vector.scalar_tensor_tensor(ring[:,1,slot],part_of(3,it,half),float(P),part_of(2,it,half),ALU.mult,ALU.add).then_inc(s("pos_ready"),1)
                    dve.wait_ge(s("pos_ready"),it*2+half+1)
                    dve.sem_inc(s("go"),1)

def mix_phase(nc,A,table,x_all,t_all,idx_all,w4_all,wdT,ident):
    with ExitStack() as ctx:
        sb=lambda n,s,d: ctx.enter_context(nc.sbuf_tensor(n,s,d))
        sem=lambda n: ctx.enter_context(nc.semaphore("m_"+n))
        bank=[ctx.enter_context(nc.psum_tensor(f"bank{i}",[P,4,P],f32)) for i in range(8)]
        stage=sb("stage",[P,3,12],u32)
        patch=sb("patch",[P,3,3,DG,4*CG],f32)
        wp=sb("wp",[P,3,4,DG,CG],f32); wpair=sb("wpair",[P,3,2,P],f32); wsum=sb("wsum",[P,3,3,P],f32)
        vT=sb("vT",[P,3,3,P],f32)
        rl=sb("rl",[P,P],f32)
        tn=sb("tn",[P,2,P],f32); st=sb("lnst",[P,NT,6],f32); mv=sb("lnmv",[P,NT,2],f32); rs=sb("lnrs",[P,NT],f32)
        tnT=sb("tnT",[P,HW],f32)
        WqT=sb("WqT",[P,HEADS,P],f32); WkT=sb("WkT",[P,P],f32); WvT=sb("WvT",[P,P],f32); WoT=sb("WoT",[P,NT,P],f32)
        KT=sb("KT",[P,8,P],f32); V=sb("V",[P,8,P],f32); QT=sb("QT",[P,HW],f32)
        pr=sb("pr",[P,2,HW],f32); mx=sb("mx",[P,2],f32); nmx=sb("nmx",[P,2],f32); sm=sb("sm",[P,2],f32); ri=sb("ri",[P,2],f32)
        wos=sb("wos",[P,2,P],f32); GT=sb("GT",[P,HW],f32); Gs=sb("Gs",[P,8,P],f32)
        wnat=sb("wnat",[P,P],f32)
        sm2=sb("sm2",[P,2,2],f32); mx2=sb("mx2",[P,2,2],f32)
        xs=sb("xs",[P,P],f32); wqh=sb("wqh",[P,P],f32)
        s_stage=[sem(f"staged{i}") for i in range(3)]; s_patch=[sem(f"patches{i}") for i in range(3)]
        s_go=sem("go"); s_xs=sem("x_tile"); s_pj=sem("projected"); s_wqh=sem("wq_head")
        s_w=[sem(f"weights{i}") for i in range(2)]; s_wt=sem("wt"); s_wte=sem("wt_out"); s_wp=sem("weighted"); s_v=sem("sampled"); s_ve=sem("sampled_out"); s_conv=sem("conv_done"); s_rl=sem("relu_out")
        s_t=sem("tokens"); s_ch=sem("head_chain"); s_l=sem("norm_chain"); s_d=sem("sample_chain"); s_var=sem("variance"); s_sd=sem("deviation")
        s_tn=sem("normalized"); s_tt=sem("tn_transposed"); s_tte=sem("tnT_ready"); s_kv=sem("kv_done"); s_kve=sem("kv_ready")
        s_q=sem("q_done"); s_qe=sem("q_ready"); s_s=sem("scores"); s_m=sem("max_ready"); s_p=sem("probs"); s_wo=sem("scaled_wo"); s_g=sem("gathered")
        s_ge=sem("GT_ready"); s_gt=sem("G_transposed"); s_gs=sem("G_ready"); s_o=sem("head_out"); s_a=sem("head_added")
        parts=[(A['L1_attn_Wq'][h*P:(h+1)*P,:],WqT[:,h,:]) for h in range(HEADS)]+[(A['L1_attn_Wk'],WkT[:,:]),(A['L1_attn_Wv'],WvT[:,:])]+[(A['L1_attn_Wo'][:,i*P:(i+1)*P],WoT[:,i,:]) for i in range(NT)]
        wbuf=lambda n: (wnat[:,:],xs[:,:])[n%2]
        flat=lambda ap: ap.rearrange("p a b -> p (a b)")
        block=ctx.enter_context(nc.Block())
        @block.sync
        def _(sp):
            for n,(src,_) in enumerate(parts):
                if n>=2: sp.wait_ge(s_wt,n-1)
                sp.dma_start(wbuf(n),src).then_inc(s_w[n%2],16)
        @block.gpsimd
        def _(pool):
            with pool.Fori(0,B*NT) as g:
                for k in range(3):
                    pool.wait_ge(s_stage[k],g+1)
                    pool.sem_inc(s_go,1)
                    for i in range(12):
                        nc.gpsimd.indirect_dma_start(out=patch[:,k,i//DG,i%DG,:],out_offset=None,in_=table,
                            in_offset=bass.IndirectOffsetOnAxis(ap=stage[:,k,i:i+1],axis=0)).then_inc(s_patch[k],16)
        @block.tensor
        def _(pe):
            for n in range(len(parts)):
                pe.wait_ge(s_w[n%2],16*(n//2)+16)
                if n>=4: pe.wait_ge(s_wte,n-3)
                nc.tensor.transpose(bank[n%4][:,0,:],wbuf(n),ident[:,:]).then_inc(s_wt,1)
            pe.wait_ge(s_wte,len(parts))
            pe.sem_inc(s_v,3); pe.sem_inc(s_pj,3); pe.sem_inc(s_tt,2); pe.sem_inc(s_g,2)
            def sample(g,k):
                pe.wait_ge(s_wp,g*3+k+1+1)
                pe.wait_ge(s_ve,g*3+k+1)
                for t in range(3): last=nc.tensor.transpose(bank[6][:,t,:],wsum[:,k,t,:],ident[:,:])
                last.then_inc(s_v,1)
            def project(g,k):
                pe.wait_ge(s_ve,g*3+k+1+1)
                if k==0: pe.wait_ge(s_rl,g+1)
                for t in range(3):
                    last=nc.tensor.matmul(bank[7][:,0,:],vT[:,k,t,:],wdT[:,3*k+t,:],start=(k+t==0),stop=(k==2 and t==2))
                last.then_inc(s_pj,1)
                if k==2:
                    pe.wait_ge(s_xs,g+1)
                    pe.wait_ge(s_t,g+1)
                    nc.tensor.transpose(bank[7][:,1,:],xs[:,:],ident[:,:]).then_inc(s_conv,1)
            def queries(hh):
                pe.wait_ge(s_wqh,hh+1)
                pe.wait_ge(s_p,hh*NT+7)
                for i in range(2):
                    nc.tensor.matmul(bank[i][:,:,:],wqh[:,:],tnT[:,i*512:(i+1)*512],start=True,stop=True).then_inc(s_q,1)
            def scores(hh,i):
                if i==0: pe.wait_ge(s_qe,hh*2+2)
                elif i==1: pe.wait_ge(s_gs,hh*2+1)
                else: pe.wait_ge(s_p,hh*NT+i+7)
                for k in range(2):
                    last=nc.tensor.matmul(bank[2*(i%2)+k][:,:,:],QT[:,i*P:(i+1)*P],KT[:,4*k:4*k+4,:],start=True,stop=True)
                last.then_inc(s_s,1)
            def gather(hh,i):
                pe.wait_ge(s_p,hh*NT+i+9); pe.wait_ge(s_wo,hh*NT+i+1)
                for k in range(2):
                    last=nc.tensor.matmul(bank[4+k][:,:,:],wos[:,i%2,:],pr[:,i%2,k*512:(k+1)*512],start=(i==0),stop=(i==NT-1))
                last.then_inc(s_g,1)
            def head(b,h,sampling,more):
                hh=b*HEADS+h; g=hh+HEADS
                scores(hh,1)
                for i in range(NT):
                    if i+2<NT: scores(hh,i+2)
                    if i==6 and more: queries(hh+1)
                    gather(hh,i)
                    if sampling and i in (1,3,5): sample(g,i//2)
                    if sampling and i in (2,4,6): project(g,i//2-1)
                if more: scores(hh+1,0)
                for k in range(2):
                    pe.wait_ge(s_ge,hh*2+k+1)
                    for j in range(4):
                        last=nc.tensor.transpose(bank[2+k][:,j,:],GT[:,(4*k+j)*P:(4*k+j+1)*P],ident[:,:])
                    last.then_inc(s_gt,1)
                for j in range(8):
                    if j==0: pe.wait_ge(s_a,hh+1)
                    if j%4==0: pe.wait_ge(s_gs,hh*2+j//4+1+1)
                    last=nc.tensor.matmul(bank[6][:,3,:],V[:,j,:],Gs[:,j,:],start=(j==0),stop=(j==7))
                last.then_inc(s_o,1)
            def image(b,sampling):
                for m in range(NT):
                    pe.wait_ge(s_tn,b*NT+m+1)
                    pe.wait_ge(s_tte,b*NT+m+1)
                    nc.tensor.transpose(bank[m%2][:,0,:],tn[:,m%2,:],ident[:,:]).then_inc(s_tt,1)
                pe.wait_ge(s_tte,b*NT+NT+2)
                for n,(w,h) in enumerate(((WkT,0),(WkT,1),(WvT,0),(WvT,1))):
                    nc.tensor.matmul(bank[2+n][:,:,:],w[:,:],tnT[:,h*512:(h+1)*512],start=True,stop=True).then_inc(s_kv,1)
                queries(b*HEADS)
                pe.wait_ge(s_kve,b*4+4)
                scores(b*HEADS,0)
                with pe.Fori(0,HEADS-1) as h: head(b,h,sampling,True)
                head(b,HEADS-1,sampling,False)
            with pe.Fori(0,NT) as g:
                for k in range(3): sample(g,k); project(g,k)
            with pe.Fori(0,B-1) as b: image(b,True)
            image(B-1,False)
        @block.scalar
        def _(act):
            for n,(_,dst) in enumerate(parts):
                act.wait_ge(s_wt,n+1)
                nc.scalar.activation(dst,bank[n%4][:,0,:],ACT.Identity).then_inc(s_wte,1)
            act.sem_inc(s_tte,2); act.sem_inc(s_p,8)
            nc.scalar.activation(wqh[:,:],WqT[:,0,:],ACT.Identity).then_inc(s_wqh,1)
            def samples_out(g,k):
                act.wait_ge(s_v,g*3+k+4)
                act.wait_ge(s_pj,g*3+k+1)
                nc.scalar.activation(vT[:,k],bank[6][:,0:3,:],ACT.Identity).then_inc(s_ve,1)
            def relu(g):
                act.wait_ge(s_conv,g+1+1)
                act.wait_ge(s_t,g+1)
                nc.scalar.activation(rl[:,:],bank[7][:,0,:],ACT.Relu).then_inc(s_rl,1)
            def queries_out(hh):
                for i in range(2):
                    act.wait_ge(s_q,hh*2+i+1)
                    nc.scalar.activation(QT[:,i*512:(i+1)*512],flat(bank[i][:,:,:]),ACT.Identity).then_inc(s_qe,1)
            def head(b,h,sampling,more):
                hh=b*HEADS+h; g=hh+HEADS
                for i in range(NT):
                    q=i%2
                    act.wait_ge(s_m,hh*NT+i+1)
                    act.wait_ge(s_g,hh*NT+i+1)
                    for k in range(2):
                        last=nc.scalar.activation(pr[:,q,k*512:(k+1)*512],flat(bank[2*q+k][:,:,:]),ACT.Exp,bias=nmx[:,q:q+1],scale=0.25,accum_out=sm2[:,q,k:k+1])
                    last.then_inc(s_p,1)
                    if sampling and i in (2,4,6): samples_out(g,i//2-1)
                    if i==1:
                        act.wait_ge(s_q,hh*2+2)
                        nc.scalar.activation(wqh[:,:],WqT[:,ds(h+1,1),:].rearrange("p a c -> p (a c)") if more else WqT[:,0,:],ACT.Identity).then_inc(s_wqh,1)
                if more: queries_out(hh+1)
                if sampling: relu(g)
                for k in range(2):
                    act.wait_ge(s_g,hh*NT+NT+2)
                    nc.scalar.activation(GT[:,k*512:(k+1)*512],flat(bank[4+k][:,:,:]),ACT.Identity).then_inc(s_ge,1)
                act.wait_ge(s_o,hh+1)
                for k in range(2):
                    act.wait_ge(s_gt,hh*2+k+1)
                    nc.scalar.activation(Gs[:,4*k:4*k+4,:],bank[2+k][:,:,:],ACT.Identity).then_inc(s_gs,1)
            def image(b,sampling):
                act.wait_ge(s_var,b+1)
                nc.scalar.activation(rs[:,:],rs[:,:],ACT.Sqrt).then_inc(s_sd,1)
                for m in range(NT):
                    act.wait_ge(s_tt,b*NT+m+3)
                    nc.scalar.activation(tnT[:,m*P:(m+1)*P],bank[m%2][:,0,:],ACT.Identity).then_inc(s_tte,1)
                for n in range(4):
                    act.wait_ge(s_kv,b*4+n+1)
                    if n<2:
                        nc.scalar.activation(KT[:,:,n*64:(n+1)*64],flat(bank[2+n][:,:,:]).rearrange("p (o j) -> p j o",j=8),ACT.Identity).then_inc(s_kve,1)
                    else:
                        nc.scalar.activation(V[:,4*(n-2):4*(n-2)+4,:],bank[2+n][:,:,:],ACT.Identity).then_inc(s_kve,1)
                queries_out(b*HEADS)
                with act.Fori(0,HEADS-1) as h: head(b,h,sampling,True)
                head(b,HEADS-1,sampling,False)
            with act.Fori(0,NT) as g:
                for k in range(3): samples_out(g,k)
                relu(g)
            with act.Fori(0,B-1) as b: image(b,True)
            image(B-1,False)
        @block.vector
        def _(dve):
            for x in (s_ve,s_rl,s_t,s_conv,s_wp,s_gs,s_a,s_o): dve.sem_inc(x,1)
            for k in range(3):
                nc.vector.tensor_copy(stage[:,k,:],idx_all[:,12*k:12*k+12]).then_inc(s_stage[k],1)
            lc=Chain(dve,s_l,LKM); hc=Chain(dve,s_ch,HKM); dc=Chain(dve,s_d,6)
            dve.wait_ge(s_wt,len(parts))
            def x_tile(b,m,g):
                dve.wait_ge(s_conv,g+1)
                nc.vector.tensor_copy(xs[:,:],x_all[:,ds(b,1),ds(m*P,P)].rearrange("p a n -> p (a n)")).then_inc(s_xs,1)
            def weigh(g,k):
                dc.base=g*6; dc.n=2*k
                dve.wait_ge(s_patch[k],g*192+192)
                dve.wait_ge(s_wp,g*3+k+1)
                dve.wait_ge(s_v,g*3+k+1)
                for t in range(3):
                    last=nc.vector.tensor_tensor(wp[:,t].rearrange("p j g c -> p g j c"),
                        patch[:,k,t].rearrange("p g (j c) -> p g j c",j=4),
                        w4_all[:,ds(g*144+(3*k+t)*16,16)].rearrange("p (g j) -> p g j",j=4).unsqueeze(3).to_broadcast([P,DG,4,CG]),ALU.mult)
                dc(last)
                nc.vector.tensor_copy(stage[:,k,:],idx_all[:,ds((g+1)*36+12*k,12)]).then_inc(s_stage[k],1)
                w=wp[:,:,:,:,:].rearrange("p t j g c -> p t j (g c)")
                dc(nc.vector.tensor_tensor(wpair[:,:,:,:],w[:,:,0:2],w[:,:,2:4],ALU.add))
                nc.vector.tensor_tensor(wsum[:,k],wpair[:,:,0],wpair[:,:,1],ALU.add).then_inc(s_wp,1)
            def add_conv(g):
                dve.wait_ge(s_rl,g+1+1)
                nc.vector.tensor_tensor(t_all[:,ds(g,1),:].rearrange("p a c -> p (a c)"),bank[7][:,1,:],rl[:,:],ALU.add).then_inc(s_t,1)
            def maximum(hh,i):
                q=i%2; hc.base=hh*HKM
                if i==0: hc.n=0
                dve.wait_ge(s_s,hh*NT+i+1)
                hc.mark(nc.vector.reduce_max(mx2[:,q,0:1],flat(bank[2*q][:,:,:]),AX.X))
                hc(nc.vector.reduce_max(mx2[:,q,1:2],flat(bank[2*q+1][:,:,:]),AX.X))
                hc(nc.vector.tensor_tensor(mx[:,q:q+1],mx2[:,q,0:1],mx2[:,q,1:2],ALU.max))
                nc.vector.tensor_scalar_mul(nmx[:,q:q+1],mx[:,q:q+1],-0.25).then_inc(s_m,1)
            def scale_wo(hh,i):
                q=i%2
                dve.wait_ge(s_p,hh*NT+i+9)
                hc(nc.vector.tensor_tensor(sm[:,q:q+1],sm2[:,q,0:1],sm2[:,q,1:2],ALU.add))
                hc(nc.vector.reciprocal(ri[:,q:q+1],sm[:,q:q+1]))
                nc.vector.tensor_scalar(wos[:,q,:],WoT[:,i,:],ri[:,q:q+1],None,ALU.mult).then_inc(s_wo,1)
            def head(b,h,sampling,more):
                hh=b*HEADS+h; g=hh+HEADS
                hc.base=hh*HKM; hc.n=3
                for i in range(NT):
                    if i+1<NT: maximum(hh,i+1)
                    scale_wo(hh,i)
                    if sampling and i in (0,2,4): weigh(g,i//2)
                    if sampling and i==1: x_tile(b+1,h,g)
                hc.end()
                if more: maximum(hh+1,0)
                if sampling: add_conv(g)
                dve.wait_ge(s_o,hh+1+1)
                nc.vector.tensor_tensor(t_all[:,ds(hh,1),:].rearrange("p a c -> p (a c)"),bank[6][:,3,:],t_all[:,ds(hh,1),:].rearrange("p a c -> p (a c)"),ALU.add).then_inc(s_a,1)
            def image(b,sampling):
                dve.wait_ge(s_t,b*NT+NT+1)
                lc.body(b)
                for m in range(NT):
                    lc.mark(nc.vector.bn_stats(st[:,m,:],t_all[:,ds(b*NT+m,1),:].rearrange("p a c -> p (a c)")))
                lc.sync()
                dve.sem_inc(s_go,1)
                for m in range(NT): lc.mark(nc.vector.bn_aggr(mv[:,m,:],st[:,m,:]))
                lc.sync()
                nc.vector.tensor_scalar_add(rs[:,:],mv[:,:,1],1e-5).then_inc(s_var,1)
                dve.wait_ge(s_sd,b+1)
                lc(nc.vector.reciprocal(rs[:,:],rs[:,:]))
                for m in range(NT):
                    dve.wait_ge(s_tt,b*NT+m+1)
                    nc.vector.tensor_scalar(tn[:,m%2,:],t_all[:,ds(b*NT+m,1),:].rearrange("p a c -> p (a c)"),mv[:,m,0:1],rs[:,m:m+1],ALU.subtract,ALU.mult).then_inc(s_tn,1)
                lc.end()
                maximum(b*HEADS,0)
                with dve.Fori(0,HEADS-1) as h: head(b,h,sampling,True)
                head(b,HEADS-1,sampling,False)
            with dve.Fori(0,NT) as g:
                x_tile(0,g,g)
                for k in range(3): weigh(g,k)
                add_conv(g)
            with dve.Fori(0,B-1) as b: image(b,True)
            image(B-1,False)
LKM=17; HKM=8*5
def gat_phase(nc,A,O,t_all,start_f,end_f,srclist,seg,pay_d,res_d,car_d,y_d,ident):
    with ExitStack() as ctx:
        sb=lambda n,s,d: ctx.enter_context(nc.sbuf_tensor(n,s,d))
        sem=lambda n: ctx.enter_context(nc.semaphore("g_"+n))
        bank=[ctx.enter_context(nc.psum_tensor(f"gb{i}",[P,4,P],f32)) for i in range(8)]
        W=sb("Wg",[P,HF],f32); att=sb("att",[P,2,HF],f32); cst=sb("lncst",[P,3,HF],f32)
        b1=sb("b1f",[P,EXP,2],f32); b2=sb("b2f",[P,EXP*P],f32)
        W1=sb("W1s",[P,EXP,2*P],f32); W2=sb("W2s",[P,EXP,2,P],f32)
        st=sb("st2",[P,NT,6],f32); mv=sb("mv2",[P,NT,2],f32); rs=sb("rs2",[P,NT],f32)
        tn=sb("tn_2",[P,2,P],f32); tT=sb("tT",[P,2,P],f32)
        sti=sb("sti",[P,HI],u32); eni=sb("eni",[P,HI],u32); rowi=sb("rowi",[P,HI],u32); srow=sb("srow",[P,HI],u32)
        ends=sb("node_ends",[P,1],f32)
        carry=sb("carry",[P,2,2*PAY],f32); gate=sb("gate",[P,HI,EXP],f32)
        rloc=sb("rloc",[P,HI,RES],f32); rcar=sb("rcar",[P,HI,2*PAY],f32)
        s_w=sem("weights"); s_ch=sem("dve_chain"); s_l=sem("dve_ln"); s_var=sem("var"); s_sd=sem("sd"); s_tn=sem("tn"); s_tt=sem("tt"); s_te=sem("tT"); s_h=sem("h"); s_he=sem("h_out")
        s_pay=sem("pay_ready"); s_payd=sem("pay_written"); s_segr=sem("seg_ready"); s_segd=sem("seg_written"); s_eni=sem("ends_ready")
        s_in=[sem(f"chunk_in{i}") for i in range(2)]; s_D=[sem(f"seg_in{i}") for i in range(2)]; s_G=[sem(f"payload{i}") for i in range(2)]; s_used=sem("chunk_used"); s_go=sem("go")
        s_c=sem("dve_scan_chain"); s_e=sem("exp_in"); s_ex=sem("exp_out"); s_r=sem("res_ready"); s_rd=[sem(f"res_written{i}") for i in range(2)]
        s_a1=sem("row_ends"); s_a2=sem("row_ends_T"); s_a3=sem("row_starts_T"); s_a4=sem("row_starts")
        s_x=sem("rows"); s_xt=sem("rows_T"); s_x1=sem("x1"); s_x2=sem("x2"); s_cr=sem("carry"); s_crT=sem("carryT"); s_cd=[sem(f"carry_written{i}") for i in range(2)]; s_ci=sem("carry_sb")
        s_en=sem("ends"); s_gr=sem("ends_in"); s_y1=sem("y1"); s_y2=sem("y2"); s_f=sem("ffn_h"); s_fe=sem("ffn_he"); s_y=sem("ffn_y"); s_ye=sem("ffn_ye"); s_yw=[sem(f"y_written{i}") for i in range(2)]
        s_yl=[sem(f"y_loaded{i}") for i in range(2)]; s_yu=sem("y_used"); s_acc=sem("summed"); s_o=sem("oT"); s_oe=sem("oTe"); s_out=[sem(f"out{i}") for i in range(2)]; s_fc=sem("sum_chain")
        resv=res_d.rearrange("(c p j) k -> c p (j k)",p=P,j=ROW); segv=seg.rearrange("(c p j) k -> c p (j k)",p=P,j=ROW); srcv=srclist.rearrange("(c p j) one -> c p (j one)",p=P,j=ROW)
        carv=car_d.rearrange("(c p) k -> c p k",p=P); yv=y_d.rearrange("(g p) n -> g p n",p=P)
        def n_end(eng):
            eng.wait_ge(s_eni,1)
            return eng.value_load(eni[P-1:P,HI-1:HI],min_val=NODES-1,max_val=NPOS-1)
        def group(c):
            return nc.s_assert_within(c,0,NGRP-1,skip_runtime_bounds_check_because="it stands where the chunk is known to be under NGRP")
        def on(c,end): return c*(P*ROW)<=end
        with ExitStack() as loop:
            lb=lambda n,s,d: loop.enter_context(nc.sbuf_tensor(n,s,d))
            tnT=lb("tn2T",[P,NODES],f32); hT=lb("hT",[P,EXP,2,512],f32); ysb=lb("ysb",[P,2,4,EXP*P],f32)
            h_all=lb("h_all",[P,HI,HF],f32); pm=lb("pm",[P,HI,HF],f32)
            pay=lb("pay",[P,HI,PAY],f32); seg_row=lb("seg_row",[P,HI,5],f32)
            idx=lb("g_idx",[P,2,ROW],i32); G=lb("G_in",[P,2,ROW,PAY],f32); D=lb("D_in",[P,2,ROW,5],f32)
            ns=lb("ns",[P,ROW],f32); ng=lb("ng",[P,ROW],f32); ad=lb("ad",[P,4,ROW],f32); rowe=lb("rowe",[P,8],f32); adin=lb("adin",[P,4],f32)
            aT=lb("aT",[4,P+1],f32); aTv=lb("aTv",[4,2,P],f32)
            e=lb("e",[P,4,ROW],f32); ex=lb("ex",[P,2,4,ROW],f32); nm=lb("nm",[P,HF,ROW],f32)
            res=lb("res",[P,2,ROW+1,RES],f32)
            ms=lb("row_sums",[P,3,PAY],f32); mT=lb("mT",[PAY,3,P],f32); cm=lb("cm",[PAY,2,P+1],f32); xt=lb("xt",[PAY,2,P],f32)
            block=loop.enter_context(nc.Block())
            @block.sync
            def _(sp):
                bc=lambda ap,n: ap.to_broadcast([P,n])
                sp.dma_start(W[:,:],A['L1_ffn_W_gat']).then_inc(s_w,16)
                sp.dma_start(att[:,0,:],bc(A['L1_ffn_att_src'].rearrange("(a h) k -> a (h k)",a=1),HF)).then_inc(s_w,16)
                sp.dma_start(att[:,1,:],bc(A['L1_ffn_att_dst'].rearrange("(a h) k -> a (h k)",a=1),HF)).then_inc(s_w,16)
                for i,n in enumerate(('b_gat','ln_gamma','ln_beta')):
                    sp.dma_start(cst[:,i,:],bc(A['L1_ffn_'+n].rearrange("(a k) -> a k",a=1),HF)).then_inc(s_w,16)
                sp.dma_start(b1[:,:,:],A['L1_ffn_b1'].rearrange("e (f p) -> p e f",p=P),allow_slow_non_contiguous=True).then_inc(s_w,16)
                sp.dma_start(b2[:,:],bc(A['L1_ffn_b2'].rearrange("(a e) c -> a (e c)",a=1),EXP*P)).then_inc(s_w,16)
                sp.dma_start(W1[:,:,:],A['L1_ffn_W1'].rearrange("e c f -> c e f")).then_inc(s_w,16)
                for ee in range(EXP): sp.dma_start(W2[:,ee],A['L1_ffn_W2'][ee].rearrange("(f p) c -> p f c",p=P)).then_inc(s_w,16)
                end=n_end(sp)
                sp.wait_ge(s_pay,1)
                sp.dma_start(pay_d.rearrange("(i p) c -> p i c",p=P),pay[:,:,:]).then_inc(s_payd,16)
                sp.wait_ge(s_segd,16*HI)
                with sp.Fori(0,NCH//2) as it:
                    for q in range(2):
                        c=it*2+q
                        with sp.If(on(c,end)):
                            sp.wait_ge(s_used,c+1)
                            sp.sem_inc(s_go,1)
                            sp.dma_start(idx[:,q,:],srcv[ds(c,1),:,:].rearrange("a p j -> (a p) j")).then_inc(s_in[q],16)
                            sp.dma_start(D[:,q].rearrange("p j k -> p (j k)"),segv[ds(c,1),:,:].rearrange("a p j -> (a p) j")).then_inc(s_D[q],16)
            @block.gpsimd
            def _(pool):
                pool.wait_ge(s_segr,1)
                for i in range(HI):
                    nc.gpsimd.indirect_dma_start(out=seg,out_offset=bass.IndirectOffsetOnAxis(ap=sti[:,i:i+1],axis=0),in_=seg_row[:,i,:],in_offset=None).then_inc(s_segd,16)
                pool.wait_ge(s_payd,16)
                end=n_end(pool)
                with pool.Fori(0,NCH//2) as it:
                    for q in range(2):
                        with pool.If(on(it*2+q,end)):
                            pool.wait_ge(s_used,it*2+q+1)
                            pool.sem_inc(s_go,1)
                            pool.wait_ge(s_in[q],it*16+16)
                            pool.sem_inc(s_go,1)
                            for i in range(ROW):
                                nc.gpsimd.indirect_dma_start(out=G[:,q,i,:],out_offset=None,in_=pay_d,in_offset=bass.IndirectOffsetOnAxis(ap=idx[:,q,i:i+1],axis=0)).then_inc(s_G[q],16)
                for q in range(2):
                    chunks=((end>>13)+2-q)>>1
                    pool.wait_ge(s_rd[q],pool.snap(chunks*16)); pool.sem_inc(s_go,1)
                    pool.wait_ge(s_cd[q],pool.snap(chunks*16)); pool.sem_inc(s_go,1)
                pool.wait_ge(s_en,1)
                for i in range(HI):
                    nc.gpsimd.indirect_dma_start(out=rloc[:,i,:],out_offset=None,in_=res_d,in_offset=bass.IndirectOffsetOnAxis(ap=eni[:,i:i+1],axis=0)).then_inc(s_gr,16)
                    nc.gpsimd.indirect_dma_start(out=rcar[:,i,:],out_offset=None,in_=car_d,in_offset=bass.IndirectOffsetOnAxis(ap=rowi[:,i:i+1],axis=0)).then_inc(s_gr,16)
                pool.wait_ge(s_gr,32*HI)
            @block.tensor
            def _(pe):
                pe.wait_ge(s_w,16*13)
                pe.sem_inc(s_tt,2); pe.sem_inc(s_h,2); pe.sem_inc(s_y,4) 
                with pe.Fori(0,HI//2) as it:
                    for q in range(2):
                        g=it*2+q
                        pe.wait_ge(s_tn,g+1)
                        pe.wait_ge(s_te,g+1)
                        nc.tensor.transpose(bank[q][:,0,:],tn[:,q,:],ident[:,:]).then_inc(s_tt,1)
                        pe.wait_ge(s_te,g+3)
                        pe.wait_ge(s_he,g+1)
                        nc.tensor.matmul(bank[2+q][:,0,0:HF],tT[:,q,:],W[:,:],start=True,stop=True).then_inc(s_h,1)
                end=n_end(pe)
                with pe.Fori(0,NCH//2) as it:
                    for q in range(2):
                        c=it*2+q
                        with pe.If(on(c,end)):
                            pe.wait_ge(s_a1,c+1)
                            pe.sem_inc(s_go,1)
                            for i in range(2): last=nc.tensor.transpose(bank[4][0:4,i,:],rowe[:,4*i:4*i+4],ident[:,:])
                            last.then_inc(s_a2,1)
                            pe.wait_ge(s_a3,c+1)
                            pe.sem_inc(s_go,1)
                            nc.tensor.transpose(bank[5][:,0,0:4],aT[:,0:P],ident[0:4,0:4]).then_inc(s_a4,1)
                            pe.wait_ge(s_x,c+1)
                            for i in range(3): last=nc.tensor.transpose(bank[6][0:PAY,i,:],ms[:,i,:],ident[:,:])
                            last.then_inc(s_xt,1)
                            pe.wait_ge(s_cr,c+1)
                            pe.sem_inc(s_go,1)
                            for i in range(2): last=nc.tensor.transpose(bank[7][:,i,0:PAY],cm[:,i,0:P],ident[0:PAY,0:PAY])
                            last.then_inc(s_crT,1)
                        with pe.If(it*2+q<NGRP):
                            for ef in range(8):
                                pe.wait_ge(s_fe,c*8+ef+1)
                                nc.tensor.matmul(bank[ef%2][:,:,:],W1[:,ef//2,(ef%2)*P:(ef%2+1)*P],tnT[:,ds(group(c)*512,512)],start=True,stop=True).then_inc(s_f,1)
                            for m in range(4):
                                pe.wait_ge(s_ye,c*4+m+1)
                                if m==0: pe.wait_ge(s_fe,c*8+10)
                                for ee in range(EXP):
                                    for f in range(2):
                                        last=nc.tensor.matmul(bank[2+m%2][:,ee,:],hT[:,ee,f,m*P:(m+1)*P],W2[:,ee,f,:],start=(f==0),stop=(f==1))
                                last.then_inc(s_y,1)
                pe.wait_ge(s_w,16*13)
            @block.scalar
            def _(act):
                act.sem_inc(s_te,2); act.sem_inc(s_fe,2)
                with act.Fori(0,B) as b:
                    act.wait_ge(s_var,b+1)
                    nc.scalar.activation(rs[:,:],rs[:,:],ACT.Sqrt).then_inc(s_sd,1)
                    for m in range(NT):
                        g=b*NT+m; q=m%2
                        act.wait_ge(s_tt,g+3)
                        act.wait_ge(s_h,g+1)
                        nc.scalar.activation(tnT[:,ds(g*P,P)],bank[q][:,0,:],ACT.Identity)
                        nc.scalar.activation(tT[:,q,:],bank[q][:,0,:],ACT.Identity).then_inc(s_te,1)
                end=n_end(act)
                with act.Fori(0,NCH//2) as it:
                    for q in range(2):
                        c=it*2+q
                        with act.If(on(c,end)):
                            act.wait_ge(s_e,c+1)
                            nc.scalar.activation(ex[:,:,:,:],ex[:,:,:,:],ACT.Exp).then_inc(s_ex,1)
                            act.wait_ge(s_r,c+1)
                            act.dma_start(resv[ds(c,1),:,:].rearrange("a p j -> (a p) j"),res[:,q,1:ROW+1,:].rearrange("p j k -> p (j k)")).then_inc(s_rd[q],16)
                            act.wait_ge(s_x1,c+1)
                            nc.scalar.activation(xt[:,:,:],xt[:,:,:],ACT.Exp).then_inc(s_x2,1)
                            act.wait_ge(s_ci,c+1)
                            act.dma_start(carv[ds(c,1),:,:].rearrange("a p k -> (a p) k"),carry[:,q,:]).then_inc(s_cd[q],16)
                        with act.If(it*2+q<NGRP):
                            for ef in range(8):
                                act.wait_ge(s_f,c*8+ef+1)
                                if ef==0: act.wait_ge(s_y,c*4+4)
                                nc.scalar.activation(hT[:,ef//2,ef%2,:],bank[ef%2][:,:,:].rearrange("p a b -> p (a b)"),ACT.Gelu,bias=b1[:,ef//2,ef%2:ef%2+1]).then_inc(s_fe,1)
                            act.wait_ge(s_ye,c*4+6)
                            act.dma_start(yv[ds(group(c),1),:,:].rearrange("a p n -> (a p) n"),ysb[:,q].rearrange("p m n -> p (m n)")).then_inc(s_yw[q],16)
                for q in range(2): act.wait_ge(s_yw[q],16*NGRP//2)
            @block.vector
            def _(dve):
                ch=Chain(dve,s_ch)
                dve.sem_inc(s_he,2); dve.sem_inc(s_used,2); dve.sem_inc(s_ye,2)
                ch.mark(nc.vector.tensor_copy(sti[:,:],start_f[:,:]))
                ch(nc.vector.tensor_copy(eni[:,:],end_f[:,:]))
                dve.sem_inc(s_eni,1)
                lc=Chain(dve,s_l,17)
                dve.wait_ge(s_w,16*13)
                with dve.Fori(0,B) as b:
                    lc.body(b)
                    for m in range(NT):
                        lc.mark(nc.vector.bn_stats(st[:,m,:],t_all[:,ds(b*NT+m,1),:].rearrange("p a c -> p (a c)")))
                    lc.sync(); dve.sem_inc(s_go,1)
                    for m in range(NT): lc.mark(nc.vector.bn_aggr(mv[:,m,:],st[:,m,:]))
                    lc.sync()
                    nc.vector.tensor_scalar_add(rs[:,:],mv[:,:,1],1e-5).then_inc(s_var,1)
                    dve.wait_ge(s_sd,b+1)
                    lc(nc.vector.reciprocal(rs[:,:],rs[:,:]))
                    def take_h(m):
                        g=b*NT+m
                        dve.wait_ge(s_h,g+3)
                        nc.vector.tensor_copy(h_all[:,ds(g,1),:].rearrange("p a k -> p (a k)"),bank[2+m%2][:,0,0:HF]).then_inc(s_he,1)
                    for m in range(NT):
                        dve.wait_ge(s_tt,b*NT+m+1)
                        nc.vector.tensor_scalar(tn[:,m%2,:],t_all[:,ds(b*NT+m,1),:].rearrange("p a c -> p (a c)"),mv[:,m,0:1],rs[:,m:m+1],ALU.subtract,ALU.mult).then_inc(s_tn,1)
                        if m>=1: take_h(m-1)
                    take_h(NT-1)
                    lc.end()
                dve.wait_ge(s_he,HI+2)
                for i in range(2):
                    ch(nc.vector.tensor_tensor(pm[:,:,:],h_all[:,:,:],att[:,i:i+1,:].to_broadcast([P,HI,HF]),ALU.mult))
                    dst=(pay[:,:,0:4],seg_row[:,:,1:5])[i]
                    ch(nc.vector.tensor_reduce(dst,pm[:,:,:].rearrange("p n (h k) -> p n h k",h=4),axis=AX.X,op=ALU.add))
                nc.vector.tensor_copy(pay[:,:,4:PAY],h_all[:,:,:]).then_inc(s_pay,1)
                nc.vector.memset(seg_row[:,:,0:1],1.0).then_inc(s_segr,1)
                ch.mark(nc.vector.memset(aT[:,:],0.0)); ch.mark(nc.vector.memset(cm[:,1,:],0.0)); ch.mark(nc.vector.memset(cm[:,0,:],NEG))
                ch.mark(nc.vector.memset(res[:,:,0,:],0.0)); ch.sync()
                ch(nc.vector.memset(res[:,:,0,0:4],NEG))
                end=n_end(dve)
                sc_=Chain(dve,s_c,2*SCK)
                with dve.Fori(0,NCH//2) as it:
                    sc_.body(it)
                    for q in range(2):
                        c=it*2+q
                        sc_.n=q*SCK
                        Dq=D[:,q]; Gq=G[:,q]; R=res[:,q]; Rh=R.rearrange("p j c -> p c j")
                        with dve.If(on(c,end)):
                            dve.wait_ge(s_D[q],it*16+16)
                            f=Dq[:,:,0]
                            sc_.mark(nc.vector.tensor_scalar(ns[:,:],f,-1.0,1.0,ALU.mult,ALU.add))
                            sc_.mark(nc.vector.tensor_scalar(ng[:,:],f,NEG,None,ALU.mult))
                            sc_(nc.vector.reduce_max(rowe[:,4:5],f,AX.X))
                            for h in range(4):
                                sc_.mark(nc.vector.tensor_tensor_scan(out=ad[:,h,:],data0=ns[:,:],data1=Dq[:,:,1+h],initial=0.0,op0=ALU.mult,op1=ALU.add))
                            sc_.mark(nc.vector.tensor_copy(rowe[:,5:8],rowe[:,4:5].to_broadcast([P,3])))
                            sc_.mark(nc.vector.tensor_copy(aT[:,0:1],aT[:,P:P+1]))
                            sc_.sync()
                            nc.vector.tensor_copy(rowe[:,0:4],ad[:,:,ROW-1]).then_inc(s_a1,1)
                            dve.wait_ge(s_a2,c+1)
                            sc_.mark(nc.vector.tensor_copy(aTv[:,0,:],bank[4][0:4,0,:]))
                            sc_(nc.vector.tensor_scalar(aTv[:,1,:],bank[4][0:4,1,:],-1.0,1.0,ALU.mult,ALU.add))
                            nc.vector.tensor_tensor_scan(out=aT[:,1:P+1],data0=aTv[:,1,:],data1=aTv[:,0,:],initial=aT[:,0:1],op0=ALU.mult,op1=ALU.add).then_inc(s_a3,1)
                            dve.wait_ge(s_a4,c+1)
                            sc_(nc.vector.tensor_copy(adin[:,:],bank[5][:,0,0:4]))
                            for h in range(4):
                                sc_.mark(nc.vector.tensor_tensor_scan(out=ad[:,h,:],data0=ns[:,:],data1=Dq[:,:,1+h],initial=adin[:,h:h+1],op0=ALU.mult,op1=ALU.add))
                            sc_.sync()
                            wait_later(dve,s_go,it,s_rd[q],it*16)
                            dve.wait_ge(s_G[q],it*16*ROW+16*ROW)
                            sc_(nc.vector.tensor_tensor(e[:,:,:],Gq[:,:,0:4].rearrange("p j h -> p h j"),ad[:,:,:],ALU.add))
                            sc_(nc.vector.scalar_tensor_tensor(e[:,:,:],e[:,:,:],0.2,e[:,:,:],ALU.mult,ALU.max))
                            for h in range(4):
                                sc_.mark(nc.vector.tensor_tensor_scan(out=R[:,1:ROW+1,h],data0=ng[:,:],data1=e[:,h,:],initial=NEG,op0=ALU.add,op1=ALU.max))
                            sc_.sync()
                            sc_.mark(nc.vector.tensor_tensor(ex[:,0],Rh[:,0:4,0:ROW],ng[:,:].unsqueeze(1).to_broadcast([P,4,ROW]),ALU.add))
                            sc_.mark(nc.vector.tensor_tensor(ex[:,1],e[:,:,:],Rh[:,0:4,1:ROW+1],ALU.subtract))
                            sc_.sync()
                            nc.vector.tensor_tensor(ex[:,0],ex[:,0],Rh[:,0:4,1:ROW+1],ALU.subtract).then_inc(s_e,1)
                            dve.wait_ge(s_ex,c+1)
                            sc_(nc.vector.tensor_tensor(nm[:,:,:].rearrange("p (h k) j -> p h k j",h=4),ex[:,1].unsqueeze(2).to_broadcast([P,4,4,ROW]),
                                Gq[:,:,4:PAY].rearrange("p j (h k) -> p h k j",h=4),ALU.mult))
                            for h in range(4):
                                sc_.mark(nc.vector.tensor_tensor_scan(out=R[:,1:ROW+1,4+h],data0=ex[:,0,h,:],data1=ex[:,1,h,:],initial=0.0,op0=ALU.mult,op1=ALU.add))
                            for k in range(HF):
                                sc_.mark(nc.vector.tensor_tensor_scan(out=R[:,1:ROW+1,8+k],data0=ex[:,0,k//4,:],data1=nm[:,k,:],initial=0.0,op0=ALU.mult,op1=ALU.add))
                            sc_.sync()
                            dve.sem_inc(s_r,1)
                            dve.sem_inc(s_used,1)
                            last=R[:,ROW,:]
                            sc_.mark(nc.vector.tensor_copy(ms[:,0,0:4],last[:,0:4]))
                            sc_.mark(nc.vector.tensor_copy(ms[:,0,4:PAY].rearrange("p (h k) -> p h k",h=4),last[:,0:4].unsqueeze(2).to_broadcast([P,4,4])))
                            sc_.mark(nc.vector.tensor_copy(ms[:,1,:],last[:,4:RES]))
                            sc_.mark(nc.vector.tensor_copy(cm[:,:,0:1],cm[:,:,P:P+1]))
                            sc_(nc.vector.tensor_copy(ms[:,2,:],rowe[:,4:5].to_broadcast([P,PAY])))
                            dve.sem_inc(s_x,1)
                            dve.wait_ge(s_xt,c+1)
                            sc_.mark(nc.vector.tensor_copy(mT[:,0:2,:],bank[6][0:PAY,0:2,:]))
                            sc_(nc.vector.tensor_scalar(mT[:,2,:],bank[6][0:PAY,2,:],NEG,None,ALU.mult))
                            sc_(nc.vector.tensor_tensor_scan(out=cm[:,0,1:P+1],data0=mT[:,2,:],data1=mT[:,0,:],initial=cm[:,0,0:1],op0=ALU.add,op1=ALU.max))
                            sc_.mark(nc.vector.tensor_tensor(xt[:,0,:],cm[:,0,0:P],mT[:,2,:],ALU.add))
                            sc_(nc.vector.tensor_tensor(xt[:,1,:],mT[:,0,:],cm[:,0,1:P+1],ALU.subtract))
                            nc.vector.tensor_tensor(xt[:,0,:],xt[:,0,:],cm[:,0,1:P+1],ALU.subtract).then_inc(s_x1,1)
                            dve.wait_ge(s_x2,c+1)
                            sc_(nc.vector.tensor_tensor(mT[:,1,:],mT[:,1,:],xt[:,1,:],ALU.mult))
                            nc.vector.tensor_tensor_scan(out=cm[:,1,1:P+1],data0=xt[:,0,:],data1=mT[:,1,:],initial=cm[:,1,0:1],op0=ALU.mult,op1=ALU.add).then_inc(s_cr,1)
                            dve.wait_ge(s_crT,c+1)
                            wait_later(dve,s_go,it,s_cd[q],it*16)
                            sc_(nc.vector.tensor_copy(carry[:,q,:].rearrange("p (a k) -> p a k",a=2),bank[7][:,0:2,0:PAY]))
                            dve.sem_inc(s_ci,1)
                        assert sc_.n==(q+1)*SCK,sc_.n
                        with dve.If(it*2+q<NGRP):
                            for m in range(4):
                                dve.wait_ge(s_y,c*4+m+5)
                                if m==0: wait_later(dve,s_go,it,s_yw[q],it*16)
                                nc.vector.tensor_tensor(ysb[:,q,m,:],bank[2+m%2][:,:,:].rearrange("p a b -> p (a b)"),b2[:,:],ALU.add).then_inc(s_ye,1)
                ch.mark(nc.vector.tensor_single_scalar(srow[:,:],sti[:,:],ROWBITS,op=ALU.logical_shift_right))
                ch(nc.vector.tensor_single_scalar(rowi[:,:],eni[:,:],ROWBITS,op=ALU.logical_shift_right))
                dve.sem_inc(s_en,1)
        with ExitStack() as tail:
            lb=lambda n,s,d: tail.enter_context(nc.sbuf_tensor(n,s,d))
            q4=lb("q4",[P,3,HI],f32); mm=lb("mm",[P,HI,EXP],f32); num=lb("num",[P,HI,PAY],f32); tmp=lb("tmp",[P,HI,PAY],f32); pm=lb("pm2",[P,HI,HF],f32)
            abx=lb("abx",[P,HI,8],f32); vv=lb("vv",[P,HI],f32)
            mu=lb("mu",[P,HI],f32); sc=lb("sc",[P,HI,EXP],f32); rk=lb("rk",[P,HI,EXP],f32); cc=lb("cc",[P,HI],f32)
            ysb=lb("ysb2",[P,2,4,EXP*P],f32); acc4=lb("acc4",[P,2,4,P],f32); oT=lb("oT",[P,2,512],f32)
            s_ch=tail.enter_context(nc.semaphore("g_tail_chain"))
            block=tail.enter_context(nc.Block())
            @block.sync
            def _(sp):
                with sp.Fori(0,NGRP//2) as it:
                    for q in range(2):
                        sp.wait_ge(s_yu,it*2+q+1)
                        sp.sem_inc(s_go,1)
                        sp.dma_start(ysb[:,q].rearrange("p m n -> p (m n)"),yv[ds(it*2+q,1),:,:].rearrange("a p n -> (a p) n")).then_inc(s_yl[q],16)
            @block.tensor
            def _(pe):
                with pe.Fori(0,NGRP//2) as it:
                    for q in range(2):
                        c=it*2+q
                        pe.wait_ge(s_acc,c+1)
                        pe.wait_ge(s_oe,c+1)
                        for m in range(4): last=nc.tensor.transpose(bank[q][:,m,:],acc4[:,q,m,:],ident[:,:])
                        last.then_inc(s_o,1)
            @block.scalar
            def _(act):
                act.wait_ge(s_y1,1)
                nc.scalar.activation(abx[:,:,:],abx[:,:,:],ACT.Exp).then_inc(s_y2,1)
                act.wait_ge(s_y1,2)
                nc.scalar.activation(vv[:,:],vv[:,:],ACT.Sqrt).then_inc(s_y2,1)
                act.wait_ge(s_y1,3)
                nc.scalar.activation(gate[:,:,:],gate[:,:,:],ACT.Exp).then_inc(s_y2,1)
                act.sem_inc(s_oe,2)
                with act.Fori(0,NGRP//2) as it:
                    for q in range(2):
                        c=it*2+q
                        act.wait_ge(s_o,c+1+1)
                        wait_later(act,s_go,it,s_out[q],it*16)
                        nc.scalar.activation(oT[:,q,:],bank[q][:,:,:].rearrange("p a b -> p (a b)"),ACT.Identity).then_inc(s_oe,1)
                        act.wait_ge(s_oe,c+3)
                        act.dma_start(O['out'].rearrange("b c h w -> c b (h w)")[:,ds(it,1),q*512:(q+1)*512].rearrange("c b n -> c (b n)"),oT[:,q,:]).then_inc(s_out[q],16)
                for q in range(2): act.wait_ge(s_out[q],16*(NGRP//2))
            @block.vector
            def _(dve):
                ch=Chain(dve,s_ch)
                dve.sem_inc(s_yu,2); dve.sem_inc(s_o,1)
                a_,b_,need=(q4[:,i,:] for i in range(3))
                ch.mark(nc.vector.tensor_copy(a_,srow[:,:])); ch(nc.vector.tensor_copy(b_,rowi[:,:]))
                ch(nc.vector.tensor_tensor(need,a_,b_,ALU.is_equal))
                ch(nc.vector.tensor_scalar(need,need,NEG,None,ALU.mult))
                ch(nc.vector.tensor_tensor(tmp[:,:,0:4],rcar[:,:,0:4],need.unsqueeze(2).to_broadcast([P,HI,4]),ALU.add))
                ch(nc.vector.tensor_tensor(mm[:,:,:],tmp[:,:,0:4],rloc[:,:,0:4],ALU.max))
                ch.mark(nc.vector.tensor_tensor(abx[:,:,0:4],rloc[:,:,0:4],mm[:,:,:],ALU.subtract))
                ch(nc.vector.tensor_tensor(abx[:,:,4:8],tmp[:,:,0:4],mm[:,:,:],ALU.subtract))
                dve.sem_inc(s_y1,1); dve.wait_ge(s_y2,1)
                for o,src,dst in ((0,rloc[:,:,4:RES],num),(4,rcar[:,:,PAY:2*PAY],tmp)):
                    ch.mark(nc.vector.tensor_tensor(dst[:,:,0:4],src[:,:,0:4],abx[:,:,o:o+4],ALU.mult))
                    for h in range(4):
                        ch.mark(nc.vector.tensor_tensor(dst[:,:,4+4*h:8+4*h],src[:,:,4+4*h:8+4*h],abx[:,:,o+h:o+h+1].to_broadcast([P,HI,4]),ALU.mult))
                ch.sync()
                ch(nc.vector.tensor_tensor(num[:,:,:],num[:,:,:],tmp[:,:,:],ALU.add))
                ch(nc.vector.tensor_scalar_add(num[:,:,0:4],num[:,:,0:4],1e-16))
                ch(nc.vector.reciprocal(mm[:,:,:],num[:,:,0:4]))
                agg=tmp[:,:,0:HF]
                for h in range(4): ch.mark(nc.vector.tensor_tensor(tmp[:,:,4*h:4*h+4],num[:,:,4+4*h:8+4*h],mm[:,:,h:h+1].to_broadcast([P,HI,4]),ALU.mult))
                ch.sync()
                row=lambda i: cst[:,i:i+1,:].to_broadcast([P,HI,HF])
                ch(nc.vector.tensor_tensor(agg,agg,row(0),ALU.add))
                ch(nc.vector.tensor_reduce(mu[:,:],agg,axis=AX.X,op=ALU.add))
                ch(nc.vector.tensor_scalar(mu[:,:],mu[:,:],1.0/HF,None,ALU.mult))
                ch(nc.vector.tensor_tensor(agg,agg,mu[:,:].unsqueeze(2).to_broadcast([P,HI,HF]),ALU.subtract))
                ch(nc.vector.tensor_tensor(pm[:,:,:],agg,agg,ALU.mult))
                ch(nc.vector.tensor_reduce(vv[:,:],pm[:,:,:],axis=AX.X,op=ALU.add))
                ch(nc.vector.tensor_scalar(vv[:,:],vv[:,:],1.0/HF,1e-5,ALU.mult,ALU.add))
                dve.sem_inc(s_y1,1); dve.wait_ge(s_y2,2)
                ch(nc.vector.reciprocal(vv[:,:],vv[:,:]))
                ch(nc.vector.tensor_tensor(agg,agg,vv[:,:].unsqueeze(2).to_broadcast([P,HI,HF]),ALU.mult))
                ch(nc.vector.tensor_tensor(agg,agg,row(1),ALU.mult))
                ch(nc.vector.tensor_tensor(agg,agg,row(2),ALU.add))
                ch(nc.vector.tensor_reduce(sc[:,:,:],agg.rearrange("p n (h e) -> p n e h",h=4),axis=AX.X,op=ALU.add))
                ch(nc.vector.tensor_scalar(sc[:,:,:],sc[:,:,:],0.25,None,ALU.mult))
                ch(nc.vector.memset(rk[:,:,:],0.0))
                for i in range(EXP):
                    for j in range(i+1,EXP):
                        ch(nc.vector.tensor_tensor(cc[:,:],sc[:,:,j],sc[:,:,i],ALU.is_gt))
                        ch.mark(nc.vector.tensor_tensor(rk[:,:,i],rk[:,:,i],cc[:,:],ALU.add))
                        ch(nc.vector.scalar_tensor_tensor(rk[:,:,j],rk[:,:,j],1.0,cc[:,:],ALU.add,ALU.subtract))
                ch(nc.vector.tensor_reduce(cc[:,:],sc[:,:,:],axis=AX.X,op=ALU.max))
                ch(nc.vector.tensor_tensor(gate[:,:,:],sc[:,:,:],cc[:,:].unsqueeze(2).to_broadcast([P,HI,EXP]),ALU.subtract))
                ch(nc.vector.tensor_scalar(rk[:,:,:],rk[:,:,:],2.0,None,ALU.is_lt))
                dve.sem_inc(s_y1,1); dve.wait_ge(s_y2,3)
                ch(nc.vector.tensor_tensor(gate[:,:,:],gate[:,:,:],rk[:,:,:],ALU.mult))
                ch(nc.vector.tensor_reduce(cc[:,:],gate[:,:,:],axis=AX.X,op=ALU.add))
                ch(nc.vector.reciprocal(cc[:,:],cc[:,:]))
                ch(nc.vector.tensor_tensor(gate[:,:,:],gate[:,:,:],cc[:,:].unsqueeze(2).to_broadcast([P,HI,EXP]),ALU.mult))
                fc=Chain(dve,s_fc,2*4*3)
                with dve.Fori(0,NGRP//2) as it:
                    fc.body(it)
                    for q in range(2):
                        dve.wait_ge(s_yl[q],it*16+16)
                        dve.wait_ge(s_o,it*2+q+1) if q else dve.wait_ge(s_o,it*2+1)
                        for m in range(4):
                            tok=(it*2+q)*4+m
                            acc=acc4[:,q,m,:]
                            fc.mark(nc.vector.scalar_tensor_tensor(acc,ysb[:,q,m,0:P],gate[:,ds(tok,1),0:1].rearrange("p a b -> p (a b)"),t_all[:,ds(tok,1),:].rearrange("p a c -> p (a c)"),ALU.mult,ALU.add))
                        for ee in range(1,EXP):
                            fc.sync()
                            for m in range(4):
                                tok=(it*2+q)*4+m
                                acc=acc4[:,q,m,:]
                                ins=nc.vector.scalar_tensor_tensor(acc,ysb[:,q,m,ee*P:(ee+1)*P],gate[:,ds(tok,1),ee:ee+1].rearrange("p a b -> p (a b)"),acc,ALU.mult,ALU.add)
                                if ee<EXP-1: fc.mark(ins)
                        ins.then_inc(s_acc,1)
                        dve.wait_ge(s_acc,it*2+q+1)
                        dve.sem_inc(s_yu,1)
                    fc.end()

C_GCH=20
SCK=57
LKM=17; HKM=40

def program(nc, A, O):
    with ExitStack() as ctx:
        keep = lambda n, s, d: ctx.enter_context(nc.sbuf_tensor(n, s, d))
        dram = lambda n, s, d: nc.dram_tensor(n, s, d, kind="Internal").ap()
        srclist = dram("sorted_sources", [NPOS, 1], i32)
        seg = dram("segment_starts", [NPOS, 5], f32)
        pay_d = dram("node_payload", [NODES, PAY], f32)
        res_d = dram("running_softmax", [NPOS, RES], f32)
        car_d = dram("carried", [NCH * P, 2 * PAY], f32)
        y_d = dram("expert_outputs", [NGRP * P, 4 * EXP * P], f32)
        table = dram("patches", [B * DG * TROWS, P], f32)
        ident = keep("ident", [P, P], f32)
        start_f = keep("start_f", [P, HI], f32)
        end_f = keep("end_f", [P, HI], f32)
        ring = keep("ring", [P, 2, C_HALVES * 2 * E_CH], i32)
        with ExitStack() as edges:
            comp = edges.enter_context(nc.sbuf_tensor("kept_edges", [P, 4, 4 * C_NCH * E_UNIT + 3 * E_UNIT], bf16))
            lim = edges.enter_context(nc.sbuf_tensor("iterations", [P, 2], i32))
            compact_phase(nc, A, srclist, seg, res_d, car_d, comp, lim, ident)
            rank_phase(nc, srclist, comp, lim, ring, start_f, end_f, ident)
        t_all = keep("t_all", [P, B * NT, C], f32)
        with ExitStack() as images:
            hold = lambda n, s, d: images.enter_context(nc.sbuf_tensor(n, s, d))
            x_all = hold("x_all", [P, B, HW], f32)
            idx_all = hold("idx_all", [P, (B * NT + 1) * 36], u32)
            w4_all = hold("w4_all", [P, B * 1152], f32)
            wdT = hold("wdT", [P, TAPS, P], f32)
            conv_phase(nc, A, table, x_all, idx_all, w4_all, wdT, ident, srclist, ring)
            mix_phase(nc, A, table, x_all, t_all, idx_all, w4_all, wdT, ident)
        gat_phase(nc, A, O, t_all, start_f, end_f, srclist, seg, pay_d, res_d, car_d, y_d, ident)


def kernel(**inputs):
    import numpy as np
    import concourse.bacc as bacc
    from concourse.bass_utils import run_bass_kernel_spmd

    nc = bacc.Bacc("TRN2", target_bir_lowering=False, num_devices=1)
    arrays = {name: np.ascontiguousarray(a) for name, a in inputs.items()}
    A = {name: nc.dram_tensor(name, a.shape, mybir.dt.from_np(a.dtype), kind="ExternalInput").ap()
         for name, a in arrays.items()}
    O = {"out": nc.dram_tensor("out", (B, C, WID, WID), f32, kind="ExternalOutput").ap()}
    program(nc, A, O)
    result = run_bass_kernel_spmd(nc, [arrays], core_ids=[0])
    return result.results[0]["out"]
```
